# Optimizing a Trainium2 kernel written in Bass

```python
import numpy as np
import jax
import jax.numpy as jnp

def _softmax(x, axis=-1):
    return jax.nn.softmax(x, axis=axis)

def _gelu(x):
    return jax.nn.gelu(x, approximate=True)

def _silu(x):
    return jax.nn.silu(x)

def _sigmoid(x):
    return jax.nn.sigmoid(x)

def _layernorm(x, axis=-1, eps=1e-05):
    m = jnp.mean(x, axis=axis, keepdims=True)
    v = jnp.var(x, axis=axis, keepdims=True)
    return (x - m) / jnp.sqrt(v + eps)

def _scatter_add(tgt, idx, src, axis=0):
    return tgt.at[idx].add(src)

def _segment_sum(src, seg, n):
    return jax.ops.segment_sum(src, seg, n)
kernel_name = 'mk_flamingo_gated_d4_seqx_r4_ef3dc3'

def setup_inputs(seed: int=0):
    np.random.seed(seed)
    _w = jnp.asarray

    def _rec_inputs():
        import jax
        import jax.numpy as jnp
        _rk = jax.random.key(seed)
        x = 7.22e-05 + 1 * jax.random.normal(jax.random.fold_in(_rk, 1), (8, 256, 256), jnp.float32)
        _lenS = 256 - jax.random.randint(jax.random.fold_in(_rk, 7), (8,), 0, max(1, 256 // 4) + 1, jnp.int32)
        _lenS2 = 256 - jax.random.randint(jax.random.fold_in(_rk, 8), (8,), 0, max(1, 256 // 4) + 1, jnp.int32)
        _ctx_1024P = jax.random.normal(jax.random.fold_in(_rk, 11), (8, 16, 256), jnp.float32)
        _ctx_1024c = jax.random.dirichlet(jax.random.fold_in(_rk, 511), 0.3 * jnp.ones((16,), jnp.float32), (8, 256))
        _ctx_1024t = jnp.einsum('bsk,bkd->bsd', _ctx_1024c, _ctx_1024P)
        _ctx_1024t = _ctx_1024t * jax.lax.rsqrt(jnp.mean(jnp.square(_ctx_1024t)) + 1e-12) * 0.953939
        ctx_1024 = 4.13588e-05 + 0.999923 * (_ctx_1024t + 0.3 * jax.random.normal(jax.random.fold_in(_rk, 611), (8, 256, 256), jnp.float32))
        _validS = jnp.arange(256)[None, :] < _lenS[:, None]
        _validS2 = jnp.arange(256)[None, :] < _lenS2[:, None]
        _causal = jnp.tril(jnp.ones((256, 256), dtype=bool))
        mask_1x1xSxS2_bk1 = jnp.broadcast_to(_validS2[0:1, None, None, :], (1, 1, 256, 256))
        mask_BxS2_bf0 = jnp.logical_not(jnp.ones((8, 256), dtype=bool))
        _g = jax.random.normal(jax.random.fold_in(_rk, 9001), (2, 4), jnp.float32)
        _g = jnp.sign(_g) * jnp.maximum(jnp.abs(_g), 1.0) + (_g == 0) * 1.0
        g_xattn = _g[0]
        g_ffn = _g[1]
        return (x, ctx_1024, mask_1x1xSxS2_bk1, mask_BxS2_bf0, g_xattn, g_ffn)
    x, ctx_1024, mask_1x1xSxS2_bk1, mask_BxS2_bf0, g_xattn, g_ffn = _rec_inputs()

    def _L0_xattn_setup():
        import jax, jax.numpy as jnp
        import numpy as np
        D_MODEL = 256
        NUM_HEADS = 16
        D_K = D_MODEL // NUM_HEADS
        BATCH = 4
        SEQ = 512

        def _split_heads(x):
            B, S, _ = x.shape
            return x.reshape(B, S, NUM_HEADS, D_K).transpose(0, 2, 1, 3)
        key = jax.random.key(seed)
        ks = jax.random.split(key, 7)
        query = jax.random.normal(ks[0], (BATCH, SEQ, D_MODEL), dtype=jnp.float32)
        k_in = jax.random.normal(ks[1], (BATCH, SEQ, D_MODEL), dtype=jnp.float32)
        v_in = jax.random.normal(ks[2], (BATCH, SEQ, D_MODEL), dtype=jnp.float32)
        mask = jnp.triu(jnp.ones((SEQ, SEQ), dtype=bool), k=1)[None, None, :, :]
        scale = 1.0 / np.sqrt(D_MODEL)
        Wq = jax.random.normal(ks[3], (D_MODEL, D_MODEL), dtype=jnp.float32) * scale
        Wk = jax.random.normal(ks[4], (D_MODEL, D_MODEL), dtype=jnp.float32) * scale
        Wv = jax.random.normal(ks[5], (D_MODEL, D_MODEL), dtype=jnp.float32) * scale
        Wo = jax.random.normal(ks[6], (D_MODEL, D_MODEL), dtype=jnp.float32) * scale
        return {'query': query, 'key': k_in, 'value': v_in, 'mask': mask, 'Wq': Wq, 'Wk': Wk, 'Wv': Wv, 'Wo': Wo}
    _L0_xattn_all = _L0_xattn_setup()
    _L0_xattn_in = {k: v for k, v in _L0_xattn_all.items() if k in ('Wq', 'Wk', 'Wv', 'Wo')}
    del _L0_xattn_all

    def _L0_ffn_setup():
        import jax, jax.numpy as jnp
        import numpy as np
        B, S, H = (4, 512, 256)
        E = 8
        GS = 2
        NG = E // GS
        F = int(H * 4 * (2.0 / 3.0))
        key = jax.random.key(seed)
        ks = jax.random.split(key, 7)
        sc_h = 1.0 / np.sqrt(H)
        sc_f = 1.0 / np.sqrt(F)
        return {'x': jax.random.normal(ks[0], (B, S, H), dtype=jnp.float32), 'Wr': jax.random.normal(ks[1], (H, E), dtype=jnp.float32) * sc_h, 'br': jnp.zeros((E,), dtype=jnp.float32), 'W_up': jax.random.normal(ks[2], (NG, H, F), dtype=jnp.float32) * sc_h, 'b_up': jax.random.normal(ks[3], (NG, F), dtype=jnp.float32) * 0.01, 'W_down': jax.random.normal(ks[4], (E, F, H), dtype=jnp.float32) * sc_f, 'b_down': jax.random.normal(ks[5], (E, H), dtype=jnp.float32) * 0.01}
    _L0_ffn_all = _L0_ffn_setup()
    _L0_ffn_in = {k: v for k, v in _L0_ffn_all.items() if k in ('Wr', 'br', 'W_up', 'b_up', 'W_down', 'b_down')}
    del _L0_ffn_all

    def _L1_xattn_setup():
        import jax, jax.numpy as jnp
        import numpy as np
        D_MODEL = 256
        N_HEADS = 16
        HEAD_DIM = D_MODEL // N_HEADS
        B, L = (2, 512)
        key = jax.random.key(seed)
        ks = jax.random.split(key, 11)
        s = 1.0 / np.sqrt(D_MODEL)
        inp = {'query': jax.random.normal(ks[0], (B, L, D_MODEL), dtype=jnp.float32), 'key': jax.random.normal(ks[1], (B, L, D_MODEL), dtype=jnp.float32), 'value': jax.random.normal(ks[2], (B, L, D_MODEL), dtype=jnp.float32), 'Wq_w': jax.random.normal(ks[3], (D_MODEL, D_MODEL), dtype=jnp.float32) * s, 'Wq_b': jnp.zeros((D_MODEL,), dtype=jnp.float32), 'Wk_w': jax.random.normal(ks[4], (D_MODEL, D_MODEL), dtype=jnp.float32) * s, 'Wk_b': jnp.zeros((D_MODEL,), dtype=jnp.float32), 'Wv_w': jax.random.normal(ks[5], (D_MODEL, D_MODEL), dtype=jnp.float32) * s, 'Wv_b': jnp.zeros((D_MODEL,), dtype=jnp.float32), 'Wo_w': jax.random.normal(ks[6], (D_MODEL, D_MODEL), dtype=jnp.float32) * s, 'Wo_b': jnp.zeros((D_MODEL,), dtype=jnp.float32)}
        return inp
    _L1_xattn_all = _L1_xattn_setup()
    _L1_xattn_in = {k: v for k, v in _L1_xattn_all.items() if k in ('Wq_w', 'Wq_b', 'Wk_w', 'Wk_b', 'Wv_w', 'Wv_b', 'Wo_w', 'Wo_b')}
    del _L1_xattn_all

    def _L1_ffn_setup():
        import jax, jax.numpy as jnp
        import numpy as np
        INT8_MAX = 127.0

        def _absmax_scale(x, axes):
            amax = jnp.max(jnp.abs(x), axis=axes, keepdims=True)
            return jnp.maximum(amax, 1e-12) / INT8_MAX
        key = jax.random.key(seed)
        k1, k2 = jax.random.split(key)
        lhs = jax.random.normal(k1, (4, 2048, 256), dtype=jnp.float32)
        rhs = jax.random.normal(k2, (256, 256), dtype=jnp.float32)
        return {'lhs': lhs, 'rhs': rhs}
    _L1_ffn_all = _L1_ffn_setup()
    _L1_ffn_in = {k: v for k, v in _L1_ffn_all.items() if k in ('rhs',)}
    del _L1_ffn_all

    def _L2_xattn_setup():
        import jax, jax.numpy as jnp
        import numpy as np
        N_HEADS = 16
        DIM = 256
        HEAD_DIM = DIM // N_HEADS

        def _split_heads(t):
            B, S, _ = t.shape
            return t.reshape(B, S, N_HEADS, HEAD_DIM).transpose(0, 2, 1, 3)
        key = jax.random.key(seed)
        ks = jax.random.split(key, 12)
        B, S = (4, 512)
        scale = 1.0 / np.sqrt(DIM)
        inp = {'x': jax.random.normal(ks[0], (B, S, DIM), jnp.float32), 'memory': jax.random.normal(ks[1], (B, S, DIM), jnp.float32), 'mask': jnp.zeros((B, S), jnp.bool_), 'wq': jax.random.normal(ks[2], (DIM, DIM), jnp.float32) * scale, 'bq': jnp.zeros((DIM,), jnp.float32), 'wk': jax.random.normal(ks[3], (DIM, DIM), jnp.float32) * scale, 'bk': jnp.zeros((DIM,), jnp.float32), 'wv': jax.random.normal(ks[4], (DIM, DIM), jnp.float32) * scale, 'bv': jnp.zeros((DIM,), jnp.float32), 'wo': jax.random.normal(ks[5], (DIM, DIM), jnp.float32) * scale, 'bo': jnp.zeros((DIM,), jnp.float32)}
        return inp
    _L2_xattn_all = _L2_xattn_setup()
    _L2_xattn_in = {k: v for k, v in _L2_xattn_all.items() if k in ('wq', 'bq', 'wk', 'bk', 'wv', 'bv', 'wo', 'bo')}
    del _L2_xattn_all

    def _L2_ffn_setup():
        import jax, jax.numpy as jnp
        import numpy as np
        D_IN, D_HID = (256, 1024)

        def _ternary(key, shape):
            return jax.random.randint(key, shape, -1, 2).astype(jnp.float32)

        def _tlin(x, w, s):
            return jnp.einsum('bsi,oi->bso', x, w) * s
        key = jax.random.key(seed)
        ks = jax.random.split(key, 12)
        inv = lambda fan: 1.0 / np.sqrt(fan).astype(np.float32)
        return {'x': jax.random.normal(ks[0], (4, 512, D_IN), dtype=jnp.float32), 'w1_w': _ternary(ks[1], (D_HID, D_IN)), 'w1_s': jax.random.uniform(ks[2], (D_HID,), dtype=jnp.float32) * inv(D_IN), 'w2_w': _ternary(ks[3], (D_HID, D_IN)), 'w2_s': jax.random.uniform(ks[4], (D_HID,), dtype=jnp.float32) * inv(D_IN), 'h1_w': _ternary(ks[5], (D_HID, D_HID)), 'h1_s': jax.random.uniform(ks[6], (D_HID,), dtype=jnp.float32) * inv(D_HID), 'h2_w': _ternary(ks[7], (D_HID, D_HID)), 'h2_s': jax.random.uniform(ks[8], (D_HID,), dtype=jnp.float32) * inv(D_HID), 'w3_w': _ternary(ks[9], (D_IN, D_HID)), 'w3_s': jax.random.uniform(ks[10], (D_IN,), dtype=jnp.float32) * inv(D_HID)}
    _L2_ffn_all = _L2_ffn_setup()
    _L2_ffn_in = {k: v for k, v in _L2_ffn_all.items() if k in ('w1_w', 'w1_s', 'w2_w', 'w2_s', 'h1_w', 'h1_s', 'h2_w', 'h2_s', 'w3_w', 'w3_s')}
    del _L2_ffn_all

    def _L3_xattn_setup():
        import jax, jax.numpy as jnp
        import numpy as np
        import math
        B, T, E, H = (2, 512, 256, 16)
        D = E // H
        key = jax.random.key(seed)
        ks = jax.random.split(key, 8)
        s = 1.0 / math.sqrt(E)
        return {'input': jax.random.normal(ks[0], (B, T, E), jnp.float32), 'encoded_features': jax.random.normal(ks[1], (B, T, E), jnp.float32), 'Wq': jax.random.normal(ks[2], (E, E), jnp.float32) * s, 'bq': jnp.zeros((E,), jnp.float32), 'Wkv': jax.random.normal(ks[3], (E, 2 * E), jnp.float32) * s, 'bkv': jnp.zeros((2 * E,), jnp.float32), 'Wo': jax.random.normal(ks[4], (E, E), jnp.float32) * s, 'bo': jnp.zeros((E,), jnp.float32)}
    _L3_xattn_all = _L3_xattn_setup()
    _L3_xattn_in = {k: v for k, v in _L3_xattn_all.items() if k in ('Wq', 'bq', 'Wkv', 'bkv', 'Wo', 'bo')}
    del _L3_xattn_all

    def _L3_ffn_setup():
        import jax, jax.numpy as jnp
        import numpy as np
        HID, FFN, E, K = (256, 1024, 8, 2)
        CAP_FACTOR = 1.25
        key = jax.random.key(seed)
        k1, k2, k3, k4 = jax.random.split(key, 4)
        B, T = (4, 512)
        x = jax.random.normal(k1, (B, T, HID), dtype=jnp.float32)
        router_w = jax.random.normal(k2, (E, HID), dtype=jnp.float32) * 0.02
        w1 = jax.random.normal(k3, (E, HID, FFN), dtype=jnp.float32) * 0.02
        w2 = jax.random.normal(k4, (E, FFN, HID), dtype=jnp.float32) * 0.02
        return {'x': x, 'router_w': router_w, 'w1': w1, 'w2': w2}
    _L3_ffn_all = _L3_ffn_setup()
    _L3_ffn_in = {k: v for k, v in _L3_ffn_all.items() if k in ('router_w', 'w1', 'w2')}
    del _L3_ffn_all
    return {'x': x, 'ctx_1024': ctx_1024, 'mask_1x1xSxS2_bk1': mask_1x1xSxS2_bk1, 'mask_BxS2_bf0': mask_BxS2_bf0, 'g_xattn': g_xattn, 'g_ffn': g_ffn, 'L0_xattn_Wq': _L0_xattn_in['Wq'], 'L0_xattn_Wk': _L0_xattn_in['Wk'], 'L0_xattn_Wv': _L0_xattn_in['Wv'], 'L0_xattn_Wo': _L0_xattn_in['Wo'], 'L0_ffn_Wr': _L0_ffn_in['Wr'], 'L0_ffn_br': _L0_ffn_in['br'], 'L0_ffn_W_up': _L0_ffn_in['W_up'], 'L0_ffn_b_up': _L0_ffn_in['b_up'], 'L0_ffn_W_down': _L0_ffn_in['W_down'], 'L0_ffn_b_down': _L0_ffn_in['b_down'], 'L1_xattn_Wq_w': _L1_xattn_in['Wq_w'], 'L1_xattn_Wq_b': _L1_xattn_in['Wq_b'], 'L1_xattn_Wk_w': _L1_xattn_in['Wk_w'], 'L1_xattn_Wk_b': _L1_xattn_in['Wk_b'], 'L1_xattn_Wv_w': _L1_xattn_in['Wv_w'], 'L1_xattn_Wv_b': _L1_xattn_in['Wv_b'], 'L1_xattn_Wo_w': _L1_xattn_in['Wo_w'], 'L1_xattn_Wo_b': _L1_xattn_in['Wo_b'], 'L1_ffn_rhs': _L1_ffn_in['rhs'], 'L2_xattn_wq': _L2_xattn_in['wq'], 'L2_xattn_bq': _L2_xattn_in['bq'], 'L2_xattn_wk': _L2_xattn_in['wk'], 'L2_xattn_bk': _L2_xattn_in['bk'], 'L2_xattn_wv': _L2_xattn_in['wv'], 'L2_xattn_bv': _L2_xattn_in['bv'], 'L2_xattn_wo': _L2_xattn_in['wo'], 'L2_xattn_bo': _L2_xattn_in['bo'], 'L2_ffn_w1_w': _L2_ffn_in['w1_w'], 'L2_ffn_w1_s': _L2_ffn_in['w1_s'], 'L2_ffn_w2_w': _L2_ffn_in['w2_w'], 'L2_ffn_w2_s': _L2_ffn_in['w2_s'], 'L2_ffn_h1_w': _L2_ffn_in['h1_w'], 'L2_ffn_h1_s': _L2_ffn_in['h1_s'], 'L2_ffn_h2_w': _L2_ffn_in['h2_w'], 'L2_ffn_h2_s': _L2_ffn_in['h2_s'], 'L2_ffn_w3_w': _L2_ffn_in['w3_w'], 'L2_ffn_w3_s': _L2_ffn_in['w3_s'], 'L3_xattn_Wq': _L3_xattn_in['Wq'], 'L3_xattn_bq': _L3_xattn_in['bq'], 'L3_xattn_Wkv': _L3_xattn_in['Wkv'], 'L3_xattn_bkv': _L3_xattn_in['bkv'], 'L3_xattn_Wo': _L3_xattn_in['Wo'], 'L3_xattn_bo': _L3_xattn_in['bo'], 'L3_ffn_router_w': _L3_ffn_in['router_w'], 'L3_ffn_w1': _L3_ffn_in['w1'], 'L3_ffn_w2': _L3_ffn_in['w2']}

def reference(x, ctx_1024, mask_1x1xSxS2_bk1, mask_BxS2_bf0, g_xattn, g_ffn, L0_xattn_Wq, L0_xattn_Wk, L0_xattn_Wv, L0_xattn_Wo, L0_ffn_Wr, L0_ffn_br, L0_ffn_W_up, L0_ffn_b_up, L0_ffn_W_down, L0_ffn_b_down, L1_xattn_Wq_w, L1_xattn_Wq_b, L1_xattn_Wk_w, L1_xattn_Wk_b, L1_xattn_Wv_w, L1_xattn_Wv_b, L1_xattn_Wo_w, L1_xattn_Wo_b, L1_ffn_rhs, L2_xattn_wq, L2_xattn_bq, L2_xattn_wk, L2_xattn_bk, L2_xattn_wv, L2_xattn_bv, L2_xattn_wo, L2_xattn_bo, L2_ffn_w1_w, L2_ffn_w1_s, L2_ffn_w2_w, L2_ffn_w2_s, L2_ffn_h1_w, L2_ffn_h1_s, L2_ffn_h2_w, L2_ffn_h2_s, L2_ffn_w3_w, L2_ffn_w3_s, L3_xattn_Wq, L3_xattn_bq, L3_xattn_Wkv, L3_xattn_bkv, L3_xattn_Wo, L3_xattn_bo, L3_ffn_router_w, L3_ffn_w1, L3_ffn_w2):
    import jax
    import jax.numpy as jnp

    def _L0_xattn_ref(query, key, value, mask, Wq, Wk, Wv, Wo):
        import jax, jax.numpy as jnp
        import numpy as np
        D_MODEL = 256
        NUM_HEADS = 16
        D_K = D_MODEL // NUM_HEADS
        BATCH = 4
        SEQ = 512

        def _split_heads(x):
            B, S, _ = x.shape
            return x.reshape(B, S, NUM_HEADS, D_K).transpose(0, 2, 1, 3)
        Q = _split_heads(query @ Wq.T)
        K = _split_heads(key @ Wk.T)
        V = _split_heads(value @ Wv.T)
        scores = jnp.einsum('bhqd,bhkd->bhqk', Q, K) / jnp.sqrt(jnp.float32(D_K))
        scores = jnp.where(mask, -jnp.inf, scores)
        attn_w = jax.nn.softmax(scores, axis=-1)
        out = jnp.einsum('bhqk,bhkd->bhqd', attn_w, V)
        B, _, S, _ = out.shape
        out = out.transpose(0, 2, 1, 3).reshape(B, S, D_MODEL)
        return out @ Wo.T

    def _L0_ffn_ref(x, Wr, br, W_up, b_up, W_down, b_down):
        import jax, jax.numpy as jnp
        import numpy as np
        B, S, H = (4, 512, 256)
        E = 8
        GS = 2
        NG = E // GS
        F = int(H * 4 * (2.0 / 3.0))
        b, s, h = x.shape
        n_tok = b * s
        k = n_tok // E
        xf = x.reshape(n_tok, h)
        logits = xf @ Wr + br
        Sm = jax.nn.softmax(logits, axis=-1)
        G_t, idx_t = jax.lax.top_k(Sm.T, k)
        G = G_t.T
        idx = idx_t.T
        tokens = xf[idx]
        group = jnp.arange(E) // GS
        Wu = W_up[group]
        bu = b_up[group]
        mid = jax.nn.silu(jnp.einsum('keh,ehf->kef', tokens, Wu) + bu)
        out = jnp.einsum('kef,efh->keh', mid, W_down) + b_down
        y = jnp.zeros_like(xf).at[idx].add(G[..., None] * out)
        return y.reshape(b, s, h)

    def _L1_xattn_ref(query, key, value, Wq_w, Wq_b, Wk_w, Wk_b, Wv_w, Wv_b, Wo_w, Wo_b):
        import jax, jax.numpy as jnp
        import numpy as np
        D_MODEL = 256
        N_HEADS = 16
        HEAD_DIM = D_MODEL // N_HEADS
        B, L = (2, 512)
        b = query.shape[0]
        Q = query @ Wq_w.T + Wq_b
        K = key @ Wk_w.T + Wk_b
        V = value @ Wv_w.T + Wv_b

        def split_heads(x):
            return x.reshape(b, -1, N_HEADS, HEAD_DIM).transpose(0, 2, 1, 3)
        Qh, Kh, Vh = (split_heads(Q), split_heads(K), split_heads(V))
        scale = 1.0 / jnp.sqrt(jnp.float32(HEAD_DIM))
        energy = jnp.einsum('bhqd,bhkd->bhqk', Qh, Kh) * scale
        attn = jax.nn.softmax(energy, axis=1)
        out = jnp.einsum('bhqk,bhkd->bhqd', attn, Vh)
        out = out.transpose(0, 2, 1, 3).reshape(b, -1, D_MODEL)
        return out @ Wo_w.T + Wo_b

    def _L1_ffn_ref(lhs, rhs):
        import jax, jax.numpy as jnp
        import numpy as np
        INT8_MAX = 127.0

        def _absmax_scale(x, axes):
            amax = jnp.max(jnp.abs(x), axis=axes, keepdims=True)
            return jnp.maximum(amax, 1e-12) / INT8_MAX
        lhs_scale = _absmax_scale(lhs, (2,))
        rhs_scale = _absmax_scale(rhs, (0,))
        q_lhs = jnp.clip(jnp.round(lhs / lhs_scale), -INT8_MAX, INT8_MAX).astype(jnp.int8)
        q_rhs = jnp.clip(jnp.round(rhs / rhs_scale), -INT8_MAX, INT8_MAX).astype(jnp.int8)
        acc = jax.lax.dot_general(q_lhs, q_rhs, (((2,), (0,)), ((), ())), preferred_element_type=jnp.int32)
        return acc.astype(jnp.float32) * lhs_scale * rhs_scale

    def _L2_xattn_ref(x, memory, mask, wq, bq, wk, bk, wv, bv, wo, bo):
        import jax, jax.numpy as jnp
        import numpy as np
        N_HEADS = 16
        DIM = 256
        HEAD_DIM = DIM // N_HEADS

        def _split_heads(t):
            B, S, _ = t.shape
            return t.reshape(B, S, N_HEADS, HEAD_DIM).transpose(0, 2, 1, 3)
        B, Sq, _ = x.shape
        q = _split_heads(x @ wq.T + bq) / np.sqrt(HEAD_DIM)
        k = _split_heads(memory @ wk.T + bk)
        v = _split_heads(memory @ wv.T + bv)
        logit = jnp.einsum('bhqd,bhkd->bhqk', q, k)
        m = mask[:, None, None, :]
        logit = jnp.where(m, -jnp.inf, logit)
        weights = jax.nn.softmax(logit, axis=-1)
        out = jnp.einsum('bhqk,bhkd->bhqd', weights, v)
        out = out.transpose(0, 2, 1, 3).reshape(B, Sq, DIM)
        return out @ wo.T + bo

    def _L2_ffn_ref(x, w1_w, w1_s, w2_w, w2_s, h1_w, h1_s, h2_w, h2_s, w3_w, w3_s):
        import jax, jax.numpy as jnp
        import numpy as np
        D_IN, D_HID = (256, 1024)

        def _ternary(key, shape):
            return jax.random.randint(key, shape, -1, 2).astype(jnp.float32)

        def _tlin(x, w, s):
            return jnp.einsum('bsi,oi->bso', x, w) * s
        h = jax.nn.silu(_tlin(x, w1_w, w1_s)) * _tlin(x, w2_w, w2_s)
        h = jax.nn.gelu(_tlin(h, h1_w, h1_s), approximate=False)
        h = jax.nn.gelu(_tlin(h, h2_w, h2_s), approximate=False)
        return _tlin(h, w3_w, w3_s)

    def _L3_xattn_ref(input, encoded_features, Wq, bq, Wkv, bkv, Wo, bo):
        import jax, jax.numpy as jnp
        import numpy as np
        import math
        B, T, E, H = (2, 512, 256, 16)
        D = E // H
        b, tq, _ = input.shape
        tk = encoded_features.shape[1]
        q = (input @ Wq + bq).reshape(b, tq, H, D).transpose(0, 2, 1, 3)
        kv = (encoded_features @ Wkv + bkv).reshape(b, tk, 2, H, D).transpose(2, 0, 3, 1, 4)
        k, v = (kv[0], kv[1])
        scores = jnp.einsum('bhqd,bhkd->bhqk', q, k) / math.sqrt(D)
        attn = jax.nn.softmax(scores, axis=2)
        out = jnp.einsum('bhqk,bhkd->bhqd', attn, v)
        out = out.transpose(0, 2, 1, 3).reshape(b, tq, H * D)
        return out @ Wo + bo

    def _L3_ffn_ref(x, router_w, w1, w2):
        import jax, jax.numpy as jnp
        import numpy as np
        HID, FFN, E, K = (256, 1024, 8, 2)
        CAP_FACTOR = 1.25
        B, T, H = x.shape
        N = B * T
        x_flat = x.reshape(N, H)
        C = max(1, int(CAP_FACTOR * N / E * K))
        logits = x_flat @ router_w.T
        probs = jax.nn.softmax(logits, axis=-1)
        top_v, top_i = jax.lax.top_k(probs, K)
        top_v = top_v / jnp.sum(top_v, axis=-1, keepdims=True)
        out = jnp.zeros_like(x_flat)
        for k in range(K):
            eid = top_i[:, k]
            gate = top_v[:, k]
            onehot = jax.nn.one_hot(eid, E, dtype=jnp.int32)
            pos = jnp.take_along_axis(jnp.cumsum(onehot, axis=0), eid[:, None], axis=1)[:, 0] - 1
            keep = pos < C
            slot = jnp.where(keep, eid * C + pos, E * C)
            buf = jnp.zeros((E * C + 1, H), dtype=x.dtype).at[slot].add(x_flat * keep[:, None].astype(x.dtype))
            expert_in = buf[:E * C].reshape(E, C, H)
            h = jax.nn.gelu(jnp.einsum('ech,ehf->ecf', expert_in, w1), approximate=False)
            y = jnp.einsum('ecf,efh->ech', h, w2)
            tok = y.reshape(E * C, H)[jnp.minimum(slot, E * C - 1)]
            out = out + tok * (gate * keep.astype(x.dtype))[:, None]
        return out.reshape(B, T, H)
    x = x + jnp.tanh(g_xattn[0]) * _L0_xattn_ref(_layernorm(x, axis=-1), ctx_1024, ctx_1024, mask_1x1xSxS2_bk1, L0_xattn_Wq, L0_xattn_Wk, L0_xattn_Wv, L0_xattn_Wo)
    x = x + jnp.tanh(g_ffn[0]) * _L0_ffn_ref(_layernorm(x, axis=-1), L0_ffn_Wr, L0_ffn_br, L0_ffn_W_up, L0_ffn_b_up, L0_ffn_W_down, L0_ffn_b_down)
    x = x + jnp.tanh(g_xattn[1]) * _L1_xattn_ref(_layernorm(x, axis=-1), ctx_1024, ctx_1024, L1_xattn_Wq_w, L1_xattn_Wq_b, L1_xattn_Wk_w, L1_xattn_Wk_b, L1_xattn_Wv_w, L1_xattn_Wv_b, L1_xattn_Wo_w, L1_xattn_Wo_b)
    x = x + jnp.tanh(g_ffn[1]) * _L1_ffn_ref(_layernorm(x, axis=-1), L1_ffn_rhs)
    x = x + jnp.tanh(g_xattn[2]) * _L2_xattn_ref(_layernorm(x, axis=-1), ctx_1024, mask_BxS2_bf0, L2_xattn_wq, L2_xattn_bq, L2_xattn_wk, L2_xattn_bk, L2_xattn_wv, L2_xattn_bv, L2_xattn_wo, L2_xattn_bo)
    x = x + jnp.tanh(g_ffn[2]) * _L2_ffn_ref(_layernorm(x, axis=-1), L2_ffn_w1_w, L2_ffn_w1_s, L2_ffn_w2_w, L2_ffn_w2_s, L2_ffn_h1_w, L2_ffn_h1_s, L2_ffn_h2_w, L2_ffn_h2_s, L2_ffn_w3_w, L2_ffn_w3_s)
    x = x + jnp.tanh(g_xattn[3]) * _L3_xattn_ref(_layernorm(x, axis=-1), ctx_1024, L3_xattn_Wq, L3_xattn_bq, L3_xattn_Wkv, L3_xattn_bkv, L3_xattn_Wo, L3_xattn_bo)
    x = x + jnp.tanh(g_ffn[3]) * _L3_ffn_ref(_layernorm(x, axis=-1), L3_ffn_router_w, L3_ffn_w1, L3_ffn_w2)
    return x

_drawn_inputs = setup_inputs


def setup_inputs(seed=0):
    import zlib

    import numpy as np

    out = dict(_drawn_inputs(seed))
    spreads = {'L0_ffn_br': (0.0, 0.1),
     'L1_xattn_Wq_b': (0.0, 0.1),
     'L1_xattn_Wk_b': (0.0, 0.1),
     'L1_xattn_Wv_b': (0.0, 0.1),
     'L1_xattn_Wo_b': (0.0, 0.1),
     'L2_xattn_bq': (0.0, 0.1),
     'L2_xattn_bk': (0.0, 0.1),
     'L2_xattn_bv': (0.0, 0.1),
     'L2_xattn_bo': (0.0, 0.1),
     'L3_xattn_bq': (0.0, 0.1),
     'L3_xattn_bkv': (0.0, 0.1),
     'L3_xattn_bo': (0.0, 0.1)}
    factors = {}
    for name, (base, spread) in spreads.items():
        noise = np.random.default_rng([zlib.crc32(name.encode()), seed]).standard_normal(out[name].shape)
        drawn = base * np.exp(spread * noise) if base else spread * noise
        out[name] = jnp.asarray(drawn.astype(out[name].dtype))
    for name, factor in factors.items():
        out[name] = (out[name] * factor).astype(out[name].dtype)
    return out
```

```python
from contextlib import ExitStack

import numpy as np

import concourse.bass as bass
from concourse import mybir

F32 = mybir.dt.float32
BF16 = mybir.dt.bfloat16
I32 = mybir.dt.int32
U8 = mybir.dt.uint8
ALU = mybir.AluOpType
ACT = mybir.ActivationFunctionType
AX = mybir.AxisListType
ds = bass.ds

P = 128
D = 256
KC = D // P
B, S = 8, 256
T = B * S
NT = T // P
ST = S // P
H, DH = 16, 16
HALF = 2
HPH = H // HALF
GROUP = 4
CH = H // GROUP
VW = P // GROUP
EPS = 1e-5
Q_PARTS = (0, 0, 1, 1, 0, 2)
K_PARTS = (0, 1, 0, 1, 2, 0)
ROWS = DH * len(Q_PARTS)
MASK_ROW, MAX_ROW = ROWS, ROWS + 1
NEG_MAX = -1e30
NEG_EXP = -3e38
INV_SQRT = 1.0 / DH ** 0.5
SOFTMAX_KEYS = (0, 2)
E0, NG0, F0 = 8, 4, 682
FT0 = -(-F0 // P)
FL0 = F0 - (FT0 - 1) * P
TOP0 = T // E0
HID = 1024
HT = HID // P
E3 = 8
CAP3 = max(1, int(1.25 * T / E3 * 2))
CHUNK = 512
NCH = T // CHUNK
TPC = CHUNK // P
FREE = 1
MAGIC = 1.5 * 2.0 ** 23


def program(nc, a, out, stages):
    ctx = ExitStack()
    with ctx:
        def sem(name):
            return ctx.enter_context(nc.semaphore(name))

        def sb(name, shape, dt, c=ctx):
            return c.enter_context(nc.sbuf_tensor(name, shape, dt))

        X = sb("X", [P, NT, D], F32)
        XNT = sb("XNT", [P, KC, T], F32)
        tg = sb("tg", [P, 8], F32)
        ident = sb("ident", [P, P], F32)
        ident_bf = sb("ident_bf", [P, P], BF16)
        ln_st = sb("ln_st", [P, NT, 6], F32)
        ln_tmp = sb("ln_tmp", [P, 8, NT], F32)
        xn = [sb(f"xn{i}", [P, ST, D], F32) for i in range(2)]
        gb = sb("gb", [P, 8], F32)
        probs_e = sb("probs_e", [P, NT, E0], F32)
        route = [sb(f"route{i}", [P, NT, E0], F32) for i in range(6)]
        row_m = sb("row_m", [P, 6, NT], F32)
        flags = sb("flags", [P, NT, 2, E0], BF16)
        totals = sb("totals", [P, NT, 2 * E0], F32)
        sums = sb("sums", [P, NT, 2 * E0], F32)
        need = sb("need", [P, E0], F32)
        coef = sb("coef", [P, NT, E0], F32)
        rev = sb("rev", [P, E0], F32)
        rev_i = sb("rev_i", [P, E0], I32)
        ones_bf = sb("ones_bf", [P, P], BF16)
        upto = sb("upto", [P, P], BF16)
        ones_f = sb("ones_f", [P, NT], F32)

        att = ExitStack()
        ctxT = [sb(f"ctxT{i}", [P, KC, S], F32, att) for i in range(2)]
        wq = sb("wq", [P, KC, D], F32, att)
        wk = sb("wk", [P, KC, D], F32, att)
        wv = sb("wv", [P, KC, D], F32, att)
        wo = sb("wo", [P, CH, D], F32, att)
        bq = sb("bq", [P, HALF], F32, att)
        bq4 = sb("bq4", [P, HALF], F32, att)
        bk = sb("bk", [P, HALF], F32, att)
        bv = sb("bv", [P, D], F32, att)
        bo = sb("bo", [P, D], F32, att)
        bog = sb("bog", [P, D], F32, att)
        qf = sb("qf", [P, HALF, S], F32, att)
        kf = sb("kf", [P, HALF, S], F32, att)
        qr = sb("qr", [P, HALF, S], F32, att)
        kr = sb("kr", [P, HALF, S], F32, att)
        QP = sb("QP", [P, 3, HALF, S], BF16, att)
        KP = sb("KP", [P, 3, HALF, S], BF16, att)
        Qpack = [sb(f"Qpack{i}", [P, H, S], BF16, att) for i in range(2)]
        Kpack = [sb(f"Kpack{i}", [P, H, S], BF16, att) for i in range(2)]
        Vb = [sb(f"Vb{i}", [P, ST, D], F32, att) for i in range(2)]
        V = [sb(f"V{i}", [P, ST, H, VW], F32, att) for i in range(2)]
        On = sb("On", [P, CH, S], F32, att)
        rden = sb("rden", [P, ST, H], F32, att)
        Oq = sb("Oq", [P, ST, D], F32, att)
        OT = sb("OT", [P, HALF, S], F32, att)
        mx = sb("mx", [P, ST, H], F32, att)
        MR = sb("MR", [H, 2, S], BF16, att)
        zrow = sb("zrow", [1, H * S], BF16, att)
        mask_u8 = sb("mask_u8", [P, 2, ST, S], U8, att)
        mask_bf = sb("mask_bf", [P, 2, ST, S], BF16, att)
        pad_u8 = sb("pad_u8", [B, S], U8, att)
        pad_bf = sb("pad_bf", [B, S], BF16, att)
        padT_u8 = sb("padT_u8", [P, ST, B], U8, att)
        keep = sb("keep", [P, ST, B], F32, att)
        nmax = sb("nmax", [P, ST, H], F32, att)
        esum = sb("esum", [P, ST, H], F32, att)
        rsum = sb("rsum", [P, ST, H], F32, att)
        pt_ctx = ExitStack()
        pT = [sb(f"pT{i}", [P, ST, S], F32, pt_ctx) for i in range(8)]
        pt_ctx.close()
        probs = sb("probs", [P, ST, H, S], F32, att)
        M2 = sb("M2", [P, ST, 2, S], F32, att)
        M1 = sb("M1", [P, ST, S], F32, att)
        m1p = sb("m1p", [P, ST, 2, S], BF16, att)
        hs = sb("hs", [P, ST, 8, S], F32, att)
        nident_bf = sb("nident_bf", [P, P], BF16, att)
        att.close()

        f0c = ExitStack()
        wu0 = sb("wu0", [P, NG0, KC, FT0 * P], F32, f0c)
        wd0 = sb("wd0", [P, E0, FT0, D], F32, f0c)
        bu0 = sb("bu0", [P, NG0, FT0], F32, f0c)
        wr0 = sb("wr0", [P, KC, E0], F32, f0c)
        br0 = sb("br0", [P, E0], F32, f0c)
        mid0 = [sb(f"mid0_{i}", [P, FT0, CHUNK], F32, f0c) for i in range(2)]
        G0s = sb("G0s", [P, TPC, E0], F32, f0c)
        thr = sb("thr", [P, E0], I32, f0c)
        cand = sb("cand", [P, E0], I32, f0c)
        step_i = sb("step_i", [P, E0], I32, f0c)
        step_f = sb("step_f", [P, E0], F32, f0c)
        taken = sb("taken", [P, E0], I32, f0c)
        cnt = sb("cnt", [P, E0], F32, f0c)
        f0c.close()
        f1c = ExitStack()
        QT1 = sb("QT1", [P, KC, T], BF16, f1c)
        rhs1 = sb("rhs1", [P, KC, D], F32, f1c)
        rmax = sb("rmax", [P, D], F32, f1c)
        rall = sb("rall", [P, D], F32, f1c)
        rscale = sb("rscale", [P, D], F32, f1c)
        rinv = sb("rinv", [P, D], F32, f1c)
        rtmp = sb("rtmp", [P, KC, D], F32, f1c)
        qrhs = sb("qrhs", [P, KC, D], BF16, f1c)
        lmax = sb("lmax", [P, NT], F32, f1c)
        lscale = sb("lscale", [P, NT], F32, f1c)
        linv = sb("linv", [P, NT], F32, f1c)
        qn = [sb(f"qn{i}", [P, ST, D], BF16, f1c) for i in range(2)]
        y1 = [sb(f"y1_{i}", [P, ST, D], F32, f1c) for i in range(2)]
        f1c.close()
        f2c = ExitStack()
        w1_2 = sb("w1_2", [P, KC, HID], F32, f2c)
        w2_2 = sb("w2_2", [P, KC, HID], F32, f2c)
        h1_2 = sb("h1_2", [P, HT, HID], F32, f2c)
        h2_2 = sb("h2_2", [P, HT, HID], F32, f2c)
        w3_2 = sb("w3_2", [P, HT, D], F32, f2c)
        sc2 = sb("sc2", [P, 4, HT], F32, f2c)
        s3_2 = sb("s3_2", [P, D], F32, f2c)
        hA = sb("hA", [P, HT, CHUNK], F32, f2c)
        hB = sb("hB", [P, HT, CHUNK], F32, f2c)
        sil = [sb(f"sil{i}", [P, CHUNK], F32, f2c) for i in range(2)]
        y2 = [sb(f"y2_{i}", [P, D], F32, f2c) for i in range(2)]
        f2c.close()
        f3c = ExitStack()
        w1_3 = [sb(f"w1_3_{i}", [P, KC, HID], F32, f3c) for i in range(2)]
        w2_3 = [sb(f"w2_3_{i}", [P, HT, D], F32, f3c) for i in range(2)]
        wr3 = sb("wr3", [P, KC, E3], F32, f3c)
        mid3 = [sb(f"mid3_{i}", [P, HT, CHUNK], F32, f3c) for i in range(2)]
        c3e = [sb(f"c3e{i}", [P, NT], F32, f3c) for i in range(2)]
        f3c.close()
        ps = [ctx.enter_context(nc.psum_tensor(f"ps{i}", [P, 2, S], F32)) for i in range(8)]
        P0, P1 = ps[0], ps[1]
        A = ps[2:6]
        O = ps[6:8]
        up_ring, down_ring = ps[0:4], ps[4:8]

        pad_dram = nc.dram_tensor("pad_rows", (B, S), BF16, kind="Internal").ap()

        names = ("x_loaded const_ready ident_ready tg_ready gates_loaded ln_stats ln_std ln_rstd ln_mid xn_ready "
                 "xnt_psum xnt_done w_loaded bias_ready bias_added ctx0 ctx1 q_psum k_psum v_psum q_evac k_evac q_r1 "
                 "k_r1 q_mid k_mid q_split k_split pack0 pack1 padrow0 padrow1 v_copied v_ready smax_ps smax_done mT_ps m_hi m_lo mrow0 "
                 "mrow1 st_ps exp_done av_done o_out oT_ps on_rden on_norm o2_ps on_ready y_ps x_res mask_loaded mask_ready pad_out st_max "
                 "nmax_ready rsum_ready vs_ready p1_ps p1_max m1_step m1_ready p2_ps exp1_done sum1_step norm1 av1_done x_ffn stored "
                 "pack_const zero_row rt_const rt_logits rt_step rt_exp rt_cnt rt_prefix coef_ready thr_step thr_cmp thr_cnt "
                 "f0_router f0_w0 f0_w1 f0_w2 f0_w3 f0_up f0_mid f0_down f0_gs f0_acc "
                 "f1_rhs f1_rmax f1_rall f1_rstep f1_qrhs f1_qstep f1_ps f1_y f1_acc "
                 "f2_w f2_up f2_sil f2_hA f2_mm f2_act f2_yps f2_y f2_acc "
                 "f3_router f3_wA f3_wB f3_up f3_mid f3_down f3_c f3_acc").split()
        s = {n: sem(n) for n in names}
        ctx_sem = [s["ctx0"], s["ctx1"]]
        pack = [s["pack0"], s["pack1"]]
        padrow = [s["padrow0"], s["padrow1"]]
        mrow = [s["mrow0"], s["mrow1"]]

        def wait(eng, semaphore, value):
            if not isinstance(value, int) or value > 0:
                eng.wait_ge(semaphore, value)

        n_att = [L for kind, L in stages if kind == "att"]
        order = {("att", L): i for i, L in enumerate(n_att)}
        m_order = {L: i for i, L in enumerate([L for L in n_att if L in SOFTMAX_KEYS])}
        s_order = {L: i for i, L in enumerate([L for L in n_att if L != 1])}
        ln_order = {st: i for i, st in enumerate(stages)}
        PACKS = 16 * 2 * len(Q_PARTS)

        def bval(b):
            return b if isinstance(b, int) else b[0]

        def ready_x(eng, n):
            if n == 0:
                eng.wait_ge(s["x_loaded"], 16)
                return
            kind, L = stages[n - 1]
            if kind == "att":
                eng.wait_ge(s["x_res"], FREE + 8 * (order["att", L] + 1))
            else:
                eng.wait_ge(s["x_ffn"], 1 + sum(k != "att" for k, _ in stages[:n - 1]))

        def slots(eng, slot):
            slot(0, 0)
            with eng.Fori(0, 3) as i:
                slot((1 + 2 * i, i), 1)
                slot((2 + 2 * i, i + 1), 0)
            slot(7, 1)

        block = ctx.enter_context(nc.Block())

        @block.sync
        def _(sp):
            sp.dma_start(X[:], a["x"].rearrange("(t p) c -> p t c", p=P)).then_inc(s["x_loaded"], 16)
            sp.dma_start(gb[:, 0:4], a["g_xattn"].partition_broadcast(P)).then_inc(s["gates_loaded"], 16)
            sp.dma_start(gb[:, 4:8], a["g_ffn"].partition_broadcast(P)).then_inc(s["gates_loaded"], 16)
            if ("att", 0) in stages:
                sp.dma_start(mask_u8[:, 0], a["mask_qk"]).then_inc(s["mask_loaded"], 16)
                sp.dma_start(mask_u8[:, 1], a["mask_kq"]).then_inc(s["mask_loaded"], 16)

            def load_ctx(b, par):
                sp.dma_start(ctxT[par][:], a["ctxT"][:, :, ds(b * S, S)]).then_inc(ctx_sem[par], 16)

            def attention(n, L):
                i = order["att", L]
                if n > 0:
                    ready_x(sp, n)
                for w, name in ((wq[:], "wq"), (wk[:], "wk"), (wv[:], "wv"), (bq[:], "bq"), (bk[:], "bk"),
                                (wo[:, 0:HALF] if L in SOFTMAX_KEYS else wo[:], "wo")):
                    sp.dma_start(w, a[f"{name}{L}"]).then_inc(s["w_loaded"], 16)
                for w, name in ((bv, "bv"), (bo, "bo")):
                    sp.dma_start(w[:], a[f"{name}{L}"].partition_broadcast(P)).then_inc(s["w_loaded"], 16)
                if L == 2:
                    sp.dma_start(pad_u8[:], a["pad"]).then_inc(s["w_loaded"], 16)
                    sp.dma_start(padT_u8[:], a["padT"]).then_inc(s["w_loaded"], 16)
                    sp.wait_ge(s["mask_ready"], 1 + (("att", 0) in stages))
                    sp.dma_start(pad_dram, pad_bf[:]).then_inc(s["pad_out"], 16)
                    sp.wait_ge(s["pad_out"], 16)
                if L == 0:
                    sp.wait_ge(s["zero_row"], 1)
                sp.wait_ge(s["pack_const"], i + 1)

                def packs(bb, par):
                    g = 8 * i + bb
                    sp.wait_ge(s["q_split"], g + 1)
                    for j, part in enumerate(Q_PARTS):
                        sp.dma_start(Qpack[par][DH * j:DH * (j + 1)].rearrange("d (e f) t -> d e (f t)", f=HALF),
                                     QP[:, part]).then_inc(pack[par], 16)
                    sp.wait_ge(s["k_split"], g + 1)
                    for j, part in enumerate(K_PARTS):
                        sp.dma_start(Kpack[par][DH * j:DH * (j + 1)].rearrange("d (e f) t -> d e (f t)", f=HALF),
                                     KP[:, part]).then_inc(pack[par], 16)
                    if L == 2:
                        sp.dma_start(Kpack[par][MASK_ROW:MASK_ROW + 1],
                                     pad_dram[ds(bb, 1), :].unsqueeze(1).to_broadcast([1, H, S])).then_inc(padrow[par], 16)
                    if L == 0:
                        sp.dma_start(Kpack[par][MASK_ROW:MASK_ROW + 1],
                                     zrow[:].rearrange("o (h t) -> o h t", h=H)).then_inc(padrow[par], 16)

                def max_rows(bb, par):
                    m = 8 * m_order[L] + bb
                    sp.wait_ge(s["m_hi"], m + 1)
                    sp.wait_ge(s["m_lo"], m + 1)
                    for r in range(2):
                        sp.dma_start(Qpack[par][MAX_ROW + r:MAX_ROW + r + 1], MR[:, r]).then_inc(mrow[par], 16)

                load_ctx(0, 0)
                load_ctx(1, 1)
                packs(0, 0)
                if L in SOFTMAX_KEYS:
                    max_rows(0, 0)

                def slot(b, par, refill):
                    if refill:
                        sp.wait_ge(s["v_psum"], 8 * i + b + 1)
                        load_ctx(b + 2, par)
                    packs(b + 1, 1 - par)
                    if L in SOFTMAX_KEYS:
                        max_rows(b + 1, 1 - par)

                slot(0, 0, True)
                with sp.Fori(0, 2) as k:
                    slot(1 + 2 * k, 1, True)
                    slot(2 + 2 * k, 0, True)
                slot(5, 1, True)
                slot(6, 0, False)

            def ffn(n, L):
                if n > 0:
                    ready_x(sp, n)
                if L == 0:
                    sp.dma_start(wr0[:], a["wr0"]).then_inc(s["f0_router"], 16)
                    sp.dma_start(br0[:], a["br0"].partition_broadcast(P)).then_inc(s["f0_router"], 16)
                    sp.dma_start(bu0[:], a["bu0"]).then_inc(s["f0_router"], 16)
                    for g in range(NG0):
                        sp.dma_start(wu0[:, g], a["wu0"][:, g]).then_inc(s[f"f0_w{g}"], 16)
                        sp.dma_start(wd0[:, 2 * g:2 * g + 2], a["wd0"][:, 2 * g:2 * g + 2]).then_inc(s[f"f0_w{g}"], 16)
                elif L == 1:
                    sp.dma_start(rhs1[:], a["rhs1"]).then_inc(s["f1_rhs"], 16)
                elif L == 2:
                    for w, name in ((sc2, "sc2"), (w1_2, "w1_2"), (w2_2, "w2_2"), (h1_2, "h1_2"), (h2_2, "h2_2"), (w3_2, "w3_2")):
                        sp.dma_start(w[:], a[name]).then_inc(s["f2_w"], 16)
                    sp.dma_start(s3_2[:], a["s3_2"].partition_broadcast(P)).then_inc(s["f2_w"], 16)
                else:
                    sp.dma_start(wr3[:], a["wr3"]).then_inc(s["f3_router"], 16)
                    for k in range(2):
                        w_sem = s["f3_wA"] if k == 0 else s["f3_wB"]
                        sp.dma_start(w1_3[k][:], a["w1_3"][k]).then_inc(w_sem, 16)
                        sp.dma_start(w2_3[k][:], a["w2_3"][k]).then_inc(w_sem, 16)
                    with sp.Fori(0, E3 // 2 - 1) as i:
                        for k in range(2):
                            w_sem = s["f3_wA"] if k == 0 else s["f3_wB"]
                            sp.wait_ge(s["f3_down"], NT * (2 * i + k + 1))
                            sp.dma_start(w1_3[k][:], a["w1_3"][ds(2 * i + 2 + k, 1)].rearrange("e p c n -> (e p) c n")).then_inc(w_sem, 16)
                            sp.dma_start(w2_3[k][:], a["w2_3"][ds(2 * i + 2 + k, 1)].rearrange("e p c n -> (e p) c n")).then_inc(w_sem, 16)

            for n, (kind, L) in enumerate(stages):
                if kind == "att":
                    attention(n, L)
                else:
                    ffn(n, L)
            ready_x(sp, len(stages))
            sp.dma_start(out.rearrange("(t p) c -> p t c", p=P), X[:]).then_inc(s["stored"], 16)
            sp.wait_ge(s["stored"], 16)

        @block.gpsimd
        def _(pool):
            pool.memset(ident[:], 0.0).then_inc(s["ident_ready"], 1)
            pool.wait_ge(s["ident_ready"], 1)
            pool.affine_select(out=ident[:], in_=ident[:], compare_op=ALU.not_equal, fill=1.0, base=0,
                               pattern=[[-1, P]], channel_multiplier=1).then_inc(s["ident_ready"], 1)
            pool.wait_ge(s["ident_ready"], 2)
            pool.tensor_copy(ident_bf[:], ident[:]).then_inc(s["ident_ready"], 1)
            pool.memset(ones_f[:], 1.0)
            pool.memset(upto[:], 1.0)
            pool.memset(ones_bf[:], 1.0).then_inc(s["rt_const"], 1)
            pool.wait_ge(s["rt_const"], 1)
            pool.affine_select(out=upto[:], in_=upto[:], compare_op=ALU.is_ge, fill=0.0, base=0,
                               pattern=[[1, P]], channel_multiplier=-1)
            pool.iota(rev_i[:], pattern=[[-1, E0]], base=E0, channel_multiplier=0).then_inc(s["rt_const"], 1)
            pool.wait_ge(s["rt_const"], 2)
            pool.tensor_copy(rev[:], rev_i[:]).then_inc(s["rt_const"], 1)

            def attention(n, L):
                i = order["att", L]
                if n > 0:
                    ready_x(pool, n)
                if L != 0:
                    pool.wait_ge(s["bias_ready"], i + 1)
                    pool.wait_ge(s["xn_ready"], 8 * (ln_order["att", L] + 1))
                    pool.tensor_tensor(X[:], X[:], bog[:].unsqueeze(1).to_broadcast([P, NT, D]), ALU.add)\
                        .then_inc(s["bias_added"], 1)

            for n, (kind, L) in enumerate(stages):
                if kind == "att":
                    attention(n, L)
                elif L == 1:
                    pool.wait_ge(s["f1_rmax"], 1)
                    pool.partition_all_reduce(rall[:], rmax[:], P, bass.bass_isa.ReduceOp.max).then_inc(s["f1_rall"], 1)

        @block.tensor
        def _(pe):
            pe.sem_inc(s["y_ps"], FREE)
            pe.wait_ge(s["ident_ready"], 3)

            def layernorm(n):
                with pe.Fori(0, 4) as t:
                    for j in range(2):
                        pair = 8 * n + 2 * t + j
                        pe.wait_ge(s["xn_ready"], pair + 1)
                        pe.wait_ge(s["xnt_done"], pair + 1)
                        if stages[n] == ("ffn", 1):
                            bank = ps[j][:].bitcast(BF16)
                            for tt in range(ST):
                                for c in range(KC):
                                    last = pe.transpose(bank[:, c, tt * P:(tt + 1) * P], qn[j][:, tt, c * P:(c + 1) * P], ident_bf[:])
                            last.then_inc(s["xnt_psum"], 1)
                            continue
                        for tt in range(ST):
                            for c in range(KC):
                                last = pe.transpose(ps[j][:, c, tt * P:(tt + 1) * P], xn[j][:, tt, c * P:(c + 1) * P], ident[:])
                        last.then_inc(s["xnt_psum"], 1)

            def attention(n, L):
                i = order["att", L]
                w_total = 16 * sum(8 + 2 * (l == 2) for l in n_att[:i + 1])

                def proj_q(b):
                    g = 8 * i + b
                    if not (isinstance(b, int) and b == 0):
                        if L in SOFTMAX_KEYS:
                            pe.wait_ge(s["m_lo"], 8 * m_order[L] + b)
                            pe.wait_ge(s["m_hi"], 8 * m_order[L] + b)
                        else:
                            pe.wait_ge(s["v_copied"], g)
                    for f in range(HALF):
                        for c in range(KC):
                            mm = pe.matmul(P0[:, f], wq[:, c, f * P:(f + 1) * P], XNT[:, c, ds(b * S, S)],
                                           start=c == 0, stop=c == KC - 1)
                    mm.then_inc(s["q_psum"], 1)

                def proj_kv(b, par, u):
                    g = 8 * i + b
                    pe.wait_ge(ctx_sem[par], 16 * (u + 1))
                    pe.wait_ge(s["x_res"], max(1, FREE + g - 2) if isinstance(b, int) else FREE + g - 2)
                    for f in range(HALF):
                        for c in range(KC):
                            mm = pe.matmul(P1[:, f], wk[:, c, f * P:(f + 1) * P], ctxT[par][:, c],
                                           start=c == 0, stop=c == KC - 1)
                    mm.then_inc(s["k_psum"], 1)
                    pe.wait_ge(s["q_evac"], g + 1)
                    for t in range(ST):
                        for c in range(KC):
                            mm = pe.matmul(P0[:, t], ctxT[par][:, c, t * P:(t + 1) * P], wv[:, c],
                                           start=c == 0, stop=c == KC - 1)
                    mm.then_inc(s["v_psum"], 1)

                def smax(b, par, u, h):
                    m = 8 * m_order[L] + b
                    if h == 0:
                        pe.wait_ge(pack[par], PACKS * (u + 1))
                        pe.wait_ge(padrow[par], 16 * (4 * m_order[L] + u - 4 * i + 1))
                    wait(pe, s["smax_done"], 16 * m + h - 1)
                    for t in range(ST):
                        mm = pe.matmul(A[2 + h % 2][:, t], Qpack[par][0:MASK_ROW + 1, h, t * P:(t + 1) * P],
                                       Kpack[par][0:MASK_ROW + 1, h], start=True, stop=L != 0)
                        if L == 0:
                            mm = pe.matmul(A[2 + h % 2][:, t], ident_bf[:], mask_bf[:, 0, t], start=False, stop=True)
                    mm.then_inc(s["smax_ps"], 1)

                def max_turn(b):
                    m = 8 * m_order[L] + b
                    pe.wait_ge(s["smax_done"], 16 * (m + 1))
                    pe.wait_ge(s["v_copied"], 8 * i + b + 1)
                    for t in range(ST):
                        mm = pe.transpose(P0[0:H, 0, t * P:(t + 1) * P], mx[:, t], ident[:])
                    mm.then_inc(s["mT_ps"], 1)

                def scores(b, par, u, h):
                    q = 16 * (8 * s_order[L] + b) + h
                    if h == 0:
                        if L in SOFTMAX_KEYS:
                            pe.wait_ge(mrow[par], 32 * (4 * m_order[L] + u - 4 * i + 1))
                        else:
                            pe.wait_ge(pack[par], PACKS * (u + 1))
                    rows = MAX_ROW + 2 if L in SOFTMAX_KEYS else ROWS
                    ring = 2 if L in SOFTMAX_KEYS else 4
                    wait(pe, s["exp_done"], q - ring + 1)
                    for t in range(ST):
                        mm = pe.matmul(A[h % ring][:, t], Kpack[par][0:rows, h, t * P:(t + 1) * P],
                                       Qpack[par][0:rows, h], start=True, stop=L != 0)
                        if L == 0:
                            mm = pe.matmul(A[h % ring][:, t], ident_bf[:], mask_bf[:, 1, t], start=False, stop=True)
                    mm.then_inc(s["st_ps"], 1)

                def values(b, par, h):
                    q = 16 * (8 * s_order[L] + b) + h
                    g = 8 * i + b
                    if h == 0:
                        wait(pe, s["on_ready"], g)
                    if L in SOFTMAX_KEYS:
                        if h == 0:
                            if L == 0:
                                pe.wait_ge(s["v_copied"], g + 1)
                            else:
                                pe.wait_ge(s["v_ready"], 8 * sum(l in (1, 2) for l in n_att[:i]) + b + 1)
                        pe.wait_ge(s["exp_done"], q + 1)
                    elif h % GROUP == 0:
                        pe.wait_ge(s["vs_ready"], 4 * b + h // GROUP + 1)
                    c, r = h // GROUP, VW * (h % GROUP)
                    for t in range(ST):
                        mm = pe.matmul(O[c // 2][r:r + VW, c % 2], V[par][:, t, h], pT[h % (4 if L in SOFTMAX_KEYS else 8)][:, t],
                                       start=t == 0, stop=t == ST - 1)
                    mm.then_inc(s["av_done"], 1)

                def output_turn(b):
                    pe.wait_ge(s["o_out"], 8 * m_order[L] + b + 1)
                    for t in range(ST):
                        for c in range(CH):
                            mm = pe.transpose(O[t][:].rearrange("p a b -> p (a b)")[:, c * P:(c + 1) * P],
                                              On[:, c, t * P:(t + 1) * P], ident[:])
                    mm.then_inc(s["oT_ps"], 1)

                def output_back(b):
                    pe.wait_ge(s["on_norm"], 8 * m_order[L] + b + 1)
                    for f in range(HALF):
                        for t in range(ST):
                            mm = pe.transpose(O[0][:, f, t * P:(t + 1) * P], Oq[:, t, f * P:(f + 1) * P], ident[:])
                    mm.then_inc(s["o2_ps"], 1)

                def output(b):
                    g = 8 * i + b
                    pe.wait_ge(s["on_ready"], g + 1)
                    if isinstance(b, int) and b >= 6:
                        pe.wait_ge(s["x_res"], FREE + g)
                    else:
                        pe.wait_ge(s["k_evac"], g + 3)
                    tiles, lhs = (HALF, OT) if L in SOFTMAX_KEYS else (CH, On)
                    for t in range(ST):
                        for c in range(tiles):
                            mm = pe.matmul(P1[:, t], lhs[:, c, t * P:(t + 1) * P], wo[:, c], start=c == 0, stop=c == tiles - 1)
                    mm.then_inc(s["y_ps"], 1)

                def heads1(b, par, u):
                    pe.wait_ge(pack[par], PACKS * (u + 1))
                    for t in range(ST):
                        for e in range(H // 2):
                            k = 8 * t + e
                            if k < 4:
                                wait(pe, s["exp1_done"], 16 * b)
                            else:
                                pe.wait_ge(s["p1_max"], 16 * b + k - 3)
                            for f in range(2):
                                mm = pe.matmul(A[k % 4][:, f], Kpack[par][0:ROWS, 2 * e + f, t * P:(t + 1) * P],
                                               Qpack[par][0:ROWS, 2 * e + f], start=True, stop=True)
                            mm.then_inc(s["p1_ps"], 1)
                    for t in range(ST):
                        pe.wait_ge(s["m1_ready"], 2 * b + t + 1)
                        if t == 0:
                            pe.wait_ge(s["p1_max"], 16 * (b + 1))
                        for e in range(H // 2):
                            k = 8 * t + e
                            if k >= 4:
                                pe.wait_ge(s["exp1_done"], 16 * b + k - 3)
                            for f in range(2):
                                pe.matmul(A[k % 4][:, f], Kpack[par][0:ROWS, 2 * e + f, t * P:(t + 1) * P],
                                          Qpack[par][0:ROWS, 2 * e + f], start=True, stop=False)
                                for r in range(2):
                                    mm = pe.matmul(A[k % 4][:, f], nident_bf[:], m1p[:, t, r], start=False, stop=r == 1)
                            mm.then_inc(s["p2_ps"], 1)
                    pe.wait_ge(s["norm1"], 2 * (b + 1))
                    pe.wait_ge(s["v_ready"], 8 * sum(l in (1, 2) for l in n_att[:i]) + b + 1)
                    wait(pe, s["on_ready"], 8 * i + b)
                    for h in range(H):
                        c, r = h // GROUP, VW * (h % GROUP)
                        for t in range(ST):
                            mm = pe.matmul(O[c // 2][r:r + VW, c % 2], V[par][:, t, h], probs[:, t, h],
                                           start=t == 0, stop=t == ST - 1)
                        mm.then_inc(s["av1_done"], 1)

                pe.wait_ge(s["w_loaded"], w_total)
                pe.wait_ge(s["xnt_done"], 8 * (n + 1) + 2)
                if L == 0:
                    pe.wait_ge(s["mask_ready"], 1)
                proj_q(0)
                proj_kv(0, 0, 4 * i)
                if L in SOFTMAX_KEYS:
                    for h in range(H):
                        smax(0, 0, 4 * i, h)
                    max_turn(0)

                def slot(b, par):
                    bb = bval(b)
                    first = isinstance(b, int) and b == 0
                    last = isinstance(b, int) and b == 7
                    u = 4 * i + (b // 2 if isinstance(b, int) else b[1])
                    un = u + par
                    turned = L in SOFTMAX_KEYS and not first
                    if turned:
                        output_turn(bb - 1)
                    if not last:
                        proj_q(bb + 1)
                    if turned:
                        output_back(bb - 1)
                    if not last:
                        proj_kv(bb + 1, 1 - par, un)
                    if not first:
                        output(bb - 1)
                    if L == 1:
                        heads1(bb, par, u)
                        return
                    lag = 2 if L in SOFTMAX_KEYS else 2 * GROUP
                    for h in range(H):
                        scores(bb, par, u, h)
                        if L in SOFTMAX_KEYS and not last and h >= H // 2:
                            for k in range(2):
                                smax(bb + 1, 1 - par, un, 2 * (h - H // 2) + k)
                        if L in SOFTMAX_KEYS:
                            if h >= lag:
                                values(bb, par, h - lag)
                        elif h % GROUP == GROUP - 1 and h >= GROUP:
                            for k in range(GROUP):
                                values(bb, par, h - 2 * GROUP + 1 + k)
                    for h in range(H - (lag if L in SOFTMAX_KEYS else GROUP), H):
                        values(bb, par, h)
                    if L in SOFTMAX_KEYS and not last:
                        max_turn(bb + 1)

                slots(pe, slot)
                if L in SOFTMAX_KEYS:
                    output_turn(7)
                    output_back(7)
                output(7)

            rt_order = {L: i for i, L in enumerate([L for k, L in stages if k == "ffn" and L in (0, 3)])}

            def router(L, w):
                for t in range(NT):
                    for c in range(KC):
                        mm = pe.matmul(ps[0][:].rearrange("p a b -> p (a b)")[:, t * E0:(t + 1) * E0], XNT[:, c, t * P:(t + 1) * P],
                                       w[:, c], start=c == 0, stop=c == KC - 1)
                mm.then_inc(s["rt_logits"], 1)

            def counts(L, bank, cols):
                pe.matmul(bank[:, 0, 0:cols], upto[:], flags[:].rearrange("p t k e -> p (t k e)")[:, 0:cols], start=True, stop=True)
                pe.matmul(bank[:, 1, 0:cols], ones_bf[:], flags[:].rearrange("p t k e -> p (t k e)")[:, 0:cols], start=True, stop=True)\
                    .then_inc(s["rt_prefix"], 1)

            def ffn0(n):
                pe.wait_ge(s["xnt_done"], 8 * (n + 1) + 2)
                pe.wait_ge(s["f0_router"], 48)
                pe.wait_ge(s["rt_const"], 3)
                router(0, wr0)
                with pe.Fori(0, 30) as i:
                    pe.wait_ge(s["thr_cmp"], i + 1)
                    pe.matmul(ps[1][:, 0, 0:NT * E0], ones_bf[:], flags[:].rearrange("p t k e -> p (t k e)")[:, 0:NT * E0],
                              start=True, stop=True).then_inc(s["thr_cnt"], 1)
                pe.wait_ge(s["thr_cmp"], 31)
                counts(0, ps[2], 2 * NT * E0)
                pe.wait_ge(s["coef_ready"], rt_order[0] + 1)

                def up(ch, g):
                    if isinstance(ch, int) and ch == 0:
                        pe.wait_ge(s[f"f0_w{g}"], 32)
                    for f in range(FT0):
                        k = (ch * NG0 + g) * FT0 + f
                        bank = up_ring[(g * FT0 + f) % 4][:].rearrange("p a b -> p (a b)")
                        wait(pe, s["f0_mid"], k - 3)
                        for c in range(KC):
                            mm = pe.matmul(bank, wu0[:, g, c, f * P:(f + 1) * P], XNT[:, c, ds(ch * CHUNK, CHUNK)],
                                           start=c == 0, stop=c == KC - 1)
                        mm.then_inc(s["f0_up"], 1)

                def down(ch, g):
                    pe.wait_ge(s["f0_mid"], (ch * NG0 + g + 1) * FT0)
                    for t in range(TPC):
                        k = (ch * NG0 + g) * TPC + t
                        wait(pe, s["f0_acc"], 2 * (k - 3))
                        for e in range(2):
                            for f in range(FT0):
                                rows = P if f < FT0 - 1 else FL0 + 1
                                mm = pe.matmul(down_ring[t][:, e], mid0[g % 2][0:rows, f, t * P:(t + 1) * P],
                                               wd0[0:rows, 2 * g + e, f], start=f == 0, stop=f == FT0 - 1)
                        mm.then_inc(s["f0_down"], 1)

                def chunk(ch):
                    up(ch, 0)
                    for g in range(NG0):
                        if g + 1 < NG0:
                            up(ch, g + 1)
                        down(ch, g)

                chunk(0)
                with pe.Fori(1, NCH) as ch:
                    chunk(ch)

            def ffn1(n):
                pe.wait_ge(s["xnt_done"], 8 * (n + 1) + 2)
                pe.wait_ge(s["f1_qrhs"], 1)

                def pair(b, j, first):
                    if not first:
                        pe.wait_ge(s["f1_y"], b - 1)
                    for t in range(ST):
                        for c in range(KC):
                            mm = pe.matmul(ps[2 + j][:, t], QT1[:, c, ds(b * S + t * P, P)], qrhs[:, c], start=c == 0, stop=c == KC - 1)
                    mm.then_inc(s["f1_ps"], 1)

                pair(0, 0, True)
                pair(1, 1, True)
                with pe.Fori(1, B // 2) as i:
                    for j in range(2):
                        pair(2 * i + j, j, False)

            def ffn2(n):
                pe.wait_ge(s["xnt_done"], 8 * (n + 1) + 2)
                pe.wait_ge(s["f2_w"], 16 * 7)

                def chunk(ch):
                    first = isinstance(ch, int)
                    for o in range(HT):
                        wait(pe, s["f2_hA"], ch * HT + o - 1)
                        for k, w in enumerate((w1_2, w2_2)):
                            bank = ps[2 * (o % 2) + k][:].rearrange("p a b -> p (a b)")
                            for c in range(KC):
                                mm = pe.matmul(bank, w[:, c, o * P:(o + 1) * P], XNT[:, c, ds(ch * CHUNK, CHUNK)],
                                               start=c == 0, stop=c == KC - 1)
                        mm.then_inc(s["f2_up"], 1)
                    for stage, (w, src) in enumerate(((h1_2, hA), (h2_2, hB))):
                        if stage == 0:
                            pe.wait_ge(s["f2_hA"], (ch + 1) * HT)
                        else:
                            pe.wait_ge(s["f2_act"], (2 * ch + 1) * HT)
                        for o in range(HT):
                            wait(pe, s["f2_act"], (2 * ch + stage) * HT + o - 1)
                            bank = ps[4 + o % 2][:].rearrange("p a b -> p (a b)")
                            for c in range(HT):
                                mm = pe.matmul(bank, w[:, c, o * P:(o + 1) * P], src[:, c], start=c == 0, stop=c == HT - 1)
                            mm.then_inc(s["f2_mm"], 1)
                    pe.wait_ge(s["f2_act"], (2 * ch + 2) * HT)
                    for t in range(TPC):
                        wait(pe, s["f2_y"], ch * TPC + t - 1)
                        for c in range(HT):
                            mm = pe.matmul(ps[6 + t % 2][:, 0], hA[:, c, t * P:(t + 1) * P], w3_2[:, c], start=c == 0, stop=c == HT - 1)
                        mm.then_inc(s["f2_yps"], 1)

                chunk(0)
                with pe.Fori(1, NCH) as ch:
                    chunk(ch)

            def ffn3(n):
                pe.wait_ge(s["xnt_done"], 8 * (n + 1) + 2)
                pe.wait_ge(s["f3_router"], 16)
                pe.wait_ge(s["rt_const"], 3)
                router(3, wr3)
                pe.wait_ge(s["rt_cnt"], 1)
                counts(3, ps[2], 2 * NT * E3)
                pe.wait_ge(s["coef_ready"], rt_order[3] + 1)

                def up(e, k, ch):
                    for f in range(HT):
                        q = (e * NCH + ch) * HT + f
                        bank = up_ring[f % 4][:].rearrange("p a b -> p (a b)")
                        wait(pe, s["f3_mid"], q - 3)
                        for c in range(KC):
                            mm = pe.matmul(bank, w1_3[k][:, c, f * P:(f + 1) * P], XNT[:, c, ch * CHUNK:(ch + 1) * CHUNK],
                                           start=c == 0, stop=c == KC - 1)
                        mm.then_inc(s["f3_up"], 1)

                def down(e, k, ch):
                    pe.wait_ge(s["f3_mid"], (e * NCH + ch + 1) * HT)
                    for t in range(TPC):
                        q = (e * NCH + ch) * TPC + t
                        wait(pe, s["f3_acc"], q - 3)
                        for c in range(HT):
                            mm = pe.matmul(down_ring[t][:, 0], mid3[ch % 2][:, c, t * P:(t + 1) * P], w2_3[k][:, c],
                                           start=c == 0, stop=c == HT - 1)
                        mm.then_inc(s["f3_down"], 1)

                def experts(i):
                    todo = [(k, ch) for k in range(2) for ch in range(NCH)]
                    for j, (k, ch) in enumerate(todo):
                        if ch == 0:
                            pe.wait_ge(s["f3_wA"] if k == 0 else s["f3_wB"], 32 * (i + 1))
                        up(2 * i + k, k, ch)
                        if j:
                            k0, ch0 = todo[j - 1]
                            down(2 * i + k0, k0, ch0)
                    down(2 * i + 1, 1, NCH - 1)

                experts(0)
                with pe.Fori(1, E3 // 2) as i:
                    experts(i)

            for n, (kind, L) in enumerate(stages):
                layernorm(n)
                if kind == "att":
                    attention(n, L)
                else:
                    (ffn0, ffn1, ffn2, ffn3)[L](n)

        @block.scalar
        def _(act):
            act.sem_inc(s["xnt_done"], 2)
            act.wait_ge(s["gates_loaded"], 32)
            act.activation(tg[:], gb[:], ACT.Tanh).then_inc(s["tg_ready"], 1)

            def layernorm(n):
                act.wait_ge(s["ln_mid"], 4 * n + 3)
                act.activation(ln_tmp[:, 5], ln_tmp[:, 4], ACT.Sqrt).then_inc(s["ln_std"], 1)
                with act.Fori(0, 4) as t:
                    for j in range(2):
                        pair = 8 * n + 2 * t + j
                        act.wait_ge(s["xnt_psum"], pair + 1)
                        if stages[n] == ("ffn", 1):
                            act.activation(QT1[:, :, ds((2 * t + j) * S, S)], ps[j][:].bitcast(BF16)[:, :, 0:S], ACT.Copy)\
                                .then_inc(s["xnt_done"], 1)
                            continue
                        act.activation(XNT[:, :, ds((2 * t + j) * S, S)], ps[j][:], ACT.Copy).then_inc(s["xnt_done"], 1)

            def attention(n, L):
                i = order["att", L]

                def split_q(b, par):
                    g = 8 * i + b
                    act.wait_ge(s["q_psum"], g + 1)
                    if isinstance(b, int) and b == 0:
                        act.wait_ge(s["bias_ready"], i + 1)
                    else:
                        act.wait_ge(pack[1 - par], PACKS * (4 * i + prev_uses(b, par)))
                        act.wait_ge(s["k_split"], g)
                    for f in range(HALF):
                        act.activation(qf[:, f], P0[:, f], ACT.Identity, bias=bq4[:, f:f + 1], scale=INV_SQRT)
                        e = act.activation(QP[:, 0, f], P0[:, f], ACT.Identity, bias=bq4[:, f:f + 1], scale=INV_SQRT)
                    e.then_inc(s["q_evac"], 1)

                def split_rest(b, par):
                    g = 8 * i + b
                    act.wait_ge(s["k_psum"], g + 1)
                    for f in range(HALF):
                        act.activation(kf[:, f], P1[:, f], ACT.Identity, bias=bk[:, f:f + 1])
                        e = act.activation(KP[:, 0, f], P1[:, f], ACT.Identity, bias=bk[:, f:f + 1])
                    e.then_inc(s["k_evac"], 1)
                    act.wait_ge(s["q_r1"], g + 1)
                    act.activation(QP[:, 1], qr[:], ACT.Copy).then_inc(s["q_mid"], 1)
                    act.wait_ge(s["k_r1"], g + 1)
                    act.activation(KP[:, 1], kr[:], ACT.Copy).then_inc(s["k_mid"], 1)

                cur = {}

                def prev_uses(b, par):
                    return cur["u_other"]

                def max_part(b, par):
                    m = 8 * m_order[L] + b
                    act.wait_ge(s["mT_ps"], m + 1)
                    if not (isinstance(b, int) and b == 0):
                        act.wait_ge(mrow[1 - par], 32 * (4 * m_order[L] + cur["u_other"]))
                    act.activation(MR[:, 0], P0[0:H, 0], ACT.Copy, scale=-1.0).then_inc(s["m_hi"], 1)

                def exps(b, h):
                    q = 16 * (8 * s_order[L] + b) + h
                    if L in SOFTMAX_KEYS:
                        act.wait_ge(s["st_ps"], q + 1)
                        wait(act, s["av_done"], q - 3)
                        act.activation(pT[h % 4][:], A[h % 2][:], ACT.Exp).then_inc(s["exp_done"], 1)
                    else:
                        act.wait_ge(s["nmax_ready"], 16 * b + h + 1)
                        wait(act, s["av_done"], q - 7)
                        for t in range(ST):
                            e = act.activation(pT[h % 8][:, t], A[h % 4][:, t], ACT.Exp, bias=nmax[:, t, h:h + 1],
                                               accum_out=esum[:, t, h:h + 1])
                        e.then_inc(s["exp_done"], 1)

                def exps1(b):
                    for t in range(ST):
                        for e in range(H // 2):
                            k = 8 * t + e
                            act.wait_ge(s["p2_ps"], 16 * b + k + 1)
                            if k == 0:
                                wait(act, s["av1_done"], 16 * b)
                            act.activation(probs[:, t, 2 * e:2 * e + 2], A[k % 4][:], ACT.Exp).then_inc(s["exp1_done"], 1)

                def outputs_out(b):
                    m = 8 * m_order[L] + b
                    act.wait_ge(s["av_done"], 16 * (8 * s_order[L] + b + 1))
                    wait(act, s["oT_ps"], m)
                    for c in range(2):
                        e = act.activation(On[:, 2 * c:2 * c + 2], O[c][:], ACT.Copy)
                    e.then_inc(s["o_out"], 1)

                def outputs_back(b):
                    act.wait_ge(s["o2_ps"], 8 * m_order[L] + b + 1)
                    act.wait_ge(s["y_ps"], FREE + 8 * i + b)
                    act.activation(OT[:], O[0][:], ACT.Copy).then_inc(s["on_ready"], 1)

                cur["u_other"] = 0
                split_q(0, 0)
                split_rest(0, 0)
                if L in SOFTMAX_KEYS:
                    max_part(0, 0)

                def slot(b, par):
                    bb = bval(b)
                    last = isinstance(b, int) and b == 7
                    u = b // 2 if isinstance(b, int) else b[1]
                    cur["u_other"] = u + 1
                    if not last:
                        split_q(bb + 1, 1 - par)
                    if L in SOFTMAX_KEYS and not (isinstance(b, int) and b == 0):
                        outputs_back(bb - 1)
                    if not last:
                        split_rest(bb + 1, 1 - par)
                    if L == 1:
                        exps1(bb)
                    else:
                        for h in range(H):
                            exps(bb, h)
                    if L in SOFTMAX_KEYS and not last:
                        max_part(bb + 1, 1 - par)
                    if L in SOFTMAX_KEYS:
                        outputs_out(bb)

                slots(act, slot)
                if L in SOFTMAX_KEYS:
                    outputs_back(7)

            rt_order = {L: i for i, L in enumerate([L for k, L in stages if k == "ffn" and L in (0, 3)])}

            def route_exp(L):
                act.wait_ge(s["rt_step"], 5 * rt_order[L] + 3)
                act.activation(route[1][:], route[0][:], ACT.Exp).then_inc(s["rt_exp"], 1)

            def ffn0(n):
                route_exp(0)

                def chunk(ch):
                    for g in range(NG0):
                        for f in range(FT0):
                            k = (ch * NG0 + g) * FT0 + f
                            rows = P if f < FT0 - 1 else FL0
                            act.wait_ge(s["f0_up"], k + 1)
                            if f == 0:
                                wait(act, s["f0_down"], (ch * NG0 + g - 1) * TPC)
                            act.activation(mid0[g % 2][0:rows, f], up_ring[(g * FT0 + f) % 4][0:rows].rearrange("p a b -> p (a b)"),
                                           ACT.Silu, bias=bu0[0:rows, g, f:f + 1]).then_inc(s["f0_mid"], 1)

                act.wait_ge(s["thr_step"], 1)
                chunk(0)
                with act.Fori(1, NCH) as ch:
                    chunk(ch)

            def ffn2(n):
                act.wait_ge(s["f2_w"], 16 * 7)

                def chunk(ch):
                    for o in range(HT):
                        act.wait_ge(s["f2_up"], ch * HT + o + 1)
                        wait(act, s["f2_hA"], ch * HT + o - 1)
                        act.activation(sil[o % 2][:], ps[2 * (o % 2)][:].rearrange("p a b -> p (a b)"), ACT.Silu, scale=sc2[:, 0, o:o + 1])\
                            .then_inc(s["f2_sil"], 1)
                    for stage, dst in enumerate((hB, hA)):
                        for o in range(HT):
                            act.wait_ge(s["f2_mm"], (2 * ch + stage) * HT + o + 1)
                            if o == 0 and stage == 1:
                                act.wait_ge(s["f2_mm"], (2 * ch + 1) * HT)
                            act.activation(dst[:, o], ps[4 + o % 2][:].rearrange("p a b -> p (a b)"), ACT.Gelu,
                                           scale=sc2[:, 2 + stage, o:o + 1]).then_inc(s["f2_act"], 1)

                chunk(0)
                with act.Fori(1, NCH) as ch:
                    chunk(ch)

            def ffn3(n):
                route_exp(3)

                def experts(i):
                    for k in range(2):
                        for ch in range(NCH):
                            for f in range(HT):
                                q = ((2 * i + k) * NCH + ch) * HT + f
                                act.wait_ge(s["f3_up"], q + 1)
                                if f == 0:
                                    wait(act, s["f3_down"], ((2 * i + k) * NCH + ch - 1) * TPC)
                                act.activation(mid3[ch % 2][:, f], up_ring[f % 4][:].rearrange("p a b -> p (a b)"), ACT.Gelu)\
                                    .then_inc(s["f3_mid"], 1)

                experts(0)
                with act.Fori(1, E3 // 2) as i:
                    experts(i)

            for n, (kind, L) in enumerate(stages):
                layernorm(n)
                if kind == "att":
                    attention(n, L)
                elif L != 1:
                    {0: ffn0, 2: ffn2, 3: ffn3}[L](n)

        @block.vector
        def _(dve):
            dve.sem_inc(s["x_res"], FREE)
            if ("att", 0) in stages:
                dve.wait_ge(s["mask_loaded"], 32)
                dve.tensor_scalar(mask_bf[:, 0], mask_u8[:, 0], NEG_MAX, None, ALU.mult)
                dve.tensor_scalar(mask_bf[:, 1], mask_u8[:, 1], NEG_EXP, None, ALU.mult).then_inc(s["mask_ready"], 1)

            def quantise(pair, j, e):
                q = 6 * pair
                cols = ds(2 * pair, 2)
                e.then_inc(s["f1_qstep"], 1)
                dve.wait_ge(s["f1_qstep"], q + 1)
                dve.tensor_reduce(lmax[:, cols], xn[j][:], AX.X, ALU.max, apply_absolute_value=True).then_inc(s["f1_qstep"], 1)
                dve.wait_ge(s["f1_qstep"], q + 2)
                dve.tensor_scalar(lscale[:, cols], lmax[:, cols], 1e-12, 1.0 / 127.0, ALU.max, ALU.mult).then_inc(s["f1_qstep"], 1)
                dve.wait_ge(s["f1_qstep"], q + 3)
                dve.reciprocal(linv[:, cols], lscale[:, cols]).then_inc(s["f1_qstep"], 1)
                dve.wait_ge(s["f1_qstep"], q + 4)
                for t in range(ST):
                    e = dve.tensor_scalar(xn[j][:, t], xn[j][:, t], linv[:, ds(2 * pair + t, 1)], -127.0, ALU.mult, ALU.max)
                e.then_inc(s["f1_qstep"], 1)
                dve.wait_ge(s["f1_qstep"], q + 5)
                dve.tensor_scalar(xn[j][:], xn[j][:], 127.0, MAGIC, ALU.min, ALU.add).then_inc(s["f1_qstep"], 1)
                dve.wait_ge(s["f1_qstep"], q + 6)
                dve.tensor_scalar(qn[j][:], xn[j][:], MAGIC, None, ALU.subtract).then_inc(s["xn_ready"], 1)

            def layernorm(n):
                ready_x(dve, n)
                with dve.Fori(0, NT) as t:
                    dve.bn_stats(ln_st[:, ds(t, 1)], X[:, ds(t, 1)]).then_inc(s["ln_stats"], 1)
                dve.wait_ge(s["ln_stats"], NT * (n + 1))
                me, mo = ln_st[:, :, 1], ln_st[:, :, 4]
                dve.tensor_tensor(ln_tmp[:, 0], me, mo, ALU.add)
                dve.tensor_tensor(ln_tmp[:, 1], me, mo, ALU.subtract)
                dve.tensor_tensor(ln_tmp[:, 2], ln_st[:, :, 2], ln_st[:, :, 5], ALU.add).then_inc(s["ln_mid"], 1)
                dve.wait_ge(s["ln_mid"], 4 * n + 1)
                dve.scalar_tensor_tensor(ln_tmp[:, 3], ln_tmp[:, 1], 0.25, ln_tmp[:, 1], ALU.mult, ALU.mult)
                dve.tensor_scalar(ln_tmp[:, 6], ln_tmp[:, 2], 1.0 / D, EPS, ALU.mult, ALU.add)
                dve.tensor_scalar(ln_tmp[:, 7], ln_tmp[:, 0], 0.5, None, ALU.mult).then_inc(s["ln_mid"], 1)
                dve.wait_ge(s["ln_mid"], 4 * n + 2)
                dve.tensor_tensor(ln_tmp[:, 4], ln_tmp[:, 3], ln_tmp[:, 6], ALU.add).then_inc(s["ln_mid"], 1)
                dve.wait_ge(s["ln_std"], n + 1)
                dve.reciprocal(ln_tmp[:, 5], ln_tmp[:, 5]).then_inc(s["ln_mid"], 1)
                dve.wait_ge(s["ln_mid"], 4 * n + 4)
                with dve.Fori(0, 4) as t:
                    for j in range(2):
                        pair = 2 * t + j
                        dve.wait_ge(s["xnt_psum"], 8 * n + pair + 1 - 2) if n > 0 else dve.wait_ge(s["xnt_done"], pair + 1)
                        for tt in range(ST):
                            i = 2 * pair + tt
                            e = dve.tensor_scalar(xn[j][:, tt], X[:, ds(i, 1)].squeeze(1), ln_tmp[:, 7, ds(i, 1)], ln_tmp[:, 5, ds(i, 1)],
                                                  ALU.subtract, ALU.mult)
                        if stages[n] == ("ffn", 1):
                            quantise(pair, j, e)
                        else:
                            e.then_inc(s["xn_ready"], 1)

            def attention(n, L):
                i = order["att", L]
                w_total = 16 * sum(8 + 2 * (l == 2) for l in n_att[:i + 1])
                dve.wait_ge(s["w_loaded"], w_total)
                dve.wait_ge(s["tg_ready"], 1)
                for par in range(2):
                    dve.memset(Qpack[par][MASK_ROW:MAX_ROW + 2], 1.0)
                    dve.memset(Kpack[par][MASK_ROW:MAX_ROW + 2], 1.0)
                    e = dve.memset(V[par][:, :, :, DH + (L == 0):VW], 0.0)
                    if L == 0:
                        e = dve.memset(V[par][:, :, :, DH:DH + 1], 1.0)
                e.then_inc(s["pack_const"], 1)
                if L == 0:
                    dve.memset(zrow[:], 0.0).then_inc(s["zero_row"], 1)
                if L == 1:
                    dve.wait_ge(s["ident_ready"], 2)
                    dve.tensor_scalar(nident_bf[:], ident[:], -1.0, None, ALU.mult)
                if L == 2:
                    dve.tensor_scalar(pad_bf[:], pad_u8[:], NEG_MAX, None, ALU.mult)
                    dve.tensor_scalar(keep[:], padT_u8[:], -1.0, 1.0, ALU.mult, ALU.add).then_inc(s["mask_ready"], 1)
                dve.tensor_scalar(bq4[:], bq[:], INV_SQRT, None, ALU.mult)
                dve.tensor_scalar(bog[:], bo[:], tg[:, L:L + 1], None, ALU.mult).then_inc(s["bias_ready"], 1)

                def remainders(b, par):
                    g = 8 * i + b
                    dve.wait_ge(s["q_evac"], g + 1)
                    dve.tensor_tensor(qr[:], qf[:], QP[:, 0], ALU.subtract).then_inc(s["q_r1"], 1)
                    dve.wait_ge(s["k_evac"], g + 1)
                    dve.tensor_tensor(kr[:], kf[:], KP[:, 0], ALU.subtract).then_inc(s["k_r1"], 1)
                    dve.wait_ge(s["v_psum"], g + 1)
                    if L == 0:
                        pv = P0[:].rearrange("p t (h d) -> p t h d", h=H)
                        for t in range(ST):
                            e = dve.tensor_copy(V[par][:, t, :, 0:DH], pv[:, t])
                        e.then_inc(s["v_copied"], 1)
                    else:
                        dve.tensor_tensor(Vb[par][:], P0[:], bv[:].unsqueeze(1).to_broadcast([P, ST, D]), ALU.add)\
                            .then_inc(s["v_copied"], 1)
                        if L != 3:
                            dve.wait_ge(s["v_copied"], g + 1)
                            if isinstance(b, int) and b == 0 and L == 2:
                                dve.wait_ge(s["mask_ready"], 1 + (("att", 0) in stages))
                            for t in range(ST):
                                vb = Vb[par][:, t].rearrange("p (h d) -> p h d", h=H)
                                if L == 2:
                                    dve.tensor_scalar(V[par][:, t, :, 0:DH], vb, keep[:, t, ds(b, 1)], None, ALU.mult)
                                    e = dve.tensor_copy(V[par][:, t, :, DH], keep[:, t, ds(b, 1)].to_broadcast([P, H]))
                                else:
                                    e = dve.tensor_copy(V[par][:, t, :, 0:DH], vb)
                            e.then_inc(s["v_ready"], 1)
                    dve.wait_ge(s["q_mid"], g + 1)
                    dve.tensor_tensor(QP[:, 2], qr[:], QP[:, 1], ALU.subtract).then_inc(s["q_split"], 1)
                    dve.wait_ge(s["k_mid"], g + 1)
                    dve.tensor_tensor(KP[:, 2], kr[:], KP[:, 1], ALU.subtract).then_inc(s["k_split"], 1)

                def row_max(b, h):
                    m = 8 * m_order[L] + b
                    dve.wait_ge(s["smax_ps"], 16 * m + h + 1)
                    dve.tensor_reduce(mx[:, :, h], A[2 + h % 2][:], AX.X, ALU.max).then_inc(s["smax_done"], 1)

                def max_rest(b):
                    m = 8 * m_order[L] + b
                    dve.wait_ge(s["m_hi"], m + 1)
                    dve.scalar_tensor_tensor(MR[:, 1], P0[0:H, 0], -1.0, MR[:, 0], ALU.mult, ALU.subtract).then_inc(s["m_lo"], 1)

                def col_max(b, h):
                    dve.wait_ge(s["st_ps"], 16 * (8 * s_order[L] + b) + h + 1)
                    dve.tensor_reduce(nmax[:, :, h], A[h % 4][:], AX.X, ALU.max, negate=True).then_inc(s["nmax_ready"], 1)

                def scale_values(b, par, c):
                    dve.wait_ge(s["exp_done"], 16 * (8 * s_order[L] + b) + GROUP * (c + 1))
                    hh = slice(GROUP * c, GROUP * (c + 1))
                    dve.reciprocal(rsum[:, :, hh], esum[:, :, hh]).then_inc(s["rsum_ready"], 1)
                    dve.wait_ge(s["rsum_ready"], CH * b + c + 1)
                    for t in range(ST):
                        vb = Vb[par][:, t].rearrange("p (h d) -> p h d", h=H)
                        e = dve.tensor_tensor(V[par][:, t, hh, 0:DH], vb[:, hh], rsum[:, t, hh].unsqueeze(2).to_broadcast([P, GROUP, DH]), ALU.mult)
                    e.then_inc(s["vs_ready"], 1)

                def normalise(b):
                    g = 8 * i + b
                    if L == 1:
                        dve.wait_ge(s["av1_done"], 16 * (b + 1))
                    else:
                        dve.wait_ge(s["av_done"], 16 * (8 * s_order[L] + b + 1))
                    dve.wait_ge(s["y_ps"], FREE + g)
                    for c in range(2):
                        e = dve.tensor_copy(On[:, 2 * c:2 * c + 2], O[c][:])
                    e.then_inc(s["on_ready"], 1)

                def divide(b):
                    m = 8 * m_order[L] + b
                    dve.wait_ge(s["oT_ps"], m + 1)
                    view = [O[t][:].rearrange("p a b -> p (a b)").rearrange("p (h w) -> p h w", w=VW) for t in range(ST)]
                    for t in range(ST):
                        e = dve.reciprocal(rden[:, t], view[t][:, :, DH])
                    e.then_inc(s["on_rden"], 1)
                    dve.wait_ge(s["on_rden"], m + 1)
                    for t in range(ST):
                        e = dve.tensor_tensor(Oq[:, t].rearrange("p (h d) -> p h d", h=H), view[t][:, :, 0:DH],
                                              rden[:, t].unsqueeze(2).to_broadcast([P, H, DH]), ALU.mult)
                    e.then_inc(s["on_norm"], 1)

                def residual(b):
                    g = 8 * i + b
                    dve.wait_ge(s["y_ps"], FREE + g + 1)
                    xt = X[:, ds(ST * b, ST)]
                    dve.scalar_tensor_tensor(xt, P1[:], tg[:, L:L + 1], xt, ALU.mult, ALU.add).then_inc(s["x_res"], 1)

                def maxima1(b):
                    for t in range(ST):
                        for e in range(H // 2):
                            k = 16 * b + 8 * t + e
                            dve.wait_ge(s["p1_ps"], k + 1)
                            bank = A[(8 * t + e) % 4]
                            if e == 0:
                                dve.tensor_copy(M2[:, t], bank[:]).then_inc(s["p1_max"], 1)
                            else:
                                dve.wait_ge(s["p1_max"], k)
                                dve.tensor_tensor(M2[:, t], bank[:], M2[:, t], ALU.max).then_inc(s["p1_max"], 1)
                        dve.wait_ge(s["p1_max"], 16 * b + 8 * (t + 1))
                        dve.tensor_tensor(M1[:, t], M2[:, t, 0], M2[:, t, 1], ALU.max).then_inc(s["m1_step"], 1)
                        dve.wait_ge(s["m1_step"], 4 * b + 2 * t + 1)
                        dve.tensor_copy(m1p[:, t, 0], M1[:, t]).then_inc(s["m1_step"], 1)
                        dve.wait_ge(s["m1_step"], 4 * b + 2 * t + 2)
                        dve.tensor_tensor(m1p[:, t, 1], M1[:, t], m1p[:, t, 0], ALU.subtract).then_inc(s["m1_ready"], 1)

                def sums1(b):
                    for t in range(ST):
                        dve.wait_ge(s["exp1_done"], 16 * b + 8 * (t + 1))
                        n_steps = 0
                        src, width = probs[:, t], H // 2
                        while width:
                            base = 10 * b + 5 * t
                            if n_steps:
                                dve.wait_ge(s["sum1_step"], base + n_steps)
                            dve.tensor_tensor(hs[:, t, 0:width], src[:, 0:width], src[:, width:2 * width], ALU.add)\
                                .then_inc(s["sum1_step"], 1)
                            src, width, n_steps = hs[:, t], width // 2, n_steps + 1
                        dve.wait_ge(s["sum1_step"], 10 * b + 5 * t + 4)
                        dve.reciprocal(hs[:, t, 0], hs[:, t, 0]).then_inc(s["sum1_step"], 1)
                        dve.wait_ge(s["sum1_step"], 10 * b + 5 * t + 5)
                        dve.tensor_tensor(probs[:, t], probs[:, t], hs[:, t, 0].unsqueeze(1).to_broadcast([P, H, S]), ALU.mult)\
                            .then_inc(s["norm1"], 1)

                dve.wait_ge(s["pack_const"], i + 1)
                remainders(0, 0)
                if L in SOFTMAX_KEYS:
                    for h in range(H):
                        row_max(0, h)
                    max_rest(0)
                if L != 0:
                    dve.wait_ge(s["bias_added"], sum(l != 0 for l in n_att[:i + 1]))

                def slot(b, par):
                    bb = bval(b)
                    first = isinstance(b, int) and b == 0
                    last = isinstance(b, int) and b == 7
                    if not first:
                        divide(bb - 1) if L in SOFTMAX_KEYS else normalise(bb - 1)
                    if not last:
                        remainders(bb + 1, 1 - par)
                    if not first:
                        residual(bb - 1)
                    if L == 1:
                        maxima1(bb)
                        sums1(bb)
                    elif L == 3:
                        for h in range(H):
                            col_max(bb, h)
                            if h % GROUP == GROUP - 1 and h >= GROUP:
                                scale_values(bb, par, h // GROUP - 1)
                        scale_values(bb, par, CH - 1)
                    elif not last:
                        for h in range(H):
                            row_max(bb + 1, h)
                        max_rest(bb + 1)

                slots(dve, slot)
                divide(7) if L in SOFTMAX_KEYS else normalise(7)
                residual(7)

            rt_order = {L: i for i, L in enumerate([L for k, L in stages if k == "ffn" and L in (0, 3)])}
            def bc_row(x):
                return x.unsqueeze(2).to_broadcast([P, NT, E0])

            def bc_exp(x):
                return x.unsqueeze(1).to_broadcast([P, NT, E0])

            def link(k, r, e):
                e.then_inc(s["rt_step"], 1)
                dve.wait_ge(s["rt_step"], k)

            def softmax_rows(L):
                r = rt_order[L]
                dve.wait_ge(s["rt_const"], 3)
                dve.wait_ge(s["rt_logits"], r + 1)
                logits = ps[0][:].rearrange("p a b -> p (a b)")[:, 0:NT * E0].rearrange("p (t e) -> p t e", e=E0)
                if L == 0:
                    dve.wait_ge(s["f0_router"], 48)
                    link(5 * r + 1, r, dve.tensor_tensor(route[2][:], logits, bc_exp(br0[:]), ALU.add))
                else:
                    link(5 * r + 1, r, dve.tensor_copy(route[2][:], logits))
                link(5 * r + 2, r, dve.tensor_reduce(row_m[:, 0], route[2][:], AX.X, ALU.max))
                dve.tensor_tensor(route[0][:], route[2][:], bc_row(row_m[:, 0]), ALU.subtract).then_inc(s["rt_step"], 1)
                dve.wait_ge(s["rt_exp"], r + 1)
                link(5 * r + 4, r, dve.tensor_reduce(row_m[:, 1], route[1][:], AX.X, ALU.add))
                link(5 * r + 5, r, dve.reciprocal(row_m[:, 2], row_m[:, 1]))

            def running_counts(nk, chain, c0, r):
                dve.wait_ge(s["rt_prefix"], r + 1)
                bank = ps[2]
                tot = bank[:, 1, 0:NT * nk].rearrange("p (t k) -> p t k", k=nk)
                chain(c0 + 1, dve.tensor_copy(totals[:, :, 0:nk], tot))
                for k in range(nk):
                    e = dve.tensor_tensor_scan(sums[:, :, k], ones_f[:], totals[:, :, k], 0.0, ALU.mult, ALU.add)
                chain(c0 + 2, e)
                chain(c0 + 3, dve.tensor_tensor(totals[:, :, 0:nk], sums[:, :, 0:nk], totals[:, :, 0:nk], ALU.subtract))
                chain(c0 + 4, dve.tensor_tensor(totals[:, :, 0:nk], totals[:, :, 0:nk],
                                                bank[:, 0, 0:NT * nk].rearrange("p (t k) -> p t k", k=nk), ALU.add))

            def route0(n):
                r = rt_order[0]
                softmax_rows(0)
                cmp = flags[:].rearrange("p t k e -> p (t k) e")[:, 0:NT]

                def chain(k, e):
                    e.then_inc(s["thr_step"], 1)
                    dve.wait_ge(s["thr_step"], k)

                dve.memset(mid0[0][32:64, FT0 - 1], 1.0)
                dve.memset(mid0[1][32:64, FT0 - 1], 1.0)
                dve.memset(thr[:], 0)
                dve.memset(step_f[:], 2.0 ** 29)
                dve.memset(step_i[:], 1 << 29)
                chain(1, dve.tensor_tensor(probs_e[:], route[1][:], bc_row(row_m[:, 2]), ALU.mult))
                with dve.Fori(0, 30) as i:
                    k = 1 + 5 * i
                    chain(k + 1, dve.tensor_tensor(cand[:], thr[:], step_i[:], ALU.bitwise_or))
                    dve.tensor_tensor(cmp, probs_e[:], bc_exp(cand[:].bitcast(F32)), ALU.is_ge).then_inc(s["thr_cmp"], 1)
                    dve.wait_ge(s["thr_cnt"], i + 1)
                    chain(k + 2, dve.tensor_reduce(cnt[:], ps[1][:, 0, 0:NT * E0].rearrange("p (t e) -> p e t", e=E0), AX.X, ALU.add))
                    chain(k + 3, dve.scalar_tensor_tensor(taken[:], cnt[:], TOP0 - 0.5, step_f[:], ALU.is_ge, ALU.mult))
                    dve.tensor_tensor(thr[:], thr[:], taken[:], ALU.bitwise_or)
                    chain(k + 4, dve.tensor_scalar(step_f[:], step_f[:], 0.5, None, ALU.mult))
                    chain(k + 5, dve.tensor_copy(step_i[:], step_f[:]))
                k = 1 + 5 * 30
                dve.tensor_tensor(flags[:, :, 0], probs_e[:], bc_exp(thr[:].bitcast(F32)), ALU.is_gt)
                dve.tensor_tensor(flags[:, :, 1], probs_e[:], bc_exp(thr[:].bitcast(F32)), ALU.is_equal).then_inc(s["thr_cmp"], 1)
                running_counts(2 * E0, chain, k, r)
                k += 4
                chain(k + 1, dve.tensor_scalar(need[:], sums[:, NT - 1, 0:E0], -1.0, float(TOP0), ALU.mult, ALU.add))
                chain(k + 2, dve.tensor_tensor(route[0][:], totals[:, :, E0:2 * E0], bc_exp(need[:]), ALU.is_le))
                chain(k + 3, dve.tensor_tensor(route[2][:], route[0][:], flags[:, :, 1], ALU.mult))
                chain(k + 4, dve.tensor_tensor(route[0][:], route[2][:], flags[:, :, 0], ALU.add))
                dve.scalar_tensor_tensor(coef[:], route[0][:], tg[:, 4:5], probs_e[:], ALU.mult, ALU.mult).then_inc(s["coef_ready"], 1)

            def ffn0(n):
                dve.wait_ge(s["tg_ready"], 1)
                route0(n)
                dve.wait_ge(s["coef_ready"], rt_order[0] + 1)

                def chunk(ch):
                    wait(dve, s["f0_acc"], 2 * NG0 * TPC * ch)
                    dve.tensor_copy(G0s[:], coef[:, ds(ch * TPC, TPC)]).then_inc(s["f0_gs"], 1)
                    dve.wait_ge(s["f0_gs"], ch + 1)
                    for g in range(NG0):
                        for t in range(TPC):
                            k = (ch * NG0 + g) * TPC + t
                            dve.wait_ge(s["f0_down"], k + 1)
                            xt = X[:, ds(ch * TPC + t, 1)].squeeze(1)
                            for e in range(2):
                                wait(dve, s["f0_acc"], 2 * k + e) if e else None
                                u = dve.scalar_tensor_tensor(xt, down_ring[t][:, e], G0s[:, t, 2 * g + e:2 * g + e + 1], xt, ALU.mult, ALU.add)
                                u.then_inc(s["f0_acc"], 1)

                chunk(0)
                with dve.Fori(1, NCH) as ch:
                    chunk(ch)
                dve.wait_ge(s["f0_acc"], 2 * NT * NG0)
                dve.sem_inc(s["x_ffn"], 1)

            def ffn1_rhs():
                dve.wait_ge(s["f1_rhs"], 16)
                dve.tensor_reduce(rmax[:], rhs1[:].rearrange("p c n -> p n c"), AX.X, ALU.max, apply_absolute_value=True).then_inc(s["f1_rmax"], 1)
                dve.wait_ge(s["f1_rall"], 1)

                def chain(k, e):
                    e.then_inc(s["f1_rstep"], 1)
                    dve.wait_ge(s["f1_rstep"], k)

                chain(1, dve.tensor_scalar(rscale[:], rall[:], 1e-12, 1.0 / 127.0, ALU.max, ALU.mult))
                chain(2, dve.reciprocal(rinv[:], rscale[:]))
                chain(3, dve.tensor_tensor(rtmp[:], rhs1[:], rinv[:].unsqueeze(1).to_broadcast([P, KC, D]), ALU.mult))
                chain(4, dve.tensor_scalar(rtmp[:], rtmp[:], -127.0, 127.0, ALU.max, ALU.min))
                chain(5, dve.tensor_scalar(rtmp[:], rtmp[:], MAGIC, None, ALU.add))
                dve.tensor_scalar(qrhs[:], rtmp[:], MAGIC, None, ALU.subtract).then_inc(s["f1_qrhs"], 1)

            def ffn1(n):
                dve.wait_ge(s["tg_ready"], 1)

                def pair(b, j):
                    dve.wait_ge(s["f1_ps"], b + 1)
                    for t in range(ST):
                        e = dve.scalar_tensor_tensor(y1[j][:, t], ps[2 + j][:, t], lscale[:, ds(ST * b + t, 1)], rscale[:], ALU.mult, ALU.mult)
                    e.then_inc(s["f1_y"], 1)
                    dve.wait_ge(s["f1_y"], b + 1)
                    xt = X[:, ds(ST * b, ST)]
                    dve.scalar_tensor_tensor(xt, y1[j][:], tg[:, 5:6], xt, ALU.mult, ALU.add).then_inc(s["f1_acc"], 1)

                with dve.Fori(0, B // 2) as i:
                    for j in range(2):
                        pair(2 * i + j, j)
                dve.wait_ge(s["f1_acc"], B)
                dve.sem_inc(s["x_ffn"], 1)

            def ffn2(n):
                dve.wait_ge(s["tg_ready"], 1)
                dve.wait_ge(s["f2_w"], 16 * 7)

                def chunk(ch):
                    for o in range(HT):
                        dve.wait_ge(s["f2_sil"], ch * HT + o + 1)
                        if o == 0:
                            wait(dve, s["f2_yps"], ch * TPC)
                        dve.scalar_tensor_tensor(hA[:, o], ps[2 * (o % 2) + 1][:].rearrange("p a b -> p (a b)"), sc2[:, 1, o:o + 1], sil[o % 2][:],
                                                 ALU.mult, ALU.mult).then_inc(s["f2_hA"], 1)
                    for t in range(TPC):
                        k = ch * TPC + t
                        dve.wait_ge(s["f2_yps"], k + 1)
                        dve.tensor_tensor(y2[t % 2][:], ps[6 + t % 2][:, 0], s3_2[:], ALU.mult).then_inc(s["f2_y"], 1)
                        dve.wait_ge(s["f2_y"], k + 1)
                        xt = X[:, ds(k, 1)].squeeze(1)
                        dve.scalar_tensor_tensor(xt, y2[t % 2][:], tg[:, 6:7], xt, ALU.mult, ALU.add).then_inc(s["f2_acc"], 1)

                chunk(0)
                with dve.Fori(1, NCH) as ch:
                    chunk(ch)
                dve.wait_ge(s["f2_acc"], NT)
                dve.sem_inc(s["x_ffn"], 1)

            def route3(n):
                r = rt_order[3]
                softmax_rows(3)
                k = [5 * (r + 1)]

                def chain(e):
                    k[0] += 1
                    e.then_inc(s["rt_step"], 1)
                    dve.wait_ge(s["rt_step"], k[0])

                chain(dve.tensor_tensor(probs_e[:], route[1][:], bc_row(row_m[:, 2]), ALU.mult))
                left = probs_e
                for j in range(2):
                    chain(dve.tensor_reduce(row_m[:, 3 + j], left[:], AX.X, ALU.max))
                    chain(dve.tensor_tensor(route[2][:], left[:], bc_row(row_m[:, 3 + j]), ALU.is_equal))
                    chain(dve.tensor_tensor(route[3][:], route[2][:], bc_exp(rev[:]), ALU.mult))
                    chain(dve.tensor_reduce(row_m[:, 0], route[3][:], AX.X, ALU.max))
                    chain(dve.tensor_tensor(flags[:, :, j], route[3][:], bc_row(row_m[:, 0]), ALU.is_equal))
                    if j == 0:
                        chain(dve.scalar_tensor_tensor(route[4][:], flags[:, :, 0], -2.0, probs_e[:], ALU.mult, ALU.add))
                        left = route[4]
                dve.sem_inc(s["rt_cnt"], 1)
                chain(dve.tensor_tensor(row_m[:, 5], row_m[:, 3], row_m[:, 4], ALU.add))
                chain(dve.reciprocal(row_m[:, 5], row_m[:, 5]))
                chain(dve.tensor_scalar(row_m[:, 5], row_m[:, 5], tg[:, 7:8], None, ALU.mult))
                for j in range(2):
                    e = dve.tensor_tensor(row_m[:, j], row_m[:, 3 + j], row_m[:, 5], ALU.mult)
                chain(e)
                running_counts(2 * E3, lambda _, e: chain(e), 0, r)
                for j in range(2):
                    chain(dve.tensor_scalar(route[j][:], totals[:, :, j * E3:(j + 1) * E3], CAP3 + 0.5, None, ALU.is_le))
                    chain(dve.tensor_tensor(route[j][:], route[j][:], flags[:, :, j], ALU.mult))
                    chain(dve.tensor_tensor(route[j][:], route[j][:], bc_row(row_m[:, j]), ALU.mult))
                dve.tensor_tensor(coef[:], route[0][:], route[1][:], ALU.add).then_inc(s["coef_ready"], 1)

            def ffn3(n):
                dve.wait_ge(s["tg_ready"], 1)
                route3(n)
                dve.wait_ge(s["coef_ready"], rt_order[3] + 1)

                def experts(i):
                    for k in range(2):
                        e = 2 * i + k
                        dve.tensor_copy(c3e[k][:], coef[:, :, ds(e, 1)].squeeze(2)).then_inc(s["f3_c"], 1)
                        dve.wait_ge(s["f3_c"], e + 1)
                        for t in range(NT):
                            q = e * NT + t
                            dve.wait_ge(s["f3_down"], q + 1)
                            dve.scalar_tensor_tensor(X[:, t], down_ring[t % TPC][:, 0], c3e[k][:, t:t + 1], X[:, t], ALU.mult, ALU.add)\
                                .then_inc(s["f3_acc"], 1)

                with dve.Fori(0, E3 // 2) as i:
                    experts(i)
                dve.wait_ge(s["f3_acc"], E3 * NT)
                dve.sem_inc(s["x_ffn"], 1)

            for n, (kind, L) in enumerate(stages):
                if (kind, L) == ("ffn", 1):
                    ffn1_rhs()
                layernorm(n)
                if kind == "att":
                    attention(n, L)
                else:
                    (ffn0, ffn1, ffn2, ffn3)[L](n)


def layout(v):
    n = {k: np.asarray(x) for k, x in v.items()}
    o = {"x": n["x"].reshape(T, D), "g_xattn": n["g_xattn"], "g_ffn": n["g_ffn"]}

    def rows(w):
        c, m = w.shape
        return w.reshape(c // P, P, m).transpose(1, 0, 2)

    o["ctxT"] = rows(n["ctx_1024"].reshape(T, D).T)
    mask = n["mask_1x1xSxS2_bk1"].reshape(S, S)
    o["mask_qk"], o["mask_kq"] = rows(mask), rows(mask.T)
    pad = n["mask_BxS2_bf0"]
    o["pad"], o["padT"] = pad, rows(pad.T)
    def heads(w):
        lead = w.shape[:-1]
        k = len(lead)
        w = w.reshape(lead + (HPH, HALF, DH))
        return w.transpose(tuple(range(k)) + (k + 1, k + 2, k)).reshape(lead + (D,))

    def padded(w):
        z = np.zeros((H, VW, D), w.dtype)
        z[:, :DH] = w.reshape(H, DH, D)
        return rows(z.reshape(H * VW, D))

    zeros = np.zeros(D, n["x"].dtype)
    kv = n["L3_xattn_Wkv"]
    ws = [
        (n["L0_xattn_Wq"].T, n["L0_xattn_Wk"].T, n["L0_xattn_Wv"].T, n["L0_xattn_Wo"].T, zeros, zeros, zeros, zeros),
        (n["L1_xattn_Wq_w"].T, n["L1_xattn_Wk_w"].T, n["L1_xattn_Wv_w"].T, n["L1_xattn_Wo_w"].T,
         n["L1_xattn_Wq_b"], n["L1_xattn_Wk_b"], n["L1_xattn_Wv_b"], n["L1_xattn_Wo_b"]),
        (n["L2_xattn_wq"].T, n["L2_xattn_wk"].T, n["L2_xattn_wv"].T, n["L2_xattn_wo"].T,
         n["L2_xattn_bq"], n["L2_xattn_bk"], n["L2_xattn_bv"], n["L2_xattn_bo"]),
        (n["L3_xattn_Wq"], kv[:, :D], kv[:, D:], n["L3_xattn_Wo"], n["L3_xattn_bq"],
         n["L3_xattn_bkv"][:D], n["L3_xattn_bkv"][D:], n["L3_xattn_bo"]),
    ]
    for L, (q, k, w, wo_, bq_, bk_, bv_, bo_) in enumerate(ws):
        o[f"wq{L}"], o[f"wk{L}"], o[f"wv{L}"] = rows(heads(q)), rows(heads(k)), rows(w)
        o[f"wo{L}"] = rows(wo_) if L in SOFTMAX_KEYS else padded(wo_)
        o[f"bq{L}"], o[f"bk{L}"] = heads(bq_).reshape(HALF, P).T, heads(bk_).reshape(HALF, P).T
        o[f"bv{L}"], o[f"bo{L}"] = bv_, bo_
    o["wr0"], o["br0"] = rows(n["L0_ffn_Wr"]), n["L0_ffn_br"]
    z = np.zeros((NG0, D, FT0 * P), n["x"].dtype)
    z[:, :, :F0] = n["L0_ffn_W_up"]
    o["wu0"] = z.reshape(NG0, KC, P, FT0 * P).transpose(2, 0, 1, 3)
    z = np.zeros((NG0, FT0 * P), n["x"].dtype)
    z[:, :F0] = n["L0_ffn_b_up"]
    o["bu0"] = z.reshape(NG0, FT0, P).transpose(2, 0, 1)
    z = np.zeros((E0, FT0 * P, D), n["x"].dtype)
    z[:, :F0], z[:, F0] = n["L0_ffn_W_down"], n["L0_ffn_b_down"]
    o["wd0"] = z.reshape(E0, FT0, P, D).transpose(2, 0, 1, 3)
    o["rhs1"] = rows(n["L1_ffn_rhs"])
    for name, key in (("w1_2", "w1"), ("w2_2", "w2"), ("h1_2", "h1"), ("h2_2", "h2"), ("w3_2", "w3")):
        o[name] = rows(n[f"L2_ffn_{key}_w"].T)
    o["sc2"] = np.stack([n[f"L2_ffn_{key}_s"].reshape(HT, P).T for key in ("w1", "w2", "h1", "h2")], 1)
    o["s3_2"] = n["L2_ffn_w3_s"]
    o["wr3"] = rows(n["L3_ffn_router_w"].T)
    o["w1_3"] = n["L3_ffn_w1"].reshape(E3, KC, P, HID).transpose(0, 2, 1, 3)
    o["w2_3"] = n["L3_ffn_w2"].reshape(E3, HT, P, D).transpose(0, 2, 1, 3)
    return {k: np.ascontiguousarray(x) for k, x in o.items()}


STAGES = [("att", 0), ("ffn", 0), ("att", 1), ("ffn", 1), ("att", 2), ("ffn", 2), ("att", 3), ("ffn", 3)]


def kernel(**inputs):
    import concourse.bacc as bacc
    from concourse.bass_utils import run_bass_kernel_spmd

    nc = bacc.Bacc("TRN2", target_bir_lowering=False, num_devices=1)
    arrays = {f"in_{k}": x for k, x in layout(inputs).items()}
    args = {k[3:]: nc.dram_tensor(k, x.shape, mybir.dt.from_np(x.dtype), kind="ExternalInput").ap() for k, x in arrays.items()}
    out = nc.dram_tensor("out", (T, D), F32, kind="ExternalOutput").ap()
    program(nc, args, out, STAGES)
    r = run_bass_kernel_spmd(nc, [arrays], core_ids=[0])
    return r.results[0]["out"].reshape(B, S, D)
```

```python
from contextlib import ExitStack

import numpy as np

import concourse.bass as bass
from concourse import mybir

F32 = mybir.dt.float32
BF16 = mybir.dt.bfloat16
I32 = mybir.dt.int32
U8 = mybir.dt.uint8
ALU = mybir.AluOpType
ACT = mybir.ActivationFunctionType
AX = mybir.AxisListType
ds = bass.ds

P = 128
D = 256
KC = D // P
B, S = 8, 256
T = B * S
NT = T // P
ST = S // P
H, DH = 16, 16
HALF = 2
HPH = H // HALF
GROUP = 4
CH = H // GROUP
VW = P // GROUP
EPS = 1e-5
Q_PARTS = (0, 0, 1, 1, 0, 2)
K_PARTS = (0, 1, 0, 1, 2, 0)
ROWS = DH * len(Q_PARTS)
MASK_ROW, MAX_ROW = ROWS, ROWS + 1
NEG_MAX = -1e30
NEG_EXP = -3e38
INV_SQRT = 1.0 / DH ** 0.5
SOFTMAX_KEYS = (0, 2)
E0, NG0, F0 = 8, 4, 682
FT0 = -(-F0 // P)
FL0 = F0 - (FT0 - 1) * P
TOP0 = T // E0
SL0 = TOP0 // P
HID = 1024
HT = HID // P
E3 = 8
CAP3 = max(1, int(1.25 * T / E3 * 2))
PAIRS3 = 2
TILES3 = -(-(T * PAIRS3 + E3 * (P - 1)) // P)
TILES3 += -TILES3 % 4
GBUF = 4
CHUNK = 512
NCH = T // CHUNK
TPC = CHUNK // P
SENT0 = 16
FREE = 1
MAGIC = 1.5 * 2.0 ** 23


def program(nc, a, out, stages):
    ctx = ExitStack()
    with ctx:
        def sem(name):
            return ctx.enter_context(nc.semaphore(name))

        def sb(name, shape, dt, c=ctx):
            return c.enter_context(nc.sbuf_tensor(name, shape, dt))

        X = sb("X", [P, NT, D], F32)
        XNT = sb("XNT", [P, KC, T], F32)
        tg = sb("tg", [P, 8], F32)
        ident = sb("ident", [P, P], F32)
        ident_bf = sb("ident_bf", [P, P], BF16)
        ln_st = sb("ln_st", [P, NT, 6], F32)
        ln_tmp = sb("ln_tmp", [P, 8, NT], F32)
        xn = [sb(f"xn{i}", [P, ST, D], F32) for i in range(2)]
        gb = sb("gb", [P, 8], F32)
        probs_e = sb("probs_e", [P, NT, E0], F32)
        route = [sb(f"route{i}", [P, NT, E0], F32) for i in range(6)]
        row_m = sb("row_m", [P, 6, NT], F32)
        flags = sb("flags", [P, NT, 2, E0], BF16)
        totals = sb("totals", [P, NT, 2 * E0], F32)
        sums = sb("sums", [P, NT, 2 * E0], F32)
        need = sb("need", [P, E0], F32)
        coef = sb("coef", [P, NT, E0], F32)
        rev = sb("rev", [P, E0], F32)
        rev_i = sb("rev_i", [P, E0], I32)
        ones_bf = sb("ones_bf", [P, P], BF16)
        upto = sb("upto", [P, P], BF16)
        ones_f = sb("ones_f", [P, NT], F32)
        col_i = sb("col_i", [P, P], I32)
        col = sb("col", [P, P], F32)
        row_i = sb("row_i", [P, 1], I32)
        row = sb("row", [P, 1], F32)
        spare = sb("spare", [P, 2], F32)

        att = ExitStack()
        ctxT = [sb(f"ctxT{i}", [P, KC, S], F32, att) for i in range(2)]
        wq = sb("wq", [P, KC, D], F32, att)
        wk = sb("wk", [P, KC, D], F32, att)
        wv = sb("wv", [P, KC, D], F32, att)
        wo = sb("wo", [P, CH, D], F32, att)
        bq = sb("bq", [P, HALF], F32, att)
        bq4 = sb("bq4", [P, HALF], F32, att)
        bk = sb("bk", [P, HALF], F32, att)
        bv = sb("bv", [P, D], F32, att)
        bo = sb("bo", [P, D], F32, att)
        bog = sb("bog", [P, D], F32, att)
        qf = sb("qf", [P, HALF, S], F32, att)
        kf = sb("kf", [P, HALF, S], F32, att)
        qr = sb("qr", [P, HALF, S], F32, att)
        kr = sb("kr", [P, HALF, S], F32, att)
        QP = sb("QP", [P, 3, HALF, S], BF16, att)
        KP = sb("KP", [P, 3, HALF, S], BF16, att)
        Qpack = [sb(f"Qpack{i}", [P, H, S], BF16, att) for i in range(2)]
        Kpack = [sb(f"Kpack{i}", [P, H, S], BF16, att) for i in range(2)]
        Vb = [sb(f"Vb{i}", [P, ST, D], F32, att) for i in range(2)]
        V = [sb(f"V{i}", [P, ST, H, VW], F32, att) for i in range(2)]
        On = sb("On", [P, CH, S], F32, att)
        rden = sb("rden", [P, ST, H], F32, att)
        Oq = sb("Oq", [P, ST, D], F32, att)
        OT = sb("OT", [P, HALF, S], F32, att)
        mx = sb("mx", [P, ST, H], F32, att)
        MR = sb("MR", [H, 2, S], BF16, att)
        zrow = sb("zrow", [1, H * S], BF16, att)
        mask_u8 = sb("mask_u8", [P, 2, ST, S], U8, att)
        mask_bf = sb("mask_bf", [P, 2, ST, S], BF16, att)
        pad_u8 = sb("pad_u8", [B, S], U8, att)
        pad_bf = sb("pad_bf", [B, S], BF16, att)
        padT_u8 = sb("padT_u8", [P, ST, B], U8, att)
        keep = sb("keep", [P, ST, B], F32, att)
        nmax = sb("nmax", [P, ST, H], F32, att)
        esum = sb("esum", [P, ST, H], F32, att)
        rsum = sb("rsum", [P, ST, H], F32, att)
        pt_ctx = ExitStack()
        pT = [sb(f"pT{i}", [P, ST, S], F32, pt_ctx) for i in range(8)]
        pt_ctx.close()
        probs = sb("probs", [P, ST, H, S], F32, att)
        M2 = sb("M2", [P, ST, 2, S], F32, att)
        M1 = sb("M1", [P, ST, S], F32, att)
        m1p = sb("m1p", [P, ST, 2, S], BF16, att)
        hs = sb("hs", [P, ST, 8, S], F32, att)
        nident_bf = sb("nident_bf", [P, P], BF16, att)
        att.close()

        f0c = ExitStack()
        wu0 = sb("wu0", [P, NG0, KC, FT0 * P], F32, f0c)
        wd0 = sb("wd0", [P, E0, FT0, D], F32, f0c)
        bu0 = sb("bu0", [P, NG0, FT0], F32, f0c)
        wr0 = sb("wr0", [P, KC, E0], F32, f0c)
        br0 = sb("br0", [P, E0], F32, f0c)
        mid0 = [sb(f"mid0_{i}", [P, FT0, TOP0], F32, f0c) for i in range(2)]
        pos_i = sb("pos_i", [P, NT, E0], I32, f0c)
        place_i = sb("place_i", [P, NT, E0], I32, f0c)
        half_i = sb("half_i", [P, NT, E0], I32, f0c)
        place0 = sb("place0", [P, NT, E0], F32, f0c)
        in_half = sb("in_half", [P, NT, E0, SL0], F32, f0c)
        lists0 = sb("lists0", [P, E0, NT, 5, SL0], BF16, f0c)
        gpart = [sb(f"gpart{i}", [P, NT, E0], BF16, f0c) for i in range(3)]
        grest = [sb(f"grest{i}", [P, NT, E0], F32, f0c) for i in range(2)]
        hot0 = [sb(f"hot0_{i}", [P, NT, P], BF16, f0c) for i in range(2)]
        idx0 = sb("idx0", [P, E0, SL0], I32, f0c)
        gate0 = sb("gate0", [P, E0, SL0], F32, f0c)
        gsum0 = sb("gsum0", [P, E0, SL0], F32, f0c)
        idl0 = sb("idl0", [P, E0, SL0], F32, f0c)
        xg0 = [sb(f"xg0_{i}", [P, SL0, D], F32, f0c) for i in range(GBUF)]
        xgT0 = [sb(f"xgT0_{i}", [P, KC, TOP0], F32, f0c) for i in range(2)]
        yg0 = [sb(f"yg0_{i}", [P, SL0, D], F32, f0c) for i in range(2)]
        thr = sb("thr", [P, E0], I32, f0c)
        cand = sb("cand", [P, E0], I32, f0c)
        step_i = sb("step_i", [P, E0], I32, f0c)
        step_f = sb("step_f", [P, E0], F32, f0c)
        taken = sb("taken", [P, E0], I32, f0c)
        cnt = sb("cnt", [P, E0], F32, f0c)
        f0c.close()
        f1c = ExitStack()
        QT1 = sb("QT1", [P, KC, T], BF16, f1c)
        rhs1 = sb("rhs1", [P, KC, D], F32, f1c)
        rmax = sb("rmax", [P, D], F32, f1c)
        rall = sb("rall", [P, D], F32, f1c)
        rscale = sb("rscale", [P, D], F32, f1c)
        rinv = sb("rinv", [P, D], F32, f1c)
        rtmp = sb("rtmp", [P, KC, D], F32, f1c)
        qrhs = sb("qrhs", [P, KC, D], BF16, f1c)
        lmax = sb("lmax", [P, NT], F32, f1c)
        lscale = sb("lscale", [P, NT], F32, f1c)
        linv = sb("linv", [P, NT], F32, f1c)
        qn = [sb(f"qn{i}", [P, ST, D], BF16, f1c) for i in range(2)]
        y1 = [sb(f"y1_{i}", [P, ST, D], F32, f1c) for i in range(2)]
        f1c.close()
        f2c = ExitStack()
        w1_2 = sb("w1_2", [P, KC, HID], F32, f2c)
        w2_2 = sb("w2_2", [P, KC, HID], F32, f2c)
        h1_2 = sb("h1_2", [P, HT, HID], F32, f2c)
        h2_2 = sb("h2_2", [P, HT, HID], F32, f2c)
        w3_2 = sb("w3_2", [P, HT, D], F32, f2c)
        sc2 = sb("sc2", [P, 4, HT], F32, f2c)
        s3_2 = sb("s3_2", [P, D], F32, f2c)
        hA = sb("hA", [P, HT, CHUNK], F32, f2c)
        hB = sb("hB", [P, HT, CHUNK], F32, f2c)
        sil = [sb(f"sil{i}", [P, CHUNK], F32, f2c) for i in range(2)]
        y2 = [sb(f"y2_{i}", [P, D], F32, f2c) for i in range(2)]
        f2c.close()
        f3c = ExitStack()
        w1_3 = sb("w1_3", [P, E3, KC, HID], F32, f3c)
        w2_3 = sb("w2_3", [P, E3, HT, D], F32, f3c)
        wr3 = sb("wr3", [P, KC, E3], F32, f3c)
        kept = [sb(f"kept{i}", [P, NT, E3], F32, f3c) for i in range(PAIRS3)]
        count3 = sb("count3", [P, PAIRS3, E3], F32, f3c)
        load3 = sb("load3", [P, E3], F32, f3c)
        load3_i = sb("load3_i", [P, E3], I32, f3c)
        tiles3 = sb("tiles3", [P, E3], F32, f3c)
        upto3 = sb("upto3", [P, E3], F32, f3c)
        start3 = sb("start3", [P, PAIRS3, E3], F32, f3c)
        slot3 = sb("slot3", [P, PAIRS3, NT], F32, f3c)
        slot3_i = sb("slot3_i", [P, PAIRS3, NT], I32, f3c)
        place3_i = sb("place3_i", [P, PAIRS3, NT], I32, f3c)
        tile3_i = sb("tile3_i", [P, PAIRS3, NT], I32, f3c)
        place3 = sb("place3", [P, PAIRS3, NT], F32, f3c)
        tile3 = sb("tile3", [P, PAIRS3, NT], F32, f3c)
        part3 = [sb(f"part3_{i}", [P, PAIRS3, NT], BF16, f3c) for i in range(3)]
        rest3 = [sb(f"rest3_{i}", [P, PAIRS3, NT], F32, f3c) for i in range(2)]
        idx3 = sb("idx3", [P, TILES3], I32, f3c)
        idl3 = [sb(f"idl3_{i}", [P, TILES3], F32, f3c) for i in range(2)]
        gate3 = [sb(f"gate3_{i}", [P, TILES3], F32, f3c) for i in range(2)]
        before3 = sb("before3", [P, TILES3, E3], F32, f3c)
        expert3 = sb("expert3", [P, TILES3], F32, f3c)
        expert3_i = sb("expert3_i", [P, TILES3], I32, f3c)
        l3c = ExitStack()
        hot3 = sb("hot3", [P, PAIRS3, NT, P], BF16, l3c)
        lists3 = sb("lists3", [P, PAIRS3, NT, 6, TILES3], BF16, l3c)
        l3c.close()
        xg3 = [sb(f"xg3_{i}", [P, D], F32, f3c) for i in range(GBUF)]
        xgT3 = [sb(f"xgT3_{i}", [P, KC, P], F32, f3c) for i in range(2)]
        mid3 = [sb(f"mid3_{i}", [P, HID], F32, f3c) for i in range(2)]
        midT3 = [sb(f"midT3_{i}", [P, HT, P], F32, f3c) for i in range(2)]
        yg3 = [sb(f"yg3_{i}", [P, D], F32, f3c) for i in range(2)]
        f3c.close()
        ps = [ctx.enter_context(nc.psum_tensor(f"ps{i}", [P, 2, S], F32)) for i in range(8)]
        P0, P1 = ps[0], ps[1]
        A = ps[2:6]
        O = ps[6:8]
        up_ring, down_ring = ps[0:4], ps[4:8]

        x_rows = nc.dram_tensor("x_rows", (T + P, D), F32, kind="Internal").ap()
        xn_rows = nc.dram_tensor("xn_rows", (T + P, D), F32, kind="Internal").ap()
        pad_dram = nc.dram_tensor("pad_rows", (B, S), BF16, kind="Internal").ap()

        names = ("x_loaded const_ready ident_ready tg_ready gates_loaded ln_stats ln_std ln_rstd ln_mid xn_ready "
                 "xnt_psum xnt_done w_loaded bias_ready bias_added ctx0 ctx1 q_psum k_psum v_psum q_evac k_evac q_r1 "
                 "k_r1 q_mid k_mid q_split k_split pack0 pack1 padrow0 padrow1 v_copied v_ready smax_ps smax_done mT_ps m_hi m_lo mrow0 "
                 "mrow1 st_ps exp_done av_done o_out oT_ps on_rden on_norm o2_ps on_ready y_ps x_res mask_loaded mask_ready pad_out st_max "
                 "nmax_ready rsum_ready vs_ready p1_ps p1_max m1_step m1_ready p2_ps exp1_done sum1_step norm1 av1_done x_ffn stored "
                 "pack_const zero_row rt_const rt_logits rt_step rt_exp rt_cnt rt_prefix coef_ready thr_step thr_cmp thr_cnt "
                 "xn_out0 xn_out1 rows_ready "
                 "f0_router f0_w0 f0_w1 f0_w2 f0_w3 f0_step f0_hot f0_list f0_idstep f0_idx f0_gather0 f0_gather1 f0_gather2 f0_gather3 "
                 "f0_xt f0_xgT f0_up f0_mid f0_down f0_yg f0_scatter x_back "
                 "f1_rhs f1_rmax f1_rall f1_rstep f1_qrhs f1_qstep f1_ps f1_y f1_acc "
                 "f2_w f2_up f2_sil f2_hA f2_mm f2_act f2_yps f2_y f2_acc "
                 "f3_router f3_w0 f3_w1 f3_w2 f3_w3 f3_w4 f3_w5 f3_w6 f3_w7 f3_loaded f3_hot f3_list f3_idx f3_gather0 f3_gather1 f3_gather2 "
                 "f3_gather3 f3_xt f3_xgT f3_up f3_mid f3_mT f3_midT f3_down f3_yg f3_scatter").split()
        s = {n: sem(n) for n in names}
        ctx_sem = [s["ctx0"], s["ctx1"]]
        pack = [s["pack0"], s["pack1"]]
        padrow = [s["padrow0"], s["padrow1"]]
        mrow = [s["mrow0"], s["mrow1"]]
        xn_out = [s["xn_out0"], s["xn_out1"]]
        GATHERED = (("ffn", 0), ("ffn", 3))
        g_order = {st: i for i, st in enumerate([st for st in stages if st in GATHERED])}

        def wait(eng, semaphore, value):
            if not isinstance(value, int) or value > 0:
                eng.wait_ge(semaphore, value)

        n_att = [L for kind, L in stages if kind == "att"]
        order = {("att", L): i for i, L in enumerate(n_att)}
        m_order = {L: i for i, L in enumerate([L for L in n_att if L in SOFTMAX_KEYS])}
        s_order = {L: i for i, L in enumerate([L for L in n_att if L != 1])}
        ln_order = {st: i for i, st in enumerate(stages)}
        PACKS = 16 * 2 * len(Q_PARTS)

        def bval(b):
            return b if isinstance(b, int) else b[0]

        def ready_x(eng, n):
            if n == 0:
                eng.wait_ge(s["x_loaded"], 16)
                return
            kind, L = stages[n - 1]
            if kind == "att":
                eng.wait_ge(s["x_res"], FREE + 8 * (order["att", L] + 1))
            else:
                eng.wait_ge(s["x_ffn"], 1 + sum(k != "att" for k, _ in stages[:n - 1]))

        def slots(eng, slot):
            slot(0, 0)
            with eng.Fori(0, 3) as i:
                slot((1 + 2 * i, i), 1)
                slot((2 + 2 * i, i + 1), 0)
            slot(7, 1)

        block = ctx.enter_context(nc.Block())

        @block.sync
        def _(sp):
            for j in range(2):
                sp.sem_inc(xn_out[j], SENT0)
            sp.dma_start(X[:], a["x"].rearrange("(t p) c -> p t c", p=P)).then_inc(s["x_loaded"], 16)
            sp.dma_start(gb[:, 0:4], a["g_xattn"].partition_broadcast(P)).then_inc(s["gates_loaded"], 16)
            sp.dma_start(gb[:, 4:8], a["g_ffn"].partition_broadcast(P)).then_inc(s["gates_loaded"], 16)
            if ("att", 0) in stages:
                sp.dma_start(mask_u8[:, 0], a["mask_qk"]).then_inc(s["mask_loaded"], 16)
                sp.dma_start(mask_u8[:, 1], a["mask_kq"]).then_inc(s["mask_loaded"], 16)

            def load_ctx(b, par):
                sp.dma_start(ctxT[par][:], a["ctxT"][:, :, ds(b * S, S)]).then_inc(ctx_sem[par], 16)

            def attention(n, L):
                i = order["att", L]
                if n > 0:
                    ready_x(sp, n)
                for w, name in ((wq[:], "wq"), (wk[:], "wk"), (wv[:], "wv"), (bq[:], "bq"), (bk[:], "bk"),
                                (wo[:, 0:HALF] if L in SOFTMAX_KEYS else wo[:], "wo")):
                    sp.dma_start(w, a[f"{name}{L}"]).then_inc(s["w_loaded"], 16)
                for w, name in ((bv, "bv"), (bo, "bo")):
                    sp.dma_start(w[:], a[f"{name}{L}"].partition_broadcast(P)).then_inc(s["w_loaded"], 16)
                if L == 2:
                    sp.dma_start(pad_u8[:], a["pad"]).then_inc(s["w_loaded"], 16)
                    sp.dma_start(padT_u8[:], a["padT"]).then_inc(s["w_loaded"], 16)
                    sp.wait_ge(s["mask_ready"], 1 + (("att", 0) in stages))
                    sp.dma_start(pad_dram, pad_bf[:]).then_inc(s["pad_out"], 16)
                    sp.wait_ge(s["pad_out"], 16)
                if L == 0:
                    sp.wait_ge(s["zero_row"], 1)
                sp.wait_ge(s["pack_const"], i + 1)

                def packs(bb, par):
                    g = 8 * i + bb
                    sp.wait_ge(s["q_split"], g + 1)
                    for j, part in enumerate(Q_PARTS):
                        sp.dma_start(Qpack[par][DH * j:DH * (j + 1)].rearrange("d (e f) t -> d e (f t)", f=HALF),
                                     QP[:, part]).then_inc(pack[par], 16)
                    sp.wait_ge(s["k_split"], g + 1)
                    for j, part in enumerate(K_PARTS):
                        sp.dma_start(Kpack[par][DH * j:DH * (j + 1)].rearrange("d (e f) t -> d e (f t)", f=HALF),
                                     KP[:, part]).then_inc(pack[par], 16)
                    if L == 2:
                        sp.dma_start(Kpack[par][MASK_ROW:MASK_ROW + 1],
                                     pad_dram[ds(bb, 1), :].unsqueeze(1).to_broadcast([1, H, S])).then_inc(padrow[par], 16)
                    if L == 0:
                        sp.dma_start(Kpack[par][MASK_ROW:MASK_ROW + 1],
                                     zrow[:].rearrange("o (h t) -> o h t", h=H)).then_inc(padrow[par], 16)

                def max_rows(bb, par):
                    m = 8 * m_order[L] + bb
                    sp.wait_ge(s["m_hi"], m + 1)
                    sp.wait_ge(s["m_lo"], m + 1)
                    for r in range(2):
                        sp.dma_start(Qpack[par][MAX_ROW + r:MAX_ROW + r + 1], MR[:, r]).then_inc(mrow[par], 16)

                load_ctx(0, 0)
                load_ctx(1, 1)
                packs(0, 0)
                if L in SOFTMAX_KEYS:
                    max_rows(0, 0)

                def slot(b, par, refill):
                    if refill:
                        sp.wait_ge(s["v_psum"], 8 * i + b + 1)
                        load_ctx(b + 2, par)
                    packs(b + 1, 1 - par)
                    if L in SOFTMAX_KEYS:
                        max_rows(b + 1, 1 - par)

                slot(0, 0, True)
                with sp.Fori(0, 2) as k:
                    slot(1 + 2 * k, 1, True)
                    slot(2 + 2 * k, 0, True)
                slot(5, 1, True)
                slot(6, 0, False)

            def send_rows(n):
                for part in range(4):
                    tiles = slice(part * NT // 4, (part + 1) * NT // 4)
                    sp.dma_start(x_rows[0:T].rearrange("(t p) c -> p t c", p=P)[:, tiles], X[:, tiles]).then_inc(s["rows_ready"], 16)
                sp.dma_start(x_rows[T:T + P], X[:, 0]).then_inc(s["rows_ready"], 16)
                sp.dma_start(xn_rows[T:T + P], X[:, 0]).then_inc(s["rows_ready"], 16)
                table = xn_rows[0:T].rearrange("(t p) c -> p t c", p=P)
                with sp.Fori(0, NT // (2 * ST)) as t:
                    for j in range(2):
                        sp.wait_ge(s["xn_ready"], 8 * n + 2 * t + j + 1)
                        sp.dma_start(table[:, ds(ST * (2 * t + j), ST)], xn[j][:]).then_inc(xn_out[j], 16)

            def ffn(n, L):
                ready_x(sp, n)
                if L == 0:
                    sp.dma_start(wr0[:], a["wr0"]).then_inc(s["f0_router"], 16)
                    sp.dma_start(br0[:], a["br0"].partition_broadcast(P)).then_inc(s["f0_router"], 16)
                    sp.dma_start(bu0[:], a["bu0"]).then_inc(s["f0_router"], 16)
                    send_rows(n)
                    for g in range(NG0):
                        sp.dma_start(wu0[:, g], a["wu0"][:, g]).then_inc(s[f"f0_w{g}"], 16)
                        sp.dma_start(wd0[:, 2 * g:2 * g + 2], a["wd0"][:, 2 * g:2 * g + 2]).then_inc(s[f"f0_w{g}"], 16)
                    sp.wait_ge(s["f0_scatter"], 16 * SL0 * E0)
                    sp.dma_start(X[:], x_rows[0:T].rearrange("(t p) c -> p t c", p=P)).then_inc(s["x_back"], 16)
                elif L == 1:
                    sp.dma_start(rhs1[:], a["rhs1"]).then_inc(s["f1_rhs"], 16)
                elif L == 2:
                    for w, name in ((sc2, "sc2"), (w1_2, "w1_2"), (w2_2, "w2_2"), (h1_2, "h1_2"), (h2_2, "h2_2"), (w3_2, "w3_2")):
                        sp.dma_start(w[:], a[name]).then_inc(s["f2_w"], 16)
                    sp.dma_start(s3_2[:], a["s3_2"].partition_broadcast(P)).then_inc(s["f2_w"], 16)
                else:
                    sp.dma_start(wr3[:], a["wr3"]).then_inc(s["f3_router"], 16)
                    send_rows(n)
                    for e in range(E3):
                        sp.dma_start(w1_3[:, e], a["w1_3"][e]).then_inc(s[f"f3_w{e}"], 16)
                        sp.dma_start(w2_3[:, e], a["w2_3"][e]).then_inc(s[f"f3_w{e}"], 16)
                        sp.wait_ge(s[f"f3_w{e}"], 32)
                        sp.sem_inc(s["f3_loaded"], 1)

            for n, (kind, L) in enumerate(stages):
                if kind == "att":
                    attention(n, L)
                else:
                    ffn(n, L)
            if stages[-1] == ("ffn", 3):
                sp.wait_ge(s["f3_scatter"], 16 * TILES3)
                sp.dma_start(out, x_rows[0:T]).then_inc(s["stored"], 16)
            else:
                ready_x(sp, len(stages))
                sp.dma_start(out.rearrange("(t p) c -> p t c", p=P), X[:]).then_inc(s["stored"], 16)
            sp.wait_ge(s["stored"], 16)

        @block.gpsimd
        def _(pool):
            pool.memset(ident[:], 0.0).then_inc(s["ident_ready"], 1)
            pool.wait_ge(s["ident_ready"], 1)
            pool.affine_select(out=ident[:], in_=ident[:], compare_op=ALU.not_equal, fill=1.0, base=0,
                               pattern=[[-1, P]], channel_multiplier=1).then_inc(s["ident_ready"], 1)
            pool.wait_ge(s["ident_ready"], 2)
            pool.tensor_copy(ident_bf[:], ident[:]).then_inc(s["ident_ready"], 1)
            pool.memset(ones_f[:], 1.0)
            pool.memset(upto[:], 1.0)
            pool.memset(ones_bf[:], 1.0).then_inc(s["rt_const"], 1)
            pool.wait_ge(s["rt_const"], 1)
            pool.affine_select(out=upto[:], in_=upto[:], compare_op=ALU.is_ge, fill=0.0, base=0,
                               pattern=[[1, P]], channel_multiplier=-1)
            pool.iota(rev_i[:], pattern=[[-1, E0]], base=E0, channel_multiplier=0).then_inc(s["rt_const"], 1)
            pool.wait_ge(s["rt_const"], 2)
            pool.tensor_copy(rev[:], rev_i[:])
            pool.iota(col_i[:], pattern=[[1, P]], base=0, channel_multiplier=0)
            pool.iota(row_i[:], pattern=[[0, 1]], base=0, channel_multiplier=1).then_inc(s["rt_const"], 1)
            pool.wait_ge(s["rt_const"], 3)
            pool.tensor_copy(col[:], col_i[:])
            pool.tensor_copy(row[:], row_i[:]).then_inc(s["rt_const"], 1)
            pool.wait_ge(s["rt_const"], 4)
            pool.tensor_scalar(spare[:, 0:1], row[:], float(T), None, ALU.add)
            pool.tensor_scalar(spare[:, 1:2], row[:], -1.0, -float(T), ALU.mult, ALU.add).then_inc(s["rt_const"], 1)

            def attention(n, L):
                i = order["att", L]
                if n > 0:
                    ready_x(pool, n)
                if L != 0:
                    pool.wait_ge(s["bias_ready"], i + 1)
                    pool.wait_ge(s["xn_ready"], 8 * (ln_order["att", L] + 1))
                    pool.tensor_tensor(X[:], X[:], bog[:].unsqueeze(1).to_broadcast([P, NT, D]), ALU.add)\
                        .then_inc(s["bias_added"], 1)

            def rows_sent(n):
                pool.wait_ge(s["rows_ready"], 6 * 16 * (g_order[stages[n]] + 1))
                for j in range(2):
                    pool.wait_ge(xn_out[j], SENT0 + 16 * NT // (2 * ST) * (g_order[stages[n]] + 1))

            def gather(to, index, done):
                pool.indirect_dma_start(out=to, out_offset=None, in_=xn_rows, in_offset=bass.IndirectOffsetOnAxis(ap=index, axis=0))\
                    .then_inc(done, 16)

            def scatter_add(frm, index, done):
                pool.indirect_dma_start(out=x_rows, out_offset=bass.IndirectOffsetOnAxis(ap=index, axis=0), in_=frm, in_offset=None,
                                        compute_op=ALU.add).then_inc(done, 16)

            def ffn0(n):
                rows_sent(n)
                def fetch(e):
                    pool.wait_ge(s["f0_idx"], e + 1)
                    wait(pool, s["f0_xt"], e - GBUF + 1)
                    for h in range(SL0):
                        gather(xg0[e % GBUF][:, h], idx0[:, e, h:h + 1], s[f"f0_gather{e % GBUF}"])
                for e in range(GBUF):
                    fetch(e)
                for e in range(E0):
                    pool.wait_ge(s["f0_yg"], e + 1)
                    wait(pool, s["f0_scatter"], 16 * SL0 * e)
                    for h in range(SL0):
                        scatter_add(yg0[e % 2][:, h], idx0[:, e, h:h + 1], s["f0_scatter"])
                    if e + GBUF < E0:
                        fetch(e + GBUF)

            def ffn3(n):
                rows_sent(n)
                pool.wait_ge(s["f3_idx"], 1)
                def fetch(t):
                    wait(pool, s["f3_xt"], t - GBUF + 1)
                    gather(xg3[t % GBUF][:], idx3[:, t:t + 1], s[f"f3_gather{t % GBUF}"])
                for t in range(GBUF):
                    fetch(t)
                for t in range(TILES3):
                    pool.wait_ge(s["f3_yg"], t + 1)
                    wait(pool, s["f3_scatter"], 16 * t)
                    scatter_add(yg3[t % 2][:], idx3[:, t:t + 1], s["f3_scatter"])
                    if t + GBUF < TILES3:
                        fetch(t + GBUF)

            for n, (kind, L) in enumerate(stages):
                if kind == "att":
                    attention(n, L)
                elif L in (0, 3):
                    (ffn0 if L == 0 else ffn3)(n)
                elif L == 1:
                    pool.wait_ge(s["f1_rmax"], 1)
                    pool.partition_all_reduce(rall[:], rmax[:], P, bass.bass_isa.ReduceOp.max).then_inc(s["f1_rall"], 1)

        @block.tensor
        def _(pe):
            pe.sem_inc(s["y_ps"], FREE)
            pe.wait_ge(s["ident_ready"], 3)

            def layernorm(n):
                with pe.Fori(0, 4) as t:
                    for j in range(2):
                        pair = 8 * n + 2 * t + j
                        pe.wait_ge(s["xn_ready"], pair + 1)
                        pe.wait_ge(s["xnt_done"], pair + 1)
                        if stages[n] == ("ffn", 1):
                            bank = ps[j][:].bitcast(BF16)
                            for tt in range(ST):
                                for c in range(KC):
                                    last = pe.transpose(bank[:, c, tt * P:(tt + 1) * P], qn[j][:, tt, c * P:(c + 1) * P], ident_bf[:])
                            last.then_inc(s["xnt_psum"], 1)
                            continue
                        for tt in range(ST):
                            for c in range(KC):
                                last = pe.transpose(ps[j][:, c, tt * P:(tt + 1) * P], xn[j][:, tt, c * P:(c + 1) * P], ident[:])
                        last.then_inc(s["xnt_psum"], 1)

            def attention(n, L):
                i = order["att", L]
                w_total = 16 * sum(8 + 2 * (l == 2) for l in n_att[:i + 1])

                def proj_q(b):
                    g = 8 * i + b
                    if not (isinstance(b, int) and b == 0):
                        if L in SOFTMAX_KEYS:
                            pe.wait_ge(s["m_lo"], 8 * m_order[L] + b)
                            pe.wait_ge(s["m_hi"], 8 * m_order[L] + b)
                        else:
                            pe.wait_ge(s["v_copied"], g)
                    for f in range(HALF):
                        for c in range(KC):
                            mm = pe.matmul(P0[:, f], wq[:, c, f * P:(f + 1) * P], XNT[:, c, ds(b * S, S)],
                                           start=c == 0, stop=c == KC - 1)
                    mm.then_inc(s["q_psum"], 1)

                def proj_kv(b, par, u):
                    g = 8 * i + b
                    pe.wait_ge(ctx_sem[par], 16 * (u + 1))
                    pe.wait_ge(s["x_res"], max(1, FREE + g - 2) if isinstance(b, int) else FREE + g - 2)
                    for f in range(HALF):
                        for c in range(KC):
                            mm = pe.matmul(P1[:, f], wk[:, c, f * P:(f + 1) * P], ctxT[par][:, c],
                                           start=c == 0, stop=c == KC - 1)
                    mm.then_inc(s["k_psum"], 1)
                    pe.wait_ge(s["q_evac"], g + 1)
                    for t in range(ST):
                        for c in range(KC):
                            mm = pe.matmul(P0[:, t], ctxT[par][:, c, t * P:(t + 1) * P], wv[:, c],
                                           start=c == 0, stop=c == KC - 1)
                    mm.then_inc(s["v_psum"], 1)

                def smax(b, par, u, h):
                    m = 8 * m_order[L] + b
                    if h == 0:
                        pe.wait_ge(pack[par], PACKS * (u + 1))
                        pe.wait_ge(padrow[par], 16 * (4 * m_order[L] + u - 4 * i + 1))
                    wait(pe, s["smax_done"], 16 * m + h - 1)
                    for t in range(ST):
                        mm = pe.matmul(A[2 + h % 2][:, t], Qpack[par][0:MASK_ROW + 1, h, t * P:(t + 1) * P],
                                       Kpack[par][0:MASK_ROW + 1, h], start=True, stop=L != 0)
                        if L == 0:
                            mm = pe.matmul(A[2 + h % 2][:, t], ident_bf[:], mask_bf[:, 0, t], start=False, stop=True)
                    mm.then_inc(s["smax_ps"], 1)

                def max_turn(b):
                    m = 8 * m_order[L] + b
                    pe.wait_ge(s["smax_done"], 16 * (m + 1))
                    pe.wait_ge(s["v_copied"], 8 * i + b + 1)
                    for t in range(ST):
                        mm = pe.transpose(P0[0:H, 0, t * P:(t + 1) * P], mx[:, t], ident[:])
                    mm.then_inc(s["mT_ps"], 1)

                def scores(b, par, u, h):
                    q = 16 * (8 * s_order[L] + b) + h
                    if h == 0:
                        if L in SOFTMAX_KEYS:
                            pe.wait_ge(mrow[par], 32 * (4 * m_order[L] + u - 4 * i + 1))
                        else:
                            pe.wait_ge(pack[par], PACKS * (u + 1))
                    rows = MAX_ROW + 2 if L in SOFTMAX_KEYS else ROWS
                    ring = 2 if L in SOFTMAX_KEYS else 4
                    wait(pe, s["exp_done"], q - ring + 1)
                    for t in range(ST):
                        mm = pe.matmul(A[h % ring][:, t], Kpack[par][0:rows, h, t * P:(t + 1) * P],
                                       Qpack[par][0:rows, h], start=True, stop=L != 0)
                        if L == 0:
                            mm = pe.matmul(A[h % ring][:, t], ident_bf[:], mask_bf[:, 1, t], start=False, stop=True)
                    mm.then_inc(s["st_ps"], 1)

                def values(b, par, h):
                    q = 16 * (8 * s_order[L] + b) + h
                    g = 8 * i + b
                    if h == 0:
                        wait(pe, s["on_ready"], g)
                    if L in SOFTMAX_KEYS:
                        if h == 0:
                            if L == 0:
                                pe.wait_ge(s["v_copied"], g + 1)
                            else:
                                pe.wait_ge(s["v_ready"], 8 * sum(l in (1, 2) for l in n_att[:i]) + b + 1)
                        pe.wait_ge(s["exp_done"], q + 1)
                    elif h % GROUP == 0:
                        pe.wait_ge(s["vs_ready"], 4 * b + h // GROUP + 1)
                    c, r = h // GROUP, VW * (h % GROUP)
                    for t in range(ST):
                        mm = pe.matmul(O[c // 2][r:r + VW, c % 2], V[par][:, t, h], pT[h % (4 if L in SOFTMAX_KEYS else 8)][:, t],
                                       start=t == 0, stop=t == ST - 1)
                    mm.then_inc(s["av_done"], 1)

                def output_turn(b):
                    pe.wait_ge(s["o_out"], 8 * m_order[L] + b + 1)
                    for t in range(ST):
                        for c in range(CH):
                            mm = pe.transpose(O[t][:].rearrange("p a b -> p (a b)")[:, c * P:(c + 1) * P],
                                              On[:, c, t * P:(t + 1) * P], ident[:])
                    mm.then_inc(s["oT_ps"], 1)

                def output_back(b):
                    pe.wait_ge(s["on_norm"], 8 * m_order[L] + b + 1)
                    for f in range(HALF):
                        for t in range(ST):
                            mm = pe.transpose(O[0][:, f, t * P:(t + 1) * P], Oq[:, t, f * P:(f + 1) * P], ident[:])
                    mm.then_inc(s["o2_ps"], 1)

                def output(b):
                    g = 8 * i + b
                    pe.wait_ge(s["on_ready"], g + 1)
                    if isinstance(b, int) and b >= 6:
                        pe.wait_ge(s["x_res"], FREE + g)
                    else:
                        pe.wait_ge(s["k_evac"], g + 3)
                    tiles, lhs = (HALF, OT) if L in SOFTMAX_KEYS else (CH, On)
                    for t in range(ST):
                        for c in range(tiles):
                            mm = pe.matmul(P1[:, t], lhs[:, c, t * P:(t + 1) * P], wo[:, c], start=c == 0, stop=c == tiles - 1)
                    mm.then_inc(s["y_ps"], 1)

                def heads1(b, par, u):
                    pe.wait_ge(pack[par], PACKS * (u + 1))
                    for t in range(ST):
                        for e in range(H // 2):
                            k = 8 * t + e
                            if k < 4:
                                wait(pe, s["exp1_done"], 16 * b)
                            else:
                                pe.wait_ge(s["p1_max"], 16 * b + k - 3)
                            for f in range(2):
                                mm = pe.matmul(A[k % 4][:, f], Kpack[par][0:ROWS, 2 * e + f, t * P:(t + 1) * P],
                                               Qpack[par][0:ROWS, 2 * e + f], start=True, stop=True)
                            mm.then_inc(s["p1_ps"], 1)
                    for t in range(ST):
                        pe.wait_ge(s["m1_ready"], 2 * b + t + 1)
                        if t == 0:
                            pe.wait_ge(s["p1_max"], 16 * (b + 1))
                        for e in range(H // 2):
                            k = 8 * t + e
                            if k >= 4:
                                pe.wait_ge(s["exp1_done"], 16 * b + k - 3)
                            for f in range(2):
                                pe.matmul(A[k % 4][:, f], Kpack[par][0:ROWS, 2 * e + f, t * P:(t + 1) * P],
                                          Qpack[par][0:ROWS, 2 * e + f], start=True, stop=False)
                                for r in range(2):
                                    mm = pe.matmul(A[k % 4][:, f], nident_bf[:], m1p[:, t, r], start=False, stop=r == 1)
                            mm.then_inc(s["p2_ps"], 1)
                    pe.wait_ge(s["norm1"], 2 * (b + 1))
                    pe.wait_ge(s["v_ready"], 8 * sum(l in (1, 2) for l in n_att[:i]) + b + 1)
                    wait(pe, s["on_ready"], 8 * i + b)
                    for h in range(H):
                        c, r = h // GROUP, VW * (h % GROUP)
                        for t in range(ST):
                            mm = pe.matmul(O[c // 2][r:r + VW, c % 2], V[par][:, t, h], probs[:, t, h],
                                           start=t == 0, stop=t == ST - 1)
                        mm.then_inc(s["av1_done"], 1)

                pe.wait_ge(s["w_loaded"], w_total)
                pe.wait_ge(s["xnt_done"], 8 * (n + 1) + 2)
                if L == 0:
                    pe.wait_ge(s["mask_ready"], 1)
                proj_q(0)
                proj_kv(0, 0, 4 * i)
                if L in SOFTMAX_KEYS:
                    for h in range(H):
                        smax(0, 0, 4 * i, h)
                    max_turn(0)

                def slot(b, par):
                    bb = bval(b)
                    first = isinstance(b, int) and b == 0
                    last = isinstance(b, int) and b == 7
                    u = 4 * i + (b // 2 if isinstance(b, int) else b[1])
                    un = u + par
                    turned = L in SOFTMAX_KEYS and not first
                    if turned:
                        output_turn(bb - 1)
                    if not last:
                        proj_q(bb + 1)
                    if turned:
                        output_back(bb - 1)
                    if not last:
                        proj_kv(bb + 1, 1 - par, un)
                    if not first:
                        output(bb - 1)
                    if L == 1:
                        heads1(bb, par, u)
                        return
                    lag = 2 if L in SOFTMAX_KEYS else 2 * GROUP
                    for h in range(H):
                        scores(bb, par, u, h)
                        if L in SOFTMAX_KEYS and not last and h >= H // 2:
                            for k in range(2):
                                smax(bb + 1, 1 - par, un, 2 * (h - H // 2) + k)
                        if L in SOFTMAX_KEYS:
                            if h >= lag:
                                values(bb, par, h - lag)
                        elif h % GROUP == GROUP - 1 and h >= GROUP:
                            for k in range(GROUP):
                                values(bb, par, h - 2 * GROUP + 1 + k)
                    for h in range(H - (lag if L in SOFTMAX_KEYS else GROUP), H):
                        values(bb, par, h)
                    if L in SOFTMAX_KEYS and not last:
                        max_turn(bb + 1)

                slots(pe, slot)
                if L in SOFTMAX_KEYS:
                    output_turn(7)
                    output_back(7)
                output(7)

            rt_order = {L: i for i, L in enumerate([L for k, L in stages if k == "ffn" and L in (0, 3)])}

            def router(L, w):
                for t in range(NT):
                    for c in range(KC):
                        mm = pe.matmul(ps[0][:].rearrange("p a b -> p (a b)")[:, t * E0:(t + 1) * E0], XNT[:, c, t * P:(t + 1) * P],
                                       w[:, c], start=c == 0, stop=c == KC - 1)
                mm.then_inc(s["rt_logits"], 1)

            def counts(L, bank, cols):
                pe.matmul(bank[:, 0, 0:cols], upto[:], flags[:].rearrange("p t k e -> p (t k e)")[:, 0:cols], start=True, stop=True)
                pe.matmul(bank[:, 1, 0:cols], ones_bf[:], flags[:].rearrange("p t k e -> p (t k e)")[:, 0:cols], start=True, stop=True)\
                    .then_inc(s["rt_prefix"], 1)

            def ffn0(n):
                pe.wait_ge(s["xnt_done"], 8 * (n + 1) + 2)
                pe.wait_ge(s["f0_router"], 48)
                pe.wait_ge(s["rt_const"], 5)
                router(0, wr0)
                with pe.Fori(0, 30) as i:
                    pe.wait_ge(s["thr_cmp"], i + 1)
                    pe.matmul(ps[1][:, 0, 0:NT * E0], ones_bf[:], flags[:].rearrange("p t k e -> p (t k e)")[:, 0:NT * E0],
                              start=True, stop=True).then_inc(s["thr_cnt"], 1)
                pe.wait_ge(s["thr_cmp"], 31)
                counts(0, ps[2], 2 * NT * E0)

                def lists(e):
                    pe.wait_ge(s["f0_hot"], e + 1)
                    for t in range(NT):
                        mm = pe.matmul(ps[3 + e % 2][:, 0, 0:5 * SL0], hot0[e % 2][:, t],
                                       lists0[:, e, t].rearrange("p v h -> p (v h)"), start=t == 0, stop=t == NT - 1)
                    mm.then_inc(s["f0_list"], 1)

                def turn(e):
                    pe.wait_ge(s[f"f0_gather{e % GBUF}"], 16 * SL0 * (e // GBUF + 1))
                    wait(pe, s["f0_xgT"], e)
                    for h in range(SL0):
                        for c in range(KC):
                            mm = pe.transpose(ps[5][:, c, h * P:(h + 1) * P], xg0[e % GBUF][:, h, c * P:(c + 1) * P], ident[:])
                    mm.then_inc(s["f0_xt"], 1)

                def up(e):
                    pe.wait_ge(s[f"f0_w{e // 2}"], 32)
                    pe.wait_ge(s["f0_xgT"], e + 1)
                    for f in range(FT0):
                        wait(pe, s["f0_mid"], FT0 * e + f - 2)
                        for c in range(KC):
                            mm = pe.matmul(ps[f % 3][:, 0], wu0[:, e // 2, c, f * P:(f + 1) * P], xgT0[e % 2][:, c],
                                           start=c == 0, stop=c == KC - 1)
                        mm.then_inc(s["f0_up"], 1)

                def down(e):
                    pe.wait_ge(s["f0_mid"], FT0 * (e + 1))
                    wait(pe, s["f0_yg"], e - 1)
                    for h in range(SL0):
                        for f in range(FT0):
                            rows = P if f < FT0 - 1 else FL0 + 1
                            mm = pe.matmul(ps[6 + e % 2][:, h], mid0[e % 2][0:rows, f, h * P:(h + 1) * P],
                                           wd0[0:rows, e, f], start=f == 0, stop=f == FT0 - 1)
                    mm.then_inc(s["f0_down"], 1)

                lists(0)
                lists(1)
                turn(0)
                for e in range(E0):
                    if e + 2 < E0:
                        lists(e + 2)
                    up(e)
                    if e + 1 < E0:
                        turn(e + 1)
                    if e:
                        down(e - 1)
                down(E0 - 1)

            def ffn1(n):
                pe.wait_ge(s["xnt_done"], 8 * (n + 1) + 2)
                pe.wait_ge(s["f1_qrhs"], 1)

                def pair(b, j, first):
                    if not first:
                        pe.wait_ge(s["f1_y"], b - 1)
                    for t in range(ST):
                        for c in range(KC):
                            mm = pe.matmul(ps[2 + j][:, t], QT1[:, c, ds(b * S + t * P, P)], qrhs[:, c], start=c == 0, stop=c == KC - 1)
                    mm.then_inc(s["f1_ps"], 1)

                pair(0, 0, True)
                pair(1, 1, True)
                with pe.Fori(1, B // 2) as i:
                    for j in range(2):
                        pair(2 * i + j, j, False)

            def ffn2(n):
                pe.wait_ge(s["xnt_done"], 8 * (n + 1) + 2)
                pe.wait_ge(s["f2_w"], 16 * 7)

                def chunk(ch):
                    first = isinstance(ch, int)
                    for o in range(HT):
                        wait(pe, s["f2_hA"], ch * HT + o - 1)
                        for k, w in enumerate((w1_2, w2_2)):
                            bank = ps[2 * (o % 2) + k][:].rearrange("p a b -> p (a b)")
                            for c in range(KC):
                                mm = pe.matmul(bank, w[:, c, o * P:(o + 1) * P], XNT[:, c, ds(ch * CHUNK, CHUNK)],
                                               start=c == 0, stop=c == KC - 1)
                        mm.then_inc(s["f2_up"], 1)
                    for stage, (w, src) in enumerate(((h1_2, hA), (h2_2, hB))):
                        if stage == 0:
                            pe.wait_ge(s["f2_hA"], (ch + 1) * HT)
                        else:
                            pe.wait_ge(s["f2_act"], (2 * ch + 1) * HT)
                        for o in range(HT):
                            wait(pe, s["f2_act"], (2 * ch + stage) * HT + o - 1)
                            bank = ps[4 + o % 2][:].rearrange("p a b -> p (a b)")
                            for c in range(HT):
                                mm = pe.matmul(bank, w[:, c, o * P:(o + 1) * P], src[:, c], start=c == 0, stop=c == HT - 1)
                            mm.then_inc(s["f2_mm"], 1)
                    pe.wait_ge(s["f2_act"], (2 * ch + 2) * HT)
                    for t in range(TPC):
                        wait(pe, s["f2_y"], ch * TPC + t - 1)
                        for c in range(HT):
                            mm = pe.matmul(ps[6 + t % 2][:, 0], hA[:, c, t * P:(t + 1) * P], w3_2[:, c], start=c == 0, stop=c == HT - 1)
                        mm.then_inc(s["f2_yps"], 1)

                chunk(0)
                with pe.Fori(1, NCH) as ch:
                    chunk(ch)

            def ffn3(n):
                pe.wait_ge(s["xnt_done"], 8 * (n + 1) + 2)
                pe.wait_ge(s["f3_router"], 16)
                pe.wait_ge(s["rt_const"], 5)
                router(3, wr3)
                pe.wait_ge(s["rt_cnt"], 1)
                counts(3, ps[2], 2 * NT * E3)
                pe.wait_ge(s["f3_hot"], 1)
                for j in range(PAIRS3):
                    for t in range(NT):
                        mm = pe.matmul(ps[3][:].rearrange("p a b -> p (a b)")[:, 0:6 * TILES3], hot3[:, j, t],
                                       lists3[:, j, t].rearrange("p v i -> p (v i)"),
                                       start=j + t == 0, stop=j == PAIRS3 - 1 and t == NT - 1)
                mm.then_inc(s["f3_list"], 1)
                pe.wait_ge(s["f3_idx"], 1)

                def expert(t):
                    return pe.value_load(expert3_i[0:1, ds(t, 1)], min_val=0, max_val=E3 - 1)

                def turn(b, k):
                    t = GBUF * b + k
                    pe.wait_ge(s[f"f3_gather{k % GBUF}"], 16 * (b + k // GBUF + 1))
                    wait(pe, s["f3_xgT"], t - 1)
                    for c in range(KC):
                        mm = pe.transpose(ps[3 + k % 2][:, 0, c * P:(c + 1) * P], xg3[k % GBUF][:, c * P:(c + 1) * P], ident[:])
                    mm.then_inc(s["f3_xt"], 1)

                def up(b, k):
                    t = GBUF * b + k
                    e = expert(t)
                    pe.wait_ge(s["f3_loaded"], e + 1)
                    pe.wait_ge(s["f3_xgT"], t + 1)
                    wait(pe, s["f3_mid"], t)
                    for half in range(2):
                        for c in range(KC):
                            mm = pe.matmul(ps[half][:].rearrange("p a b -> p (a b)"), xgT3[k % 2][:, c],
                                           w1_3[:, ds(e, 1), c, half * CHUNK:(half + 1) * CHUNK].squeeze(1), start=c == 0, stop=c == KC - 1)
                    mm.then_inc(s["f3_up"], 1)

                def turn_mid(b, k):
                    t = GBUF * b + k
                    pe.wait_ge(s["f3_mid"], t + 1)
                    wait(pe, s["f3_midT"], t)
                    for c in range(HT):
                        mm = pe.transpose(ps[2 + 4 * (c // 4)][:].rearrange("p a b -> p (a b)")[:, (c % 4) * P:(c % 4 + 1) * P],
                                          mid3[k % 2][:, c * P:(c + 1) * P], ident[:])
                    mm.then_inc(s["f3_mT"], 1)

                def down(b, k):
                    t = GBUF * b + k
                    e = expert(t)
                    pe.wait_ge(s["f3_midT"], t + 1)
                    wait(pe, s["f3_yg"], t - 1)
                    for c in range(HT):
                        mm = pe.matmul(ps[5 + 2 * (k % 2)][:, 0], midT3[k % 2][:, c], w2_3[:, ds(e, 1), c].squeeze(1), start=c == 0, stop=c == HT - 1)
                    mm.then_inc(s["f3_down"], 1)

                def tiles(b):
                    first, last = (isinstance(b, int) and b == n for n in (0, BLOCKS - 1))
                    for k in range(GBUF):
                        if not last or k + 1 < GBUF:
                            up(b, k + 1)
                        if not last or k + 2 < GBUF:
                            turn(b, k + 2)
                        turn_mid(b, k)
                        if not first or k > 0:
                            down(b, k - 1)

                BLOCKS = TILES3 // GBUF
                turn(0, 0)
                up(0, 0)
                turn(0, 1)
                tiles(0)
                with pe.Fori(1, BLOCKS - 1) as b:
                    tiles(b)
                tiles(BLOCKS - 1)
                down(BLOCKS - 1, GBUF - 1)

            for n, (kind, L) in enumerate(stages):
                layernorm(n)
                if kind == "att":
                    attention(n, L)
                else:
                    (ffn0, ffn1, ffn2, ffn3)[L](n)

        @block.scalar
        def _(act):
            act.sem_inc(s["xnt_done"], 2)
            act.wait_ge(s["gates_loaded"], 32)
            act.activation(tg[:], gb[:], ACT.Tanh).then_inc(s["tg_ready"], 1)

            def layernorm(n):
                act.wait_ge(s["ln_mid"], 4 * n + 3)
                act.activation(ln_tmp[:, 5], ln_tmp[:, 4], ACT.Sqrt).then_inc(s["ln_std"], 1)
                with act.Fori(0, 4) as t:
                    for j in range(2):
                        pair = 8 * n + 2 * t + j
                        act.wait_ge(s["xnt_psum"], pair + 1)
                        if stages[n] == ("ffn", 1):
                            act.activation(QT1[:, :, ds((2 * t + j) * S, S)], ps[j][:].bitcast(BF16)[:, :, 0:S], ACT.Copy)\
                                .then_inc(s["xnt_done"], 1)
                            continue
                        act.activation(XNT[:, :, ds((2 * t + j) * S, S)], ps[j][:], ACT.Copy).then_inc(s["xnt_done"], 1)

            def attention(n, L):
                i = order["att", L]

                def split_q(b, par):
                    g = 8 * i + b
                    act.wait_ge(s["q_psum"], g + 1)
                    if isinstance(b, int) and b == 0:
                        act.wait_ge(s["bias_ready"], i + 1)
                    else:
                        act.wait_ge(pack[1 - par], PACKS * (4 * i + prev_uses(b, par)))
                        act.wait_ge(s["k_split"], g)
                    for f in range(HALF):
                        act.activation(qf[:, f], P0[:, f], ACT.Identity, bias=bq4[:, f:f + 1], scale=INV_SQRT)
                        e = act.activation(QP[:, 0, f], P0[:, f], ACT.Identity, bias=bq4[:, f:f + 1], scale=INV_SQRT)
                    e.then_inc(s["q_evac"], 1)

                def split_rest(b, par):
                    g = 8 * i + b
                    act.wait_ge(s["k_psum"], g + 1)
                    for f in range(HALF):
                        act.activation(kf[:, f], P1[:, f], ACT.Identity, bias=bk[:, f:f + 1])
                        e = act.activation(KP[:, 0, f], P1[:, f], ACT.Identity, bias=bk[:, f:f + 1])
                    e.then_inc(s["k_evac"], 1)
                    act.wait_ge(s["q_r1"], g + 1)
                    act.activation(QP[:, 1], qr[:], ACT.Copy).then_inc(s["q_mid"], 1)
                    act.wait_ge(s["k_r1"], g + 1)
                    act.activation(KP[:, 1], kr[:], ACT.Copy).then_inc(s["k_mid"], 1)

                cur = {}

                def prev_uses(b, par):
                    return cur["u_other"]

                def max_part(b, par):
                    m = 8 * m_order[L] + b
                    act.wait_ge(s["mT_ps"], m + 1)
                    if not (isinstance(b, int) and b == 0):
                        act.wait_ge(mrow[1 - par], 32 * (4 * m_order[L] + cur["u_other"]))
                    act.activation(MR[:, 0], P0[0:H, 0], ACT.Copy, scale=-1.0).then_inc(s["m_hi"], 1)

                def exps(b, h):
                    q = 16 * (8 * s_order[L] + b) + h
                    if L in SOFTMAX_KEYS:
                        act.wait_ge(s["st_ps"], q + 1)
                        wait(act, s["av_done"], q - 3)
                        act.activation(pT[h % 4][:], A[h % 2][:], ACT.Exp).then_inc(s["exp_done"], 1)
                    else:
                        act.wait_ge(s["nmax_ready"], 16 * b + h + 1)
                        wait(act, s["av_done"], q - 7)
                        for t in range(ST):
                            e = act.activation(pT[h % 8][:, t], A[h % 4][:, t], ACT.Exp, bias=nmax[:, t, h:h + 1],
                                               accum_out=esum[:, t, h:h + 1])
                        e.then_inc(s["exp_done"], 1)

                def exps1(b):
                    for t in range(ST):
                        for e in range(H // 2):
                            k = 8 * t + e
                            act.wait_ge(s["p2_ps"], 16 * b + k + 1)
                            if k == 0:
                                wait(act, s["av1_done"], 16 * b)
                            act.activation(probs[:, t, 2 * e:2 * e + 2], A[k % 4][:], ACT.Exp).then_inc(s["exp1_done"], 1)

                def outputs_out(b):
                    m = 8 * m_order[L] + b
                    act.wait_ge(s["av_done"], 16 * (8 * s_order[L] + b + 1))
                    wait(act, s["oT_ps"], m)
                    for c in range(2):
                        e = act.activation(On[:, 2 * c:2 * c + 2], O[c][:], ACT.Copy)
                    e.then_inc(s["o_out"], 1)

                def outputs_back(b):
                    act.wait_ge(s["o2_ps"], 8 * m_order[L] + b + 1)
                    act.wait_ge(s["y_ps"], FREE + 8 * i + b)
                    act.activation(OT[:], O[0][:], ACT.Copy).then_inc(s["on_ready"], 1)

                cur["u_other"] = 0
                split_q(0, 0)
                split_rest(0, 0)
                if L in SOFTMAX_KEYS:
                    max_part(0, 0)

                def slot(b, par):
                    bb = bval(b)
                    last = isinstance(b, int) and b == 7
                    u = b // 2 if isinstance(b, int) else b[1]
                    cur["u_other"] = u + 1
                    if not last:
                        split_q(bb + 1, 1 - par)
                    if L in SOFTMAX_KEYS and not (isinstance(b, int) and b == 0):
                        outputs_back(bb - 1)
                    if not last:
                        split_rest(bb + 1, 1 - par)
                    if L == 1:
                        exps1(bb)
                    else:
                        for h in range(H):
                            exps(bb, h)
                    if L in SOFTMAX_KEYS and not last:
                        max_part(bb + 1, 1 - par)
                    if L in SOFTMAX_KEYS:
                        outputs_out(bb)

                slots(act, slot)
                if L in SOFTMAX_KEYS:
                    outputs_back(7)

            rt_order = {L: i for i, L in enumerate([L for k, L in stages if k == "ffn" and L in (0, 3)])}

            def route_exp(L):
                act.wait_ge(s["rt_step"], 5 * rt_order[L] + 3)
                act.activation(route[1][:], route[0][:], ACT.Exp).then_inc(s["rt_exp"], 1)

            def ffn0(n):
                route_exp(0)

                act.wait_ge(s["thr_step"], 1)
                def copy(e):
                    act.wait_ge(s["f0_xt"], e + 1)
                    wait(act, s["f0_up"], FT0 * (e - 1))
                    act.activation(xgT0[e % 2][:], ps[5][:], ACT.Copy).then_inc(s["f0_xgT"], 1)

                copy(0)
                for e in range(E0):
                    for f in range(FT0):
                        rows = P if f < FT0 - 1 else FL0
                        act.wait_ge(s["f0_up"], FT0 * e + f + 1)
                        if f == 0:
                            wait(act, s["f0_down"], e - 1)
                        act.activation(mid0[e % 2][0:rows, f], ps[f % 3][0:rows, 0], ACT.Silu,
                                       bias=bu0[0:rows, e // 2, f:f + 1]).then_inc(s["f0_mid"], 1)
                    if e + 1 < E0:
                        copy(e + 1)

            def ffn2(n):
                act.wait_ge(s["f2_w"], 16 * 7)

                def chunk(ch):
                    for o in range(HT):
                        act.wait_ge(s["f2_up"], ch * HT + o + 1)
                        wait(act, s["f2_hA"], ch * HT + o - 1)
                        act.activation(sil[o % 2][:], ps[2 * (o % 2)][:].rearrange("p a b -> p (a b)"), ACT.Silu, scale=sc2[:, 0, o:o + 1])\
                            .then_inc(s["f2_sil"], 1)
                    for stage, dst in enumerate((hB, hA)):
                        for o in range(HT):
                            act.wait_ge(s["f2_mm"], (2 * ch + stage) * HT + o + 1)
                            if o == 0 and stage == 1:
                                act.wait_ge(s["f2_mm"], (2 * ch + 1) * HT)
                            act.activation(dst[:, o], ps[4 + o % 2][:].rearrange("p a b -> p (a b)"), ACT.Gelu,
                                           scale=sc2[:, 2 + stage, o:o + 1]).then_inc(s["f2_act"], 1)

                chunk(0)
                with act.Fori(1, NCH) as ch:
                    chunk(ch)

            def ffn3(n):
                route_exp(3)

                def hidden(t, k):
                    act.wait_ge(s["f3_up"], t + 1)
                    wait(act, s["f3_mT"], t - 1)
                    for half in range(2):
                        e = act.activation(mid3[k][:, half * CHUNK:(half + 1) * CHUNK], ps[half][:].rearrange("p a b -> p (a b)"), ACT.Gelu)
                    e.then_inc(s["f3_mid"], 1)

                for t in range(2):
                    hidden(t, t)
                with act.Fori(1, TILES3 // 2) as i:
                    for k in range(2):
                        hidden(2 * i + k, k)

            for n, (kind, L) in enumerate(stages):
                layernorm(n)
                if kind == "att":
                    attention(n, L)
                elif L != 1:
                    {0: ffn0, 2: ffn2, 3: ffn3}[L](n)

        @block.vector
        def _(dve):
            dve.sem_inc(s["x_res"], FREE)
            if ("att", 0) in stages:
                dve.wait_ge(s["mask_loaded"], 32)
                dve.tensor_scalar(mask_bf[:, 0], mask_u8[:, 0], NEG_MAX, None, ALU.mult)
                dve.tensor_scalar(mask_bf[:, 1], mask_u8[:, 1], NEG_EXP, None, ALU.mult).then_inc(s["mask_ready"], 1)

            def quantise(pair, j, e):
                q = 6 * pair
                cols = ds(2 * pair, 2)
                e.then_inc(s["f1_qstep"], 1)
                dve.wait_ge(s["f1_qstep"], q + 1)
                dve.tensor_reduce(lmax[:, cols], xn[j][:], AX.X, ALU.max, apply_absolute_value=True).then_inc(s["f1_qstep"], 1)
                dve.wait_ge(s["f1_qstep"], q + 2)
                dve.tensor_scalar(lscale[:, cols], lmax[:, cols], 1e-12, 1.0 / 127.0, ALU.max, ALU.mult).then_inc(s["f1_qstep"], 1)
                dve.wait_ge(s["f1_qstep"], q + 3)
                dve.reciprocal(linv[:, cols], lscale[:, cols]).then_inc(s["f1_qstep"], 1)
                dve.wait_ge(s["f1_qstep"], q + 4)
                for t in range(ST):
                    e = dve.tensor_scalar(xn[j][:, t], xn[j][:, t], linv[:, ds(2 * pair + t, 1)], -127.0, ALU.mult, ALU.max)
                e.then_inc(s["f1_qstep"], 1)
                dve.wait_ge(s["f1_qstep"], q + 5)
                dve.tensor_scalar(xn[j][:], xn[j][:], 127.0, MAGIC, ALU.min, ALU.add).then_inc(s["f1_qstep"], 1)
                dve.wait_ge(s["f1_qstep"], q + 6)
                dve.tensor_scalar(qn[j][:], xn[j][:], MAGIC, None, ALU.subtract).then_inc(s["xn_ready"], 1)

            def layernorm(n):
                ready_x(dve, n)
                with dve.Fori(0, NT) as t:
                    dve.bn_stats(ln_st[:, ds(t, 1)], X[:, ds(t, 1)]).then_inc(s["ln_stats"], 1)
                dve.wait_ge(s["ln_stats"], NT * (n + 1))
                me, mo = ln_st[:, :, 1], ln_st[:, :, 4]
                dve.tensor_tensor(ln_tmp[:, 0], me, mo, ALU.add)
                dve.tensor_tensor(ln_tmp[:, 1], me, mo, ALU.subtract)
                dve.tensor_tensor(ln_tmp[:, 2], ln_st[:, :, 2], ln_st[:, :, 5], ALU.add).then_inc(s["ln_mid"], 1)
                dve.wait_ge(s["ln_mid"], 4 * n + 1)
                dve.scalar_tensor_tensor(ln_tmp[:, 3], ln_tmp[:, 1], 0.25, ln_tmp[:, 1], ALU.mult, ALU.mult)
                dve.tensor_scalar(ln_tmp[:, 6], ln_tmp[:, 2], 1.0 / D, EPS, ALU.mult, ALU.add)
                dve.tensor_scalar(ln_tmp[:, 7], ln_tmp[:, 0], 0.5, None, ALU.mult).then_inc(s["ln_mid"], 1)
                dve.wait_ge(s["ln_mid"], 4 * n + 2)
                dve.tensor_tensor(ln_tmp[:, 4], ln_tmp[:, 3], ln_tmp[:, 6], ALU.add).then_inc(s["ln_mid"], 1)
                dve.wait_ge(s["ln_std"], n + 1)
                dve.reciprocal(ln_tmp[:, 5], ln_tmp[:, 5]).then_inc(s["ln_mid"], 1)
                dve.wait_ge(s["ln_mid"], 4 * n + 4)
                with dve.Fori(0, 4) as t:
                    for j in range(2):
                        pair = 2 * t + j
                        if stages[n] in GATHERED or n and stages[n - 1] in GATHERED:
                            sent = sum(st in GATHERED for st in stages[:n]) * NT // (2 * ST)
                            dve.wait_ge(xn_out[j], SENT0 + 16 * (sent + (t if stages[n] in GATHERED else 0)))
                        dve.wait_ge(s["xnt_psum"], 8 * n + pair + 1 - 2) if n > 0 else dve.wait_ge(s["xnt_done"], pair + 1)
                        for tt in range(ST):
                            i = 2 * pair + tt
                            e = dve.tensor_scalar(xn[j][:, tt], X[:, ds(i, 1)].squeeze(1), ln_tmp[:, 7, ds(i, 1)], ln_tmp[:, 5, ds(i, 1)],
                                                  ALU.subtract, ALU.mult)
                        if stages[n] == ("ffn", 1):
                            quantise(pair, j, e)
                        else:
                            e.then_inc(s["xn_ready"], 1)

            def attention(n, L):
                i = order["att", L]
                w_total = 16 * sum(8 + 2 * (l == 2) for l in n_att[:i + 1])
                dve.wait_ge(s["w_loaded"], w_total)
                dve.wait_ge(s["tg_ready"], 1)
                for par in range(2):
                    dve.memset(Qpack[par][MASK_ROW:MAX_ROW + 2], 1.0)
                    dve.memset(Kpack[par][MASK_ROW:MAX_ROW + 2], 1.0)
                    e = dve.memset(V[par][:, :, :, DH + (L == 0):VW], 0.0)
                    if L == 0:
                        e = dve.memset(V[par][:, :, :, DH:DH + 1], 1.0)
                e.then_inc(s["pack_const"], 1)
                if L == 0:
                    dve.memset(zrow[:], 0.0).then_inc(s["zero_row"], 1)
                if L == 1:
                    dve.wait_ge(s["ident_ready"], 2)
                    dve.tensor_scalar(nident_bf[:], ident[:], -1.0, None, ALU.mult)
                if L == 2:
                    dve.tensor_scalar(pad_bf[:], pad_u8[:], NEG_MAX, None, ALU.mult)
                    dve.tensor_scalar(keep[:], padT_u8[:], -1.0, 1.0, ALU.mult, ALU.add).then_inc(s["mask_ready"], 1)
                dve.tensor_scalar(bq4[:], bq[:], INV_SQRT, None, ALU.mult)
                dve.tensor_scalar(bog[:], bo[:], tg[:, L:L + 1], None, ALU.mult).then_inc(s["bias_ready"], 1)

                def remainders(b, par):
                    g = 8 * i + b
                    dve.wait_ge(s["q_evac"], g + 1)
                    dve.tensor_tensor(qr[:], qf[:], QP[:, 0], ALU.subtract).then_inc(s["q_r1"], 1)
                    dve.wait_ge(s["k_evac"], g + 1)
                    dve.tensor_tensor(kr[:], kf[:], KP[:, 0], ALU.subtract).then_inc(s["k_r1"], 1)
                    dve.wait_ge(s["v_psum"], g + 1)
                    if L == 0:
                        pv = P0[:].rearrange("p t (h d) -> p t h d", h=H)
                        for t in range(ST):
                            e = dve.tensor_copy(V[par][:, t, :, 0:DH], pv[:, t])
                        e.then_inc(s["v_copied"], 1)
                    else:
                        dve.tensor_tensor(Vb[par][:], P0[:], bv[:].unsqueeze(1).to_broadcast([P, ST, D]), ALU.add)\
                            .then_inc(s["v_copied"], 1)
                        if L != 3:
                            dve.wait_ge(s["v_copied"], g + 1)
                            if isinstance(b, int) and b == 0 and L == 2:
                                dve.wait_ge(s["mask_ready"], 1 + (("att", 0) in stages))
                            for t in range(ST):
                                vb = Vb[par][:, t].rearrange("p (h d) -> p h d", h=H)
                                if L == 2:
                                    dve.tensor_scalar(V[par][:, t, :, 0:DH], vb, keep[:, t, ds(b, 1)], None, ALU.mult)
                                    e = dve.tensor_copy(V[par][:, t, :, DH], keep[:, t, ds(b, 1)].to_broadcast([P, H]))
                                else:
                                    e = dve.tensor_copy(V[par][:, t, :, 0:DH], vb)
                            e.then_inc(s["v_ready"], 1)
                    dve.wait_ge(s["q_mid"], g + 1)
                    dve.tensor_tensor(QP[:, 2], qr[:], QP[:, 1], ALU.subtract).then_inc(s["q_split"], 1)
                    dve.wait_ge(s["k_mid"], g + 1)
                    dve.tensor_tensor(KP[:, 2], kr[:], KP[:, 1], ALU.subtract).then_inc(s["k_split"], 1)

                def row_max(b, h):
                    m = 8 * m_order[L] + b
                    dve.wait_ge(s["smax_ps"], 16 * m + h + 1)
                    dve.tensor_reduce(mx[:, :, h], A[2 + h % 2][:], AX.X, ALU.max).then_inc(s["smax_done"], 1)

                def max_rest(b):
                    m = 8 * m_order[L] + b
                    dve.wait_ge(s["m_hi"], m + 1)
                    dve.scalar_tensor_tensor(MR[:, 1], P0[0:H, 0], -1.0, MR[:, 0], ALU.mult, ALU.subtract).then_inc(s["m_lo"], 1)

                def col_max(b, h):
                    dve.wait_ge(s["st_ps"], 16 * (8 * s_order[L] + b) + h + 1)
                    dve.tensor_reduce(nmax[:, :, h], A[h % 4][:], AX.X, ALU.max, negate=True).then_inc(s["nmax_ready"], 1)

                def scale_values(b, par, c):
                    dve.wait_ge(s["exp_done"], 16 * (8 * s_order[L] + b) + GROUP * (c + 1))
                    hh = slice(GROUP * c, GROUP * (c + 1))
                    dve.reciprocal(rsum[:, :, hh], esum[:, :, hh]).then_inc(s["rsum_ready"], 1)
                    dve.wait_ge(s["rsum_ready"], CH * b + c + 1)
                    for t in range(ST):
                        vb = Vb[par][:, t].rearrange("p (h d) -> p h d", h=H)
                        e = dve.tensor_tensor(V[par][:, t, hh, 0:DH], vb[:, hh], rsum[:, t, hh].unsqueeze(2).to_broadcast([P, GROUP, DH]), ALU.mult)
                    e.then_inc(s["vs_ready"], 1)

                def normalise(b):
                    g = 8 * i + b
                    if L == 1:
                        dve.wait_ge(s["av1_done"], 16 * (b + 1))
                    else:
                        dve.wait_ge(s["av_done"], 16 * (8 * s_order[L] + b + 1))
                    dve.wait_ge(s["y_ps"], FREE + g)
                    for c in range(2):
                        e = dve.tensor_copy(On[:, 2 * c:2 * c + 2], O[c][:])
                    e.then_inc(s["on_ready"], 1)

                def divide(b):
                    m = 8 * m_order[L] + b
                    dve.wait_ge(s["oT_ps"], m + 1)
                    view = [O[t][:].rearrange("p a b -> p (a b)").rearrange("p (h w) -> p h w", w=VW) for t in range(ST)]
                    for t in range(ST):
                        e = dve.reciprocal(rden[:, t], view[t][:, :, DH])
                    e.then_inc(s["on_rden"], 1)
                    dve.wait_ge(s["on_rden"], m + 1)
                    for t in range(ST):
                        e = dve.tensor_tensor(Oq[:, t].rearrange("p (h d) -> p h d", h=H), view[t][:, :, 0:DH],
                                              rden[:, t].unsqueeze(2).to_broadcast([P, H, DH]), ALU.mult)
                    e.then_inc(s["on_norm"], 1)

                def residual(b):
                    g = 8 * i + b
                    dve.wait_ge(s["y_ps"], FREE + g + 1)
                    xt = X[:, ds(ST * b, ST)]
                    dve.scalar_tensor_tensor(xt, P1[:], tg[:, L:L + 1], xt, ALU.mult, ALU.add).then_inc(s["x_res"], 1)

                def maxima1(b):
                    for t in range(ST):
                        for e in range(H // 2):
                            k = 16 * b + 8 * t + e
                            dve.wait_ge(s["p1_ps"], k + 1)
                            bank = A[(8 * t + e) % 4]
                            if e == 0:
                                dve.tensor_copy(M2[:, t], bank[:]).then_inc(s["p1_max"], 1)
                            else:
                                dve.wait_ge(s["p1_max"], k)
                                dve.tensor_tensor(M2[:, t], bank[:], M2[:, t], ALU.max).then_inc(s["p1_max"], 1)
                        dve.wait_ge(s["p1_max"], 16 * b + 8 * (t + 1))
                        dve.tensor_tensor(M1[:, t], M2[:, t, 0], M2[:, t, 1], ALU.max).then_inc(s["m1_step"], 1)
                        dve.wait_ge(s["m1_step"], 4 * b + 2 * t + 1)
                        dve.tensor_copy(m1p[:, t, 0], M1[:, t]).then_inc(s["m1_step"], 1)
                        dve.wait_ge(s["m1_step"], 4 * b + 2 * t + 2)
                        dve.tensor_tensor(m1p[:, t, 1], M1[:, t], m1p[:, t, 0], ALU.subtract).then_inc(s["m1_ready"], 1)

                def sums1(b):
                    for t in range(ST):
                        dve.wait_ge(s["exp1_done"], 16 * b + 8 * (t + 1))
                        n_steps = 0
                        src, width = probs[:, t], H // 2
                        while width:
                            base = 10 * b + 5 * t
                            if n_steps:
                                dve.wait_ge(s["sum1_step"], base + n_steps)
                            dve.tensor_tensor(hs[:, t, 0:width], src[:, 0:width], src[:, width:2 * width], ALU.add)\
                                .then_inc(s["sum1_step"], 1)
                            src, width, n_steps = hs[:, t], width // 2, n_steps + 1
                        dve.wait_ge(s["sum1_step"], 10 * b + 5 * t + 4)
                        dve.reciprocal(hs[:, t, 0], hs[:, t, 0]).then_inc(s["sum1_step"], 1)
                        dve.wait_ge(s["sum1_step"], 10 * b + 5 * t + 5)
                        dve.tensor_tensor(probs[:, t], probs[:, t], hs[:, t, 0].unsqueeze(1).to_broadcast([P, H, S]), ALU.mult)\
                            .then_inc(s["norm1"], 1)

                dve.wait_ge(s["pack_const"], i + 1)
                remainders(0, 0)
                if L in SOFTMAX_KEYS:
                    for h in range(H):
                        row_max(0, h)
                    max_rest(0)
                if L != 0:
                    dve.wait_ge(s["bias_added"], sum(l != 0 for l in n_att[:i + 1]))

                def slot(b, par):
                    bb = bval(b)
                    first = isinstance(b, int) and b == 0
                    last = isinstance(b, int) and b == 7
                    if not first:
                        divide(bb - 1) if L in SOFTMAX_KEYS else normalise(bb - 1)
                    if not last:
                        remainders(bb + 1, 1 - par)
                    if not first:
                        residual(bb - 1)
                    if L == 1:
                        maxima1(bb)
                        sums1(bb)
                    elif L == 3:
                        for h in range(H):
                            col_max(bb, h)
                            if h % GROUP == GROUP - 1 and h >= GROUP:
                                scale_values(bb, par, h // GROUP - 1)
                        scale_values(bb, par, CH - 1)
                    elif not last:
                        for h in range(H):
                            row_max(bb + 1, h)
                        max_rest(bb + 1)

                slots(dve, slot)
                divide(7) if L in SOFTMAX_KEYS else normalise(7)
                residual(7)

            rt_order = {L: i for i, L in enumerate([L for k, L in stages if k == "ffn" and L in (0, 3)])}
            def bc_row(x):
                return x.unsqueeze(2).to_broadcast([P, NT, E0])

            def bc_exp(x):
                return x.unsqueeze(1).to_broadcast([P, NT, E0])

            def link(k, r, e):
                e.then_inc(s["rt_step"], 1)
                dve.wait_ge(s["rt_step"], k)

            def softmax_rows(L):
                r = rt_order[L]
                dve.wait_ge(s["rt_const"], 5)
                dve.wait_ge(s["rt_logits"], r + 1)
                logits = ps[0][:].rearrange("p a b -> p (a b)")[:, 0:NT * E0].rearrange("p (t e) -> p t e", e=E0)
                if L == 0:
                    dve.wait_ge(s["f0_router"], 48)
                    link(5 * r + 1, r, dve.tensor_tensor(route[2][:], logits, bc_exp(br0[:]), ALU.add))
                else:
                    link(5 * r + 1, r, dve.tensor_copy(route[2][:], logits))
                link(5 * r + 2, r, dve.tensor_reduce(row_m[:, 0], route[2][:], AX.X, ALU.max))
                dve.tensor_tensor(route[0][:], route[2][:], bc_row(row_m[:, 0]), ALU.subtract).then_inc(s["rt_step"], 1)
                dve.wait_ge(s["rt_exp"], r + 1)
                link(5 * r + 4, r, dve.tensor_reduce(row_m[:, 1], route[1][:], AX.X, ALU.add))
                link(5 * r + 5, r, dve.reciprocal(row_m[:, 2], row_m[:, 1]))

            def running_counts(nk, chain, c0, r):
                dve.wait_ge(s["rt_prefix"], r + 1)
                bank = ps[2]
                tot = bank[:, 1, 0:NT * nk].rearrange("p (t k) -> p t k", k=nk)
                chain(c0 + 1, dve.tensor_copy(totals[:, :, 0:nk], tot))
                for k in range(nk):
                    e = dve.tensor_tensor_scan(sums[:, :, k], ones_f[:], totals[:, :, k], 0.0, ALU.mult, ALU.add)
                chain(c0 + 2, e)
                chain(c0 + 3, dve.tensor_tensor(totals[:, :, 0:nk], sums[:, :, 0:nk], totals[:, :, 0:nk], ALU.subtract))
                chain(c0 + 4, dve.tensor_tensor(totals[:, :, 0:nk], totals[:, :, 0:nk],
                                                bank[:, 0, 0:NT * nk].rearrange("p (t k) -> p t k", k=nk), ALU.add))

            def route0(n):
                r = rt_order[0]
                softmax_rows(0)
                cmp = flags[:].rearrange("p t k e -> p (t k) e")[:, 0:NT]

                def chain(k, e):
                    e.then_inc(s["thr_step"], 1)
                    dve.wait_ge(s["thr_step"], k)

                dve.memset(mid0[0][32:64, FT0 - 1], 1.0)
                dve.memset(mid0[1][32:64, FT0 - 1], 1.0)
                dve.memset(thr[:], 0)
                dve.memset(step_f[:], 2.0 ** 29)
                dve.memset(step_i[:], 1 << 29)
                chain(1, dve.tensor_tensor(probs_e[:], route[1][:], bc_row(row_m[:, 2]), ALU.mult))
                with dve.Fori(0, 30) as i:
                    k = 1 + 5 * i
                    chain(k + 1, dve.tensor_tensor(cand[:], thr[:], step_i[:], ALU.bitwise_or))
                    dve.tensor_tensor(cmp, probs_e[:], bc_exp(cand[:].bitcast(F32)), ALU.is_ge).then_inc(s["thr_cmp"], 1)
                    dve.wait_ge(s["thr_cnt"], i + 1)
                    chain(k + 2, dve.tensor_reduce(cnt[:], ps[1][:, 0, 0:NT * E0].rearrange("p (t e) -> p e t", e=E0), AX.X, ALU.add))
                    chain(k + 3, dve.scalar_tensor_tensor(taken[:], cnt[:], TOP0 - 0.5, step_f[:], ALU.is_ge, ALU.mult))
                    dve.tensor_tensor(thr[:], thr[:], taken[:], ALU.bitwise_or)
                    chain(k + 4, dve.tensor_scalar(step_f[:], step_f[:], 0.5, None, ALU.mult))
                    chain(k + 5, dve.tensor_copy(step_i[:], step_f[:]))
                k = 1 + 5 * 30
                dve.tensor_tensor(flags[:, :, 0], probs_e[:], bc_exp(thr[:].bitcast(F32)), ALU.is_gt)
                dve.tensor_tensor(flags[:, :, 1], probs_e[:], bc_exp(thr[:].bitcast(F32)), ALU.is_equal).then_inc(s["thr_cmp"], 1)
                running_counts(2 * E0, chain, k, r)
                k += 4
                chain(k + 1, dve.tensor_scalar(need[:], sums[:, NT - 1, 0:E0], -1.0, float(TOP0), ALU.mult, ALU.add))
                chain(k + 2, dve.tensor_tensor(route[0][:], totals[:, :, E0:2 * E0], bc_exp(need[:]), ALU.is_le))
                chain(k + 3, dve.tensor_tensor(route[2][:], route[0][:], flags[:, :, 1], ALU.mult))
                chain(k + 4, dve.tensor_tensor(route[0][:], route[2][:], flags[:, :, 0], ALU.add))
                chain(k + 5, dve.scalar_tensor_tensor(coef[:], route[0][:], tg[:, 4:5], probs_e[:], ALU.mult, ALU.mult))
                chain(k + 6, dve.tensor_tensor(route[1][:], totals[:, :, E0:2 * E0], bc_exp(need[:]), ALU.min))
                chain(k + 7, dve.tensor_tensor(route[2][:], route[1][:], totals[:, :, 0:E0], ALU.add))
                chain(k + 8, dve.tensor_tensor(route[1][:], route[2][:], route[0][:], ALU.mult))
                chain(k + 9, dve.tensor_scalar(pos_i[:], route[1][:], 1.0, None, ALU.subtract))

            def parts(x, part, rest, step):
                step(dve.tensor_copy(part[0][:], x))
                step(dve.tensor_tensor(rest[0][:], x, part[0][:], ALU.subtract))
                step(dve.tensor_copy(part[1][:], rest[0][:]))
                step(dve.tensor_tensor(part[2][:], rest[0][:], part[1][:], ALU.subtract))

            def ffn0(n):
                dve.wait_ge(s["tg_ready"], 1)
                route0(n)
                steps = [0]

                def step(e):
                    steps[0] += 1
                    e.then_inc(s["f0_step"], 1)
                    dve.wait_ge(s["f0_step"], steps[0])

                dve.tensor_scalar(place_i[:], pos_i[:], P - 1, None, ALU.bitwise_and)
                step(dve.tensor_scalar(half_i[:], pos_i[:], P.bit_length() - 1, None, ALU.arith_shift_right))
                dve.tensor_copy(place0[:], place_i[:])
                step(dve.tensor_copy(route[3][:], half_i[:]))
                for h in range(SL0):
                    e = dve.tensor_scalar(in_half[:, :, :, h], route[3][:], float(h), None, ALU.is_equal)
                step(e)
                parts(coef[:], gpart, grest, step)
                per = in_half[:].rearrange("p t e h -> p e t h")
                wide = [P, E0, NT, SL0]
                dve.tensor_tensor(lists0[:, :, :, 0], per, col[:, 0:NT].unsqueeze(1).unsqueeze(3).to_broadcast(wide), ALU.mult)
                dve.tensor_scalar(lists0[:, :, :, 1], per, row[:], None, ALU.mult)
                for v in range(3):
                    e = dve.tensor_tensor(lists0[:, :, :, 2 + v], per, gpart[v][:].rearrange("p t e -> p e t").unsqueeze(3).to_broadcast(wide), ALU.mult)
                step(e)

                def hot(e):
                    dve.tensor_tensor(hot0[e % 2][:], place0[:, :, e].unsqueeze(2).to_broadcast([P, NT, P]),
                                      col[:].unsqueeze(1).to_broadcast([P, NT, P]), ALU.is_equal).then_inc(s["f0_hot"], 1)

                def index(e):
                    dve.wait_ge(s["f0_list"], e + 1)
                    got = ps[3 + e % 2][:, 0, 0:5 * SL0].rearrange("p (v h) -> p v h", v=5)
                    dve.tensor_copy(idl0[:, e], got[:, 1])
                    dve.tensor_copy(gsum0[:, e], got[:, 3]).then_inc(s["f0_idstep"], 1)
                    dve.wait_ge(s["f0_idstep"], 3 * e + 1)
                    dve.scalar_tensor_tensor(idx0[:, e], got[:, 0], float(P), idl0[:, e], ALU.mult, ALU.add)
                    dve.tensor_tensor(gate0[:, e], got[:, 2], gsum0[:, e], ALU.add).then_inc(s["f0_idstep"], 1)
                    dve.wait_ge(s["f0_idstep"], 3 * e + 2)
                    dve.tensor_tensor(gate0[:, e], gate0[:, e], got[:, 4], ALU.add).then_inc(s["f0_idstep"], 1)
                    dve.wait_ge(s["f0_idstep"], 3 * e + 3)
                    dve.sem_inc(s["f0_idx"], 1)

                def weigh(e):
                    dve.wait_ge(s["f0_down"], e + 1)
                    wait(dve, s["f0_scatter"], 16 * SL0 * (e - 1))
                    for h in range(SL0):
                        y = dve.tensor_scalar(yg0[e % 2][:, h], ps[6 + e % 2][:, h], gate0[:, e, h:h + 1], None, ALU.mult)
                    y.then_inc(s["f0_yg"], 1)

                hot(0)
                hot(1)
                for e in range(E0):
                    index(e)
                    if e + 2 < E0:
                        hot(e + 2)
                    if e >= 3:
                        weigh(e - 3)
                for e in range(E0 - 3, E0):
                    weigh(e)
                dve.wait_ge(s["x_back"], 16)
                dve.sem_inc(s["x_ffn"], 1)

            def ffn1_rhs():
                dve.wait_ge(s["f1_rhs"], 16)
                dve.tensor_reduce(rmax[:], rhs1[:].rearrange("p c n -> p n c"), AX.X, ALU.max, apply_absolute_value=True).then_inc(s["f1_rmax"], 1)
                dve.wait_ge(s["f1_rall"], 1)

                def chain(k, e):
                    e.then_inc(s["f1_rstep"], 1)
                    dve.wait_ge(s["f1_rstep"], k)

                chain(1, dve.tensor_scalar(rscale[:], rall[:], 1e-12, 1.0 / 127.0, ALU.max, ALU.mult))
                chain(2, dve.reciprocal(rinv[:], rscale[:]))
                chain(3, dve.tensor_tensor(rtmp[:], rhs1[:], rinv[:].unsqueeze(1).to_broadcast([P, KC, D]), ALU.mult))
                chain(4, dve.tensor_scalar(rtmp[:], rtmp[:], -127.0, 127.0, ALU.max, ALU.min))
                chain(5, dve.tensor_scalar(rtmp[:], rtmp[:], MAGIC, None, ALU.add))
                dve.tensor_scalar(qrhs[:], rtmp[:], MAGIC, None, ALU.subtract).then_inc(s["f1_qrhs"], 1)

            def ffn1(n):
                dve.wait_ge(s["tg_ready"], 1)

                def pair(b, j):
                    dve.wait_ge(s["f1_ps"], b + 1)
                    for t in range(ST):
                        e = dve.scalar_tensor_tensor(y1[j][:, t], ps[2 + j][:, t], lscale[:, ds(ST * b + t, 1)], rscale[:], ALU.mult, ALU.mult)
                    e.then_inc(s["f1_y"], 1)
                    dve.wait_ge(s["f1_y"], b + 1)
                    xt = X[:, ds(ST * b, ST)]
                    dve.scalar_tensor_tensor(xt, y1[j][:], tg[:, 5:6], xt, ALU.mult, ALU.add).then_inc(s["f1_acc"], 1)

                with dve.Fori(0, B // 2) as i:
                    for j in range(2):
                        pair(2 * i + j, j)
                dve.wait_ge(s["f1_acc"], B)
                dve.sem_inc(s["x_ffn"], 1)

            def ffn2(n):
                dve.wait_ge(s["tg_ready"], 1)
                dve.wait_ge(s["f2_w"], 16 * 7)

                def chunk(ch):
                    for o in range(HT):
                        dve.wait_ge(s["f2_sil"], ch * HT + o + 1)
                        if o == 0:
                            wait(dve, s["f2_yps"], ch * TPC)
                        dve.scalar_tensor_tensor(hA[:, o], ps[2 * (o % 2) + 1][:].rearrange("p a b -> p (a b)"), sc2[:, 1, o:o + 1], sil[o % 2][:],
                                                 ALU.mult, ALU.mult).then_inc(s["f2_hA"], 1)
                    for t in range(TPC):
                        k = ch * TPC + t
                        dve.wait_ge(s["f2_yps"], k + 1)
                        dve.tensor_tensor(y2[t % 2][:], ps[6 + t % 2][:, 0], s3_2[:], ALU.mult).then_inc(s["f2_y"], 1)
                        dve.wait_ge(s["f2_y"], k + 1)
                        xt = X[:, ds(k, 1)].squeeze(1)
                        dve.scalar_tensor_tensor(xt, y2[t % 2][:], tg[:, 6:7], xt, ALU.mult, ALU.add).then_inc(s["f2_acc"], 1)

                chunk(0)
                with dve.Fori(1, NCH) as ch:
                    chunk(ch)
                dve.wait_ge(s["f2_acc"], NT)
                dve.sem_inc(s["x_ffn"], 1)

            def route3(n):
                r = rt_order[3]
                softmax_rows(3)
                k = [5 * (r + 1)]

                def chain(e):
                    k[0] += 1
                    e.then_inc(s["rt_step"], 1)
                    dve.wait_ge(s["rt_step"], k[0])

                chain(dve.tensor_tensor(probs_e[:], route[1][:], bc_row(row_m[:, 2]), ALU.mult))
                left = probs_e
                for j in range(2):
                    chain(dve.tensor_reduce(row_m[:, 3 + j], left[:], AX.X, ALU.max))
                    chain(dve.tensor_tensor(route[2][:], left[:], bc_row(row_m[:, 3 + j]), ALU.is_equal))
                    chain(dve.tensor_tensor(route[3][:], route[2][:], bc_exp(rev[:]), ALU.mult))
                    chain(dve.tensor_reduce(row_m[:, 0], route[3][:], AX.X, ALU.max))
                    chain(dve.tensor_tensor(flags[:, :, j], route[3][:], bc_row(row_m[:, 0]), ALU.is_equal))
                    if j == 0:
                        chain(dve.scalar_tensor_tensor(route[4][:], flags[:, :, 0], -2.0, probs_e[:], ALU.mult, ALU.add))
                        left = route[4]
                dve.sem_inc(s["rt_cnt"], 1)
                chain(dve.tensor_tensor(row_m[:, 5], row_m[:, 3], row_m[:, 4], ALU.add))
                chain(dve.reciprocal(row_m[:, 5], row_m[:, 5]))
                chain(dve.tensor_scalar(row_m[:, 5], row_m[:, 5], tg[:, 7:8], None, ALU.mult))
                for j in range(2):
                    e = dve.tensor_tensor(row_m[:, j], row_m[:, 3 + j], row_m[:, 5], ALU.mult)
                chain(e)
                running_counts(2 * E3, lambda _, e: chain(e), 0, r)
                for j in range(PAIRS3):
                    of = slice(j * E3, (j + 1) * E3)
                    dve.scalar_tensor_tensor(kept[j][:], totals[:, :, of], CAP3 + 0.5, flags[:, :, j], ALU.is_le, ALU.mult)
                    e = dve.tensor_scalar(count3[:, j], sums[:, NT - 1, of], float(CAP3), None, ALU.min)
                chain(e)
                chain(dve.scalar_tensor_tensor(load3_i[:], count3[:, 0], float(P - 1), count3[:, 1], ALU.add, ALU.add))
                chain(dve.tensor_scalar(load3_i[:], load3_i[:], P.bit_length() - 1, None, ALU.arith_shift_right))
                chain(dve.tensor_copy(tiles3[:], load3_i[:]))
                chain(dve.tensor_tensor_scan(upto3[:], ones_f[:, 0:E3], tiles3[:], 0.0, ALU.mult, ALU.add))
                chain(dve.tensor_tensor(load3[:], upto3[:], tiles3[:], ALU.subtract))
                chain(dve.tensor_scalar(start3[:, 0], load3[:], float(P), None, ALU.mult))
                chain(dve.tensor_tensor(start3[:, 1], start3[:, 0], count3[:, 0], ALU.add))
                for j in range(PAIRS3):
                    chain(dve.tensor_tensor(route[j][:], totals[:, :, j * E3:(j + 1) * E3], bc_exp(start3[:, j]), ALU.add))
                    chain(dve.tensor_tensor(route[2 + j][:], route[j][:], kept[j][:], ALU.mult))
                    chain(dve.tensor_reduce(slot3[:, j], route[2 + j][:], AX.X, ALU.add))
                chain(dve.tensor_scalar(slot3_i[:], slot3[:], 1.0, None, ALU.subtract))
                dve.tensor_scalar(place3_i[:], slot3_i[:], P - 1, None, ALU.bitwise_and)
                chain(dve.tensor_scalar(tile3_i[:], slot3_i[:], P.bit_length() - 1, None, ALU.arith_shift_right))
                dve.tensor_copy(place3[:], place3_i[:])
                chain(dve.tensor_copy(tile3[:], tile3_i[:]))
                parts(row_m[:, 0:PAIRS3], part3, rest3, chain)
                per = lists3[:, :, :, 0]
                wide = [P, PAIRS3, NT, TILES3]
                chain(dve.tensor_tensor(per, tile3[:].unsqueeze(3).to_broadcast(wide),
                                        col[:, 0:TILES3].unsqueeze(1).unsqueeze(1).to_broadcast(wide), ALU.is_equal))
                dve.tensor_tensor(hot3[:].rearrange("p j t c -> p (j t) c"), place3[:].rearrange("p j t -> p (j t)").unsqueeze(2).to_broadcast([P, PAIRS3 * NT, P]),
                                  col[:].unsqueeze(1).to_broadcast([P, PAIRS3 * NT, P]), ALU.is_equal)
                dve.tensor_tensor(lists3[:, :, :, 1], per, col[:, 0:NT].unsqueeze(1).unsqueeze(3).to_broadcast(wide), ALU.mult)
                dve.tensor_scalar(lists3[:, :, :, 2], per, row[:], None, ALU.mult)
                for v in range(3):
                    e = dve.tensor_tensor(lists3[:, :, :, 3 + v], per, part3[v][:].unsqueeze(3).to_broadcast(wide), ALU.mult)
                e.then_inc(s["f3_hot"], 1)
                wide = [P, TILES3, E3]
                chain(dve.tensor_tensor(before3[:], col[:, 0:TILES3].unsqueeze(2).to_broadcast(wide),
                                        upto3[:].unsqueeze(1).to_broadcast(wide), ALU.is_ge))
                chain(dve.tensor_reduce(expert3[:], before3[:], AX.X, ALU.add))
                chain(dve.tensor_scalar(expert3_i[:], expert3[:], E3 - 1.0, None, ALU.min))
                dve.wait_ge(s["f3_list"], 1)
                got = ps[3][:].rearrange("p a b -> p (a b)")[:, 0:6 * TILES3].rearrange("p (v i) -> p v i", v=6)
                dve.tensor_scalar(idl3[0][:], got[:, 0], spare[:, 1:2], spare[:, 0:1], ALU.mult, ALU.add)
                chain(dve.tensor_copy(gate3[1][:], got[:, 4]))
                dve.tensor_tensor(gate3[0][:], got[:, 3], gate3[1][:], ALU.add)
                chain(dve.scalar_tensor_tensor(idl3[1][:], got[:, 1], float(P), idl3[0][:], ALU.mult, ALU.add))
                dve.tensor_tensor(idx3[:], idl3[1][:], got[:, 2], ALU.add)
                chain(dve.tensor_tensor(gate3[1][:], gate3[0][:], got[:, 5], ALU.add))
                dve.sem_inc(s["f3_idx"], 1)

            def ffn3(n):
                dve.wait_ge(s["tg_ready"], 1)
                route3(n)

                def copy(t, k):
                    dve.wait_ge(s["f3_xt"], t + 1)
                    wait(dve, s["f3_up"], t - 1)
                    dve.tensor_copy(xgT3[k % 2][:], ps[3 + k % 2][:, 0].rearrange("p (c t) -> p c t", c=KC)).then_inc(s["f3_xgT"], 1)

                def copy_mid(t, k):
                    dve.wait_ge(s["f3_mT"], t + 1)
                    wait(dve, s["f3_down"], t - 1)
                    for half in range(2):
                        e = dve.tensor_copy(midT3[k % 2][:, 4 * half:4 * half + 4], ps[2 + 4 * half][:].rearrange("p a (c t) -> p (a c) t", t=P))
                    e.then_inc(s["f3_midT"], 1)

                def weigh(t, k, tv):
                    dve.wait_ge(s["f3_down"], t + 1)
                    wait(dve, s["f3_scatter"], 16 * (t - 1))
                    dve.tensor_scalar(yg3[k % 2][:], ps[5 + 2 * (k % 2)][:, 0], gate3[1][:, ds(tv, 1)], None, ALU.mult).then_inc(s["f3_yg"], 1)

                def pair(t0):
                    for k in range(2):
                        t = t0 + k
                        known = isinstance(t, int)
                        if not known or t + 2 < TILES3:
                            copy(t + 2, k)
                        copy_mid(t, k)
                        if not known or t > 0:
                            weigh(t - 1, k + 1, t - 1)

                copy(0, 0)
                copy(1, 1)
                pair(0)
                pair(2)
                with dve.Fori(2, TILES3 // 2 - 1) as i:
                    pair(2 * i)
                pair(TILES3 - 2)
                weigh(TILES3 - 1, 1, TILES3 - 1)

            for n, (kind, L) in enumerate(stages):
                if (kind, L) == ("ffn", 1):
                    ffn1_rhs()
                layernorm(n)
                if kind == "att":
                    attention(n, L)
                else:
                    (ffn0, ffn1, ffn2, ffn3)[L](n)


def layout(v):
    n = {k: np.asarray(x) for k, x in v.items()}
    o = {"x": n["x"].reshape(T, D), "g_xattn": n["g_xattn"], "g_ffn": n["g_ffn"]}

    def rows(w):
        c, m = w.shape
        return w.reshape(c // P, P, m).transpose(1, 0, 2)

    o["ctxT"] = rows(n["ctx_1024"].reshape(T, D).T)
    mask = n["mask_1x1xSxS2_bk1"].reshape(S, S)
    o["mask_qk"], o["mask_kq"] = rows(mask), rows(mask.T)
    pad = n["mask_BxS2_bf0"]
    o["pad"], o["padT"] = pad, rows(pad.T)
    def heads(w):
        lead = w.shape[:-1]
        k = len(lead)
        w = w.reshape(lead + (HPH, HALF, DH))
        return w.transpose(tuple(range(k)) + (k + 1, k + 2, k)).reshape(lead + (D,))

    def padded(w):
        z = np.zeros((H, VW, D), w.dtype)
        z[:, :DH] = w.reshape(H, DH, D)
        return rows(z.reshape(H * VW, D))

    zeros = np.zeros(D, n["x"].dtype)
    kv = n["L3_xattn_Wkv"]
    ws = [
        (n["L0_xattn_Wq"].T, n["L0_xattn_Wk"].T, n["L0_xattn_Wv"].T, n["L0_xattn_Wo"].T, zeros, zeros, zeros, zeros),
        (n["L1_xattn_Wq_w"].T, n["L1_xattn_Wk_w"].T, n["L1_xattn_Wv_w"].T, n["L1_xattn_Wo_w"].T,
         n["L1_xattn_Wq_b"], n["L1_xattn_Wk_b"], n["L1_xattn_Wv_b"], n["L1_xattn_Wo_b"]),
        (n["L2_xattn_wq"].T, n["L2_xattn_wk"].T, n["L2_xattn_wv"].T, n["L2_xattn_wo"].T,
         n["L2_xattn_bq"], n["L2_xattn_bk"], n["L2_xattn_bv"], n["L2_xattn_bo"]),
        (n["L3_xattn_Wq"], kv[:, :D], kv[:, D:], n["L3_xattn_Wo"], n["L3_xattn_bq"],
         n["L3_xattn_bkv"][:D], n["L3_xattn_bkv"][D:], n["L3_xattn_bo"]),
    ]
    for L, (q, k, w, wo_, bq_, bk_, bv_, bo_) in enumerate(ws):
        o[f"wq{L}"], o[f"wk{L}"], o[f"wv{L}"] = rows(heads(q)), rows(heads(k)), rows(w)
        o[f"wo{L}"] = rows(wo_) if L in SOFTMAX_KEYS else padded(wo_)
        o[f"bq{L}"], o[f"bk{L}"] = heads(bq_).reshape(HALF, P).T, heads(bk_).reshape(HALF, P).T
        o[f"bv{L}"], o[f"bo{L}"] = bv_, bo_
    o["wr0"], o["br0"] = rows(n["L0_ffn_Wr"]), n["L0_ffn_br"]
    z = np.zeros((NG0, D, FT0 * P), n["x"].dtype)
    z[:, :, :F0] = n["L0_ffn_W_up"]
    o["wu0"] = z.reshape(NG0, KC, P, FT0 * P).transpose(2, 0, 1, 3)
    z = np.zeros((NG0, FT0 * P), n["x"].dtype)
    z[:, :F0] = n["L0_ffn_b_up"]
    o["bu0"] = z.reshape(NG0, FT0, P).transpose(2, 0, 1)
    z = np.zeros((E0, FT0 * P, D), n["x"].dtype)
    z[:, :F0], z[:, F0] = n["L0_ffn_W_down"], n["L0_ffn_b_down"]
    o["wd0"] = z.reshape(E0, FT0, P, D).transpose(2, 0, 1, 3)
    o["rhs1"] = rows(n["L1_ffn_rhs"])
    for name, key in (("w1_2", "w1"), ("w2_2", "w2"), ("h1_2", "h1"), ("h2_2", "h2"), ("w3_2", "w3")):
        o[name] = rows(n[f"L2_ffn_{key}_w"].T)
    o["sc2"] = np.stack([n[f"L2_ffn_{key}_s"].reshape(HT, P).T for key in ("w1", "w2", "h1", "h2")], 1)
    o["s3_2"] = n["L2_ffn_w3_s"]
    o["wr3"] = rows(n["L3_ffn_router_w"].T)
    o["w1_3"] = n["L3_ffn_w1"].reshape(E3, KC, P, HID).transpose(0, 2, 1, 3)
    o["w2_3"] = n["L3_ffn_w2"].reshape(E3, HT, P, D).transpose(0, 2, 1, 3)
    return {k: np.ascontiguousarray(x) for k, x in o.items()}


STAGES = [("att", 0), ("ffn", 0), ("att", 1), ("ffn", 1), ("att", 2), ("ffn", 2), ("att", 3), ("ffn", 3)]


def kernel(**inputs):
    import concourse.bacc as bacc
    from concourse.bass_utils import run_bass_kernel_spmd

    nc = bacc.Bacc("TRN2", target_bir_lowering=False, num_devices=1)
    arrays = {f"in_{k}": x for k, x in layout(inputs).items()}
    args = {k[3:]: nc.dram_tensor(k, x.shape, mybir.dt.from_np(x.dtype), kind="ExternalInput").ap() for k, x in arrays.items()}
    out = nc.dram_tensor("out", (T, D), F32, kind="ExternalOutput").ap()
    program(nc, args, out, STAGES)
    r = run_bass_kernel_spmd(nc, [arrays], core_ids=[0])
    return r.results[0]["out"].reshape(B, S, D)
```

```python
from contextlib import ExitStack

import numpy as np

import concourse.bass as bass
from concourse import mybir

F32 = mybir.dt.float32
BF16 = mybir.dt.bfloat16
I32 = mybir.dt.int32
U8 = mybir.dt.uint8
U16 = mybir.dt.uint16
ALU = mybir.AluOpType
ACT = mybir.ActivationFunctionType
AX = mybir.AxisListType
ds = bass.ds

P = 128
D = 256
KC = D // P
B, S = 8, 256
T = B * S
NT = T // P
ST = S // P
H, DH = 16, 16
HALF = 2
HPH = H // HALF
GROUP = 4
CH = H // GROUP
VW = P // GROUP
EPS = 1e-5
Q_PARTS = (0, 0, 1, 1, 0, 2)
K_PARTS = (0, 1, 0, 1, 2, 0)
ROWS = DH * len(Q_PARTS)
MASK_ROW, MAX_ROW = ROWS, ROWS + 1
NEG_MAX = -1e30
NEG_EXP = -3e38
INV_SQRT = 1.0 / DH ** 0.5
SOFTMAX_KEYS = (0, 2)
E0, NG0, F0 = 8, 4, 682
FT0 = -(-F0 // P)
FL0 = F0 - (FT0 - 1) * P
TOP0 = T // E0
SL0 = TOP0 // P
DIGIT_BITS, DIGITS, UNROLL0 = 2, 15, 3
DIGIT = (1 << DIGIT_BITS) - 1
HID = 1024
HT = HID // P
E3 = 8
CAP3 = max(1, int(1.25 * T / E3 * 2))
PAIRS3 = 2
TILES3 = -(-(T * PAIRS3 + E3 * (P - 1)) // P)
TILES3 += -TILES3 % 4
GBUF = 4
CHUNK = 512
NCH = T // CHUNK
TPC = CHUNK // P
CHECK = 1024
CHECK_H1, CHECK_REST = HT * HID // CHECK, (HT * HID + 2 * KC * HID + HT * D) // CHECK
SPLITS = 3 * HT
LNB = 4
PAIRS = NT // ST
SENT0 = 16
FREE = 1
MAGIC = 1.5 * 2.0 ** 23


def program(nc, a, out, stages):
    ctx = ExitStack()
    with ctx:
        def sem(name):
            return ctx.enter_context(nc.semaphore(name))

        def sb(name, shape, dt, c=ctx):
            return c.enter_context(nc.sbuf_tensor(name, shape, dt))

        X = sb("X", [P, NT, D], F32)
        XNT = sb("XNT", [P, KC, T], F32)
        tg = sb("tg", [P, 8], F32)
        ident = sb("ident", [P, P], F32)
        ident_bf = sb("ident_bf", [P, P], BF16)
        ln_st = sb("ln_st", [P, NT, 6], F32)
        ln_tmp = sb("ln_tmp", [P, 8, NT], F32)
        xn = [sb(f"xn{i}", [P, ST, D], F32) for i in range(LNB)]
        gb = sb("gb", [P, 8], F32)
        probs_e = sb("probs_e", [P, NT, E0], F32)
        route = [sb(f"route{i}", [P, NT, E0], F32) for i in range(6)]
        row_m = sb("row_m", [P, 6, NT], F32)
        flags = sb("flags", [P, NT, 2, E0], BF16)
        totals = sb("totals", [P, NT, 2 * E0], F32)
        sums = sb("sums", [P, NT, 2 * E0], F32)
        rev = sb("rev", [P, E0], F32)
        rev_i = sb("rev_i", [P, E0], I32)
        ones_bf = sb("ones_bf", [P, P], BF16)
        zeros_bf = sb("zeros_bf", [1, P], BF16)
        upto = sb("upto", [P, P], BF16)
        ones_f = sb("ones_f", [P, NT], F32)
        col_i = sb("col_i", [P, P], I32)
        col = sb("col", [P, P], F32)
        row_i = sb("row_i", [P, 1], I32)
        row = sb("row", [P, 1], F32)
        spare = sb("spare", [P, 2], F32)

        att = ExitStack()
        ctxT = [sb(f"ctxT{i}", [P, KC, S], F32, att) for i in range(2)]
        wq = sb("wq", [P, KC, D], F32, att)
        wk = sb("wk", [P, KC, D], F32, att)
        wv = sb("wv", [P, KC, D], F32, att)
        wo = sb("wo", [P, CH, D], F32, att)
        bq = sb("bq", [P, HALF], F32, att)
        bq4 = sb("bq4", [P, HALF], F32, att)
        bk = sb("bk", [P, HALF], F32, att)
        bv = sb("bv", [P, D], F32, att)
        bo = sb("bo", [P, D], F32, att)
        bog = sb("bog", [P, D], F32, att)
        qf = sb("qf", [P, HALF, S], F32, att)
        kf = sb("kf", [P, HALF, S], F32, att)
        qr = sb("qr", [P, HALF, S], F32, att)
        kr = sb("kr", [P, HALF, S], F32, att)
        QP = [sb(f"QP{i}", [P, 3, HALF, S], BF16, att) for i in range(2)]
        KP = [sb(f"KP{i}", [P, 3, HALF, S], BF16, att) for i in range(2)]
        Qpack = [sb(f"Qpack{i}", [P, H, S], BF16, att) for i in range(2)]
        Kpack = [sb(f"Kpack{i}", [P, H, S], BF16, att) for i in range(2)]
        Vb = [sb(f"Vb{i}", [P, ST, D], F32, att) for i in range(2)]
        V = [sb(f"V{i}", [P, ST, H, VW], F32, att) for i in range(2)]
        On = sb("On", [P, CH, S], F32, att)
        rden = sb("rden", [P, ST, H], F32, att)
        Oq = sb("Oq", [P, ST, D], F32, att)
        OT = sb("OT", [P, HALF, S], F32, att)
        mx = sb("mx", [P, ST, H], F32, att)
        MR = sb("MR", [H, 2, S], BF16, att)
        mask_u8 = sb("mask_u8", [P, 2, ST, S], U8, att)
        mask_bf = sb("mask_bf", [P, 2, ST, S], BF16, att)
        pad_u8 = sb("pad_u8", [B, S], U8, att)
        pad_bf = sb("pad_bf", [B, S], BF16, att)
        padT_u8 = sb("padT_u8", [P, ST, B], U8, att)
        keep = sb("keep", [P, ST, B], F32, att)
        nmax = sb("nmax", [P, ST, H], F32, att)
        esum = sb("esum", [P, ST, H], F32, att)
        rsum = sb("rsum", [P, ST, H], F32, att)
        pt_ctx = ExitStack()
        pT = [sb(f"pT{i}", [P, ST, S], F32, pt_ctx) for i in range(8)]
        pt_ctx.close()
        probs = sb("probs", [P, ST, H, S], F32, att)
        M2 = sb("M2", [P, 2, 2, S], F32, att)
        M1 = sb("M1", [P, ST, S], F32, att)
        m1p = sb("m1p", [P, ST, 2, S], BF16, att)
        hpart = sb("hpart", [P, 2, S], F32, att)
        hsum = sb("hsum", [P, ST, S], F32, att)
        nident_bf = sb("nident_bf", [P, P], BF16, att)
        att.close()

        f0c = ExitStack()
        wu0 = sb("wu0", [P, NG0, KC, FT0 * P], F32, f0c)
        wd0 = sb("wd0", [P, E0, FT0, D], F32, f0c)
        bu0 = sb("bu0", [P, NG0, FT0], F32, f0c)
        wr0 = sb("wr0", [P, KC, E0], F32, f0c)
        br0 = sb("br0", [P, E0], F32, f0c)
        mid0 = [sb(f"mid0_{i}", [P, FT0, TOP0], F32, f0c) for i in range(2)]
        pos_i = sb("pos_i", [P, NT, E0], I32, f0c)
        place_i = sb("place_i", [P, NT, E0], I32, f0c)
        half_i = sb("half_i", [P, NT, E0], I32, f0c)
        place0 = sb("place0", [P, NT, E0], F32, f0c)
        in_half = sb("in_half", [P, NT, E0, SL0], F32, f0c)
        lists0 = sb("lists0", [P, E0, NT, 5, SL0], BF16, f0c)
        gpart = [sb(f"gpart{i}", [P, NT, E0], BF16, f0c) for i in range(3)]
        grest = [sb(f"grest{i}", [P, NT, E0], F32, f0c) for i in range(2)]
        hot0 = [sb(f"hot0_{i}", [P, NT, P], BF16, f0c) for i in range(2)]
        idx0 = sb("idx0", [P, E0, SL0], I32, f0c)
        gate0 = sb("gate0", [P, E0, SL0], F32, f0c)
        gsum0 = sb("gsum0", [P, E0, SL0], F32, f0c)
        idl0 = sb("idl0", [P, E0, SL0], F32, f0c)
        xg0 = [sb(f"xg0_{i}", [P, SL0, D], F32, f0c) for i in range(GBUF)]
        xgT0 = [sb(f"xgT0_{i}", [P, KC, TOP0], F32, f0c) for i in range(2)]
        yg0 = [sb(f"yg0_{i}", [P, SL0, D], F32, f0c) for i in range(2)]
        thr = sb("thr", [P, E0], I32, f0c)
        need = sb("need", [P, E0], F32, f0c)
        coef = sb("coef", [P, NT, E0], F32, f0c)
        cand = sb("cand", [P, DIGIT, E0], I32, f0c)
        step_i = sb("step_i", [P, DIGIT, E0], I32, f0c)
        step_f = sb("step_f", [P, DIGIT, E0], F32, f0c)
        reached = sb("reached", [P, DIGIT, E0], F32, f0c)
        taken = sb("taken", [P, E0], I32, f0c)
        cnt = sb("cnt", [P, DIGIT, E0], F32, f0c)
        above = sb("above", [P, DIGIT, NT, E0], BF16, f0c)
        f0c.close()
        f1c = ExitStack()
        QT1 = sb("QT1", [P, KC, T], BF16, f1c)
        rhs1 = sb("rhs1", [P, KC, D], F32, f1c)
        rmax = sb("rmax", [P, D], F32, f1c)
        rall = sb("rall", [P, D], F32, f1c)
        rscale = sb("rscale", [P, D], F32, f1c)
        rinv = sb("rinv", [P, D], F32, f1c)
        rtmp = sb("rtmp", [P, KC, D], F32, f1c)
        qrhs = sb("qrhs", [P, KC, D], BF16, f1c)
        lmax = sb("lmax", [P, NT], F32, f1c)
        lscale = sb("lscale", [P, NT], F32, f1c)
        linv = sb("linv", [P, NT], F32, f1c)
        qn = [sb(f"qn{i}", [P, ST, D], BF16, f1c) for i in range(LNB)]
        y1 = [sb(f"y1_{i}", [P, ST, D], F32, f1c) for i in range(2)]
        f1c.close()
        f2c = ExitStack()
        w1_2 = sb("w1_2", [P, KC, HID], F32, f2c)
        w2_2 = sb("w2_2", [P, KC, HID], F32, f2c)
        h1_2 = sb("h1_2", [P, HT, HID], F32, f2c)
        h2_2 = sb("h2_2", [P, HT, HID], F32, f2c)
        w3_2 = sb("w3_2", [P, HT, D], F32, f2c)
        sc2 = sb("sc2", [P, 4, HT], F32, f2c)
        s3_2 = sb("s3_2", [P, D], F32, f2c)
        hA = sb("hA", [P, HT, CHUNK], F32, f2c)
        hB = sb("hB", [P, HT, CHUNK], F32, f2c)
        left2, leftX = [xn[i][:].rearrange("p t c -> p (t c)") for i in range(2)]
        sil = [xn[2 + i][:].rearrange("p t c -> p (t c)") for i in range(2)]
        y2 = [xn[1][:, i] for i in range(ST)]
        partA = sb("partA", [P, 2, HT, CHUNK], BF16, f2c)
        partB = sb("partB", [P, 2, HT, CHUNK], BF16, f2c)
        partX = sb("partX", [P, 2, KC, CHUNK], BF16, f2c)
        low2 = sb("low2", [P, CHECK_H1 + CHECK_REST], F32, f2c)
        lowest2 = sb("lowest2", [1, 2], F32, f2c)
        wide2 = sb("wide2", [1, 2], I32, f2c)
        f2c.close()
        f3c = ExitStack()
        w1_3 = sb("w1_3", [P, E3, KC, HID], F32, f3c)
        w2_3 = sb("w2_3", [P, E3, HT, D], F32, f3c)
        wr3 = sb("wr3", [P, KC, E3], F32, f3c)
        kept = [sb(f"kept{i}", [P, NT, E3], F32, f3c) for i in range(PAIRS3)]
        count3 = sb("count3", [P, PAIRS3, E3], F32, f3c)
        load3 = sb("load3", [P, E3], F32, f3c)
        load3_i = sb("load3_i", [P, E3], I32, f3c)
        tiles3 = sb("tiles3", [P, E3], F32, f3c)
        upto3 = sb("upto3", [P, E3], F32, f3c)
        start3 = sb("start3", [P, PAIRS3, E3], F32, f3c)
        slot3 = sb("slot3", [P, PAIRS3, NT], F32, f3c)
        slot3_i = sb("slot3_i", [P, PAIRS3, NT], I32, f3c)
        place3_i = sb("place3_i", [P, PAIRS3, NT], I32, f3c)
        tile3_i = sb("tile3_i", [P, PAIRS3, NT], I32, f3c)
        place3 = sb("place3", [P, PAIRS3, NT], F32, f3c)
        tile3 = sb("tile3", [P, PAIRS3, NT], F32, f3c)
        part3 = [sb(f"part3_{i}", [P, PAIRS3, NT], BF16, f3c) for i in range(3)]
        rest3 = [sb(f"rest3_{i}", [P, PAIRS3, NT], F32, f3c) for i in range(2)]
        idx3 = sb("idx3", [P, TILES3], I32, f3c)
        idl3 = [sb(f"idl3_{i}", [P, TILES3], F32, f3c) for i in range(2)]
        gate3 = [sb(f"gate3_{i}", [P, TILES3], F32, f3c) for i in range(2)]
        before3 = sb("before3", [P, TILES3, E3], F32, f3c)
        expert3 = sb("expert3", [P, TILES3], F32, f3c)
        expert3_i = sb("expert3_i", [P, TILES3], I32, f3c)
        l3c = ExitStack()
        hot3 = sb("hot3", [P, PAIRS3, NT, P], BF16, l3c)
        lists3 = sb("lists3", [P, PAIRS3, NT, 6, TILES3], BF16, l3c)
        l3c.close()
        xg3 = [sb(f"xg3_{i}", [P, D], F32, f3c) for i in range(GBUF)]
        xgT3 = [sb(f"xgT3_{i}", [P, KC, P], F32, f3c) for i in range(2)]
        w1_tile = [XNT[:, i].rearrange("p (c n) -> p c n", c=KC) for i in range(2)]
        mid3 = [sb(f"mid3_{i}", [P, HT, P], F32, f3c) for i in range(2)]
        yg3 = [sb(f"yg3_{i}", [P, D], F32, f3c) for i in range(2)]
        f3c.close()
        ps = [ctx.enter_context(nc.psum_tensor(f"ps{i}", [P, 2, S], F32)) for i in range(8)]
        P0, P1 = ps[0], ps[1]
        A = ps[2:6]
        O = ps[6:8]
        UP3 = ((ps[0], ps[1]), (ps[2], ps[6]))

        x_rows = nc.dram_tensor("x_rows", (T + P, D), F32, kind="Internal").ap()
        xn_rows = nc.dram_tensor("xn_rows", (T + P, D), F32, kind="Internal").ap()
        pad_dram = nc.dram_tensor("pad_rows", (B, S), BF16, kind="Internal").ap()

        names = ("x_loaded ident_ready tg_ready gates_loaded ln_stats ln_std ln_mid xn_ready "
                 "xnt_psum xnt_done w_loaded qk_loaded bias_ready bias_added ctx0 ctx1 q_psum k_psum v_psum q_evac k_evac q_r1 "
                 "k_r1 q_mid k_mid q_split k_split pack0 pack1 pack_k0 pack_k1 padrow0 padrow1 v_copied v_ready smax_ps smax_done mT_ps m_hi m_lo mrow0 "
                 "mrow1 st_ps exp_done av_done o_out oT_ps on_rden on_norm o2_ps on_ready y_ps x_res mask_loaded mask_ready pad_out "
                 "nmax_ready rsum_ready vs_ready p1_ps p1_max m1_step m1_ready p2_ps exp1_done sum1_step norm1 av1_done x_ffn stored "
                 "pack_const pack_rows rt_const rt_logits rt_step rt_exp rt_cnt rt_prefix thr_step thr_cmp thr_cnt "
                 "xn_out0 xn_out1 xn_out2 xn_out3 rows_ready "
                 "experts_w0 experts_w1 experts_w2 experts_w3 experts_w4 experts_w5 experts_w6 experts_w7 "
                 "f0_router f0_step f0_hot f0_list f0_idstep f0_idx "
                 "f0_xt f0_xgT f0_up f0_mid f0_down f0_yg f0_scatter x_back "
                 "f1_rhs f1_rmax f1_rall f1_rstep f1_qrhs f1_qstep f1_ps f1_y f1_acc "
                 "f2_w f2_h1 f2_h2 f2_w3 f2_low f2_low_ps f2_wide f2_xstep f2_xpart f2_step f2_part f2_up f2_sil f2_hA f2_mm f2_act f2_yps f2_y f2_acc "
                 "f3_router f3_place f3_gates f3_loaded f3_hot f3_list f3_idx "
                 "gather0 gather1 gather2 gather3 f3_xt f3_xgT f3_up f3_w1_act f3_w1_dve f3_mid f3_down f3_yg f3_scatter").split()
        s = {n: sem(n) for n in names}
        ctx_sem = [s["ctx0"], s["ctx1"]]
        pack = [s["pack0"], s["pack1"]]
        pack_k = [s["pack_k0"], s["pack_k1"]]
        padrow = [s["padrow0"], s["padrow1"]]
        mrow = [s["mrow0"], s["mrow1"]]
        xn_out = [s[f"xn_out{j}"] for j in range(LNB)]
        GATHERED = (("ffn", 0), ("ffn", 3))
        g_order = {st: i for i, st in enumerate([st for st in stages if st in GATHERED])}

        def wait(eng, semaphore, value):
            if not isinstance(value, int) or value > 0:
                eng.wait_ge(semaphore, value)

        n_att = [L for kind, L in stages if kind == "att"]
        order = {("att", L): i for i, L in enumerate(n_att)}
        m_order = {L: i for i, L in enumerate([L for L in n_att if L in SOFTMAX_KEYS])}
        s_order = {L: i for i, L in enumerate([L for L in n_att if L != 1])}
        ln_order = {st: i for i, st in enumerate(stages)}
        def qk_total(i):
            return 16 * sum(4 + 2 * (l == 2) for l in n_att[:i + 1])

        def pack_keys(eng, par, done):
            for j, part in enumerate(K_PARTS):
                eng.dma_start(Kpack[par][DH * j:DH * (j + 1)].rearrange("d (e f) t -> d e (f t)", f=HALF),
                              KP[par][:, part]).then_inc(done, 16)

        SENT = 16 * len(Q_PARTS)

        def packed(i, v):
            per = [SENT * (1 if l in SOFTMAX_KEYS else 2) for l in n_att[:i + 1]]
            return B // 2 * sum(per[:i]) + per[i] * v

        def keys_packed(i, v):
            return SENT * (B // 2 * sum(l in SOFTMAX_KEYS for l in n_att[:i]) + v)


        def ready_x(eng, n):
            if n == 0:
                eng.wait_ge(s["x_loaded"], 16)
                return
            kind, L = stages[n - 1]
            if kind == "att":
                eng.wait_ge(s["x_res"], FREE + 8 * (order["att", L] + 1))
            else:
                eng.wait_ge(s["x_ffn"], 1 + sum(k != "att" for k, _ in stages[:n - 1]))

        def slots(eng, slot):
            slot(0, 0, 0)
            with eng.Fori(0, 2) as i:
                slot(1 + 2 * i, 1, i)
                slot(2 + 2 * i, 0, i + 1)
            for b in range(B - 3, B):
                slot(b, b % 2, b // 2)

        def high(x):
            k = len(x.shape)
            return x.bitcast(BF16).rearrange({2: "p (n two) -> p n two", 3: "p c (n two) -> p c n two"}[k], two=2)[(slice(None),) * k + (1,)]

        def low(x):
            return x.bitcast(U16).rearrange("p (n two) -> p n two", two=2)[:, :, 0]

        def exists(b):
            return not isinstance(b, int) or 0 <= b < B

        block = ctx.enter_context(nc.Block())

        @block.sync
        def _(sp):
            for j in range(LNB):
                sp.sem_inc(xn_out[j], SENT0)
            sp.dma_start(X[:], a["x"].rearrange("(t p) c -> p t c", p=P)).then_inc(s["x_loaded"], 16)
            sp.dma_start(gb[:, 0:4], a["g_xattn"].partition_broadcast(P)).then_inc(s["gates_loaded"], 16)
            sp.dma_start(gb[:, 4:8], a["g_ffn"].partition_broadcast(P)).then_inc(s["gates_loaded"], 16)
            if ("att", 0) in stages:
                sp.dma_start(mask_u8[:, 0], a["mask_qk"]).then_inc(s["mask_loaded"], 16)
                sp.dma_start(mask_u8[:, 1], a["mask_kq"]).then_inc(s["mask_loaded"], 16)

            def load_ctx(b, par):
                sp.dma_start(ctxT[par][:], a["ctxT"][:, :, ds(b * S, S)]).then_inc(ctx_sem[par], 16)

            def attention(n, L):
                i = order["att", L]
                if n > 0:
                    ready_x(sp, n)
                load_ctx(0, 0)
                for w, name in ((wk[:], "wk"), (bk[:], "bk"), (wq[:], "wq"), (bq[:], "bq")):
                    sp.dma_start(w, a[f"{name}{L}"]).then_inc(s["qk_loaded"], 16)
                if L == 2:
                    sp.dma_start(pad_u8[:], a["pad"]).then_inc(s["qk_loaded"], 16)
                    sp.dma_start(padT_u8[:], a["padT"]).then_inc(s["qk_loaded"], 16)
                sp.dma_start(wv[:], a[f"wv{L}"]).then_inc(s["w_loaded"], 16)
                load_ctx(1, 1)
                for w, name in ((bv, "bv"), (bo, "bo")):
                    sp.dma_start(w[:], a[f"{name}{L}"].partition_broadcast(P)).then_inc(s["w_loaded"], 16)
                sp.dma_start(wo[:, 0:HALF] if L in SOFTMAX_KEYS else wo[:], a[f"wo{L}"]).then_inc(s["w_loaded"], 16)
                if L in SOFTMAX_KEYS:
                    sp.wait_ge(s["rt_const"], 1)
                    for par in range(2):
                        for rows, src in ((Kpack[par][MASK_ROW:MAX_ROW + 2], ones_bf[0:3]),
                                          (Qpack[par][MASK_ROW:MASK_ROW + 1], (zeros_bf if L == 0 else ones_bf)[0:1])):
                            sp.dma_start(rows.rearrange("r h (a c) -> r (h a) c", c=P),
                                         src.unsqueeze(1).to_broadcast([src.shape[0], H * S // P, P])).then_inc(s["pack_rows"], 16)
                if L == 2:
                    sp.wait_ge(s["mask_ready"], 1 + (("att", 0) in stages))
                    sp.dma_start(pad_dram, pad_bf[:]).then_inc(s["pad_out"], 16)
                if L in SOFTMAX_KEYS:
                    sp.wait_ge(s["pack_rows"], 64 * (m_order[L] + 1))
                if L == 2:
                    sp.wait_ge(s["pad_out"], 16)

                def packs(b, par):
                    first = isinstance(b, int) and b == 0
                    if first and L not in SOFTMAX_KEYS:
                        sp.wait_ge(s["k_split"], 8 * i + 1)
                    elif L not in SOFTMAX_KEYS:
                        sp.wait_ge(s["q_split"], 8 * i + b + 1)
                    if L not in SOFTMAX_KEYS:
                        pack_keys(sp, par, pack[par])
                    if first:
                        sp.wait_ge(s["v_psum"], 8 * i + 1)
                        load_ctx(2, 0)
                        sp.wait_ge(s["q_split"], 8 * i + 1)
                    for j, part in enumerate(Q_PARTS):
                        sp.dma_start(Qpack[par][DH * j:DH * (j + 1)].rearrange("d (e f) t -> d e (f t)", f=HALF),
                                     QP[par][:, part]).then_inc(pack[par], 16)
                    if L == 2:
                        sp.dma_start(Kpack[par][MASK_ROW:MASK_ROW + 1],
                                     pad_dram[ds(b, 1), :].unsqueeze(1).to_broadcast([1, H, S])).then_inc(padrow[par], 16)

                def max_rows(b, par):
                    if L in SOFTMAX_KEYS:
                        sp.wait_ge(s["m_lo"], 8 * m_order[L] + b + 1)
                        for row_ in range(2):
                            sp.dma_start(Qpack[par][MAX_ROW + row_:MAX_ROW + row_ + 1], MR[:, row_]).then_inc(mrow[par], 16)

                packs(0, 0)
                max_rows(0, 0)

                def slot(b, par, v):
                    if exists(b + 1):
                        packs(b + 1, 1 - par)
                    if exists(b + 3):
                        sp.wait_ge(s["v_psum"], 8 * i + b + 2)
                        load_ctx(b + 3, 1 - par)
                    if exists(b + 1):
                        max_rows(b + 1, 1 - par)

                slots(sp, slot)

            def send_rows(n):
                for part in range(4):
                    tiles = slice(part * NT // 4, (part + 1) * NT // 4)
                    sp.dma_start(x_rows[0:T].rearrange("(t p) c -> p t c", p=P)[:, tiles], X[:, tiles]).then_inc(s["rows_ready"], 16)
                sp.dma_start(x_rows[T:T + P], X[:, 0]).then_inc(s["rows_ready"], 16)
                sp.dma_start(xn_rows[T:T + P], X[:, 0]).then_inc(s["rows_ready"], 16)

            def send_normed(n):
                table = xn_rows[0:T].rearrange("(t p) c -> p t c", p=P)
                with sp.Fori(0, PAIRS // LNB) as t:
                    for j in range(LNB):
                        sp.wait_ge(s["xn_ready"], PAIRS * n + LNB * t + j + 1)
                        sp.dma_start(table[:, ds(ST * (LNB * t + j), ST)], xn[j][:]).then_inc(xn_out[j], 16)

            def ffn(n, L):
                ready_x(sp, n)
                if L == 0:
                    sp.dma_start(wr0[:], a["wr0"]).then_inc(s["f0_router"], 16)
                    sp.dma_start(br0[:], a["br0"].partition_broadcast(P)).then_inc(s["f0_router"], 16)
                    sp.dma_start(bu0[:], a["bu0"]).then_inc(s["f0_router"], 16)
                    send_rows(n)
                    send_normed(n)
                    for g in range(NG0):
                        sp.dma_start(wu0[:, g], a["wu0"][:, g]).then_inc(s[f"experts_w{g}"], 16)
                        sp.dma_start(wd0[:, 2 * g:2 * g + 2], a["wd0"][:, 2 * g:2 * g + 2]).then_inc(s[f"experts_w{g}"], 16)
                    sp.wait_ge(s["f0_scatter"], 16 * SL0 * E0)
                    sp.dma_start(X[:], x_rows[0:T].rearrange("(t p) c -> p t c", p=P)).then_inc(s["x_back"], 16)
                elif L == 1:
                    sp.dma_start(rhs1[:], a["rhs1"]).then_inc(s["f1_rhs"], 16)
                elif L == 2:
                    for w, name in ((sc2, "sc2"), (w1_2, "w1_2"), (w2_2, "w2_2")):
                        sp.dma_start(w[:], a[name]).then_inc(s["f2_w"], 16)
                    for w, name in ((h1_2, "h1_2"), (h2_2, "h2_2"), (w3_2, "w3_2")):
                        sp.dma_start(w[:], a[name]).then_inc(s[f"f2_{name[:2]}"], 16)
                    sp.dma_start(s3_2[:], a["s3_2"].partition_broadcast(P)).then_inc(s["f2_w3"], 16)
                else:
                    sp.dma_start(wr3[:], a["wr3"]).then_inc(s["f3_router"], 16)
                    send_rows(n)

                    def load(e):
                        sp.dma_start(w1_3[:, e], a["w1_3"][e]).then_inc(s[f"experts_w{e}"], 16)
                        sp.dma_start(w2_3[:, e], a["w2_3"][e]).then_inc(s[f"experts_w{e}"], 16)

                    load(0)
                    send_normed(n)
                    for e in range(E3):
                        if e:
                            load(e)
                        sp.wait_ge(s[f"experts_w{e}"], 32 + 32 * (("ffn", 0) in stages and e < NG0))
                        sp.sem_inc(s["f3_loaded"], 1)

            for n, (kind, L) in enumerate(stages):
                if kind == "att":
                    attention(n, L)
                else:
                    ffn(n, L)
            if stages[-1] == ("ffn", 3):
                sp.wait_ge(s["f3_scatter"], 16 * TILES3)
                sp.dma_start(out, x_rows[0:T]).then_inc(s["stored"], 16)
            else:
                ready_x(sp, len(stages))
                sp.dma_start(out.rearrange("(t p) c -> p t c", p=P), X[:]).then_inc(s["stored"], 16)
            sp.wait_ge(s["stored"], 16)

        @block.gpsimd
        def _(pool):
            pool.memset(ident[:], 0.0).then_inc(s["ident_ready"], 1)
            pool.wait_ge(s["ident_ready"], 1)
            pool.affine_select(out=ident[:], in_=ident[:], compare_op=ALU.not_equal, fill=1.0, base=0,
                               pattern=[[-1, P]], channel_multiplier=1).then_inc(s["ident_ready"], 1)
            pool.wait_ge(s["ident_ready"], 2)
            pool.tensor_copy(ident_bf[:], ident[:]).then_inc(s["ident_ready"], 1)
            pool.memset(ones_f[:], 1.0)
            pool.memset(upto[:], 1.0)
            pool.memset(zeros_bf[:], 0.0)
            pool.memset(ones_bf[:], 1.0).then_inc(s["rt_const"], 1)
            pool.wait_ge(s["rt_const"], 1)
            pool.affine_select(out=upto[:], in_=upto[:], compare_op=ALU.is_ge, fill=0.0, base=0,
                               pattern=[[1, P]], channel_multiplier=-1)
            pool.iota(rev_i[:], pattern=[[-1, E0]], base=E0, channel_multiplier=0).then_inc(s["rt_const"], 1)
            pool.wait_ge(s["rt_const"], 2)
            pool.tensor_copy(rev[:], rev_i[:])
            pool.iota(col_i[:], pattern=[[1, P]], base=0, channel_multiplier=0)
            pool.iota(row_i[:], pattern=[[0, 1]], base=0, channel_multiplier=1).then_inc(s["rt_const"], 1)
            pool.wait_ge(s["rt_const"], 3)
            pool.tensor_copy(col[:], col_i[:])
            pool.tensor_copy(row[:], row_i[:]).then_inc(s["rt_const"], 1)
            pool.wait_ge(s["rt_const"], 4)
            pool.tensor_scalar(spare[:, 0:1], row[:], float(T), None, ALU.add)
            pool.tensor_scalar(spare[:, 1:2], row[:], -1.0, -float(T), ALU.mult, ALU.add).then_inc(s["rt_const"], 1)

            def attention(n, L):
                i = order["att", L]
                if n > 0:
                    ready_x(pool, n)
                if L in SOFTMAX_KEYS:
                    pool.wait_ge(s["k_split"], 8 * i + 1)
                    pool.wait_ge(s["pack_rows"], 64 * (m_order[L] + 1))
                    pack_keys(pool, 0, pack_k[0])
                if L != 0:
                    pool.wait_ge(s["bias_ready"], 2 * i + 2)
                    pool.wait_ge(s["xn_ready"], 8 * (ln_order["att", L] + 1))
                    pool.tensor_tensor(X[:], X[:], bog[:].unsqueeze(1).to_broadcast([P, NT, D]), ALU.add)\
                        .then_inc(s["bias_added"], 1)
                if L in SOFTMAX_KEYS:
                    for b in range(1, B):
                        pool.wait_ge(s["m_lo"], 8 * m_order[L] + b)
                        pack_keys(pool, b % 2, pack_k[b % 2])

            def rows_sent(n):
                pool.wait_ge(s["rows_ready"], 6 * 16 * (g_order[stages[n]] + 1))
                for j in range(LNB):
                    pool.wait_ge(xn_out[j], SENT0 + 16 * (PAIRS // LNB) * (g_order[stages[n]] + 1))

            def gather(to, index, done):
                pool.indirect_dma_start(out=to, out_offset=None, in_=xn_rows, in_offset=bass.IndirectOffsetOnAxis(ap=index, axis=0))\
                    .then_inc(done, 16)

            def scatter_add(frm, index, done):
                pool.indirect_dma_start(out=x_rows, out_offset=bass.IndirectOffsetOnAxis(ap=index, axis=0), in_=frm, in_offset=None,
                                        compute_op=ALU.add).then_inc(done, 16)

            def ffn0(n):
                rows_sent(n)
                def fetch(e):
                    pool.wait_ge(s["f0_idx"], e + 1)
                    wait(pool, s["f0_xt"], e - GBUF + 1)
                    for h in range(SL0):
                        gather(xg0[e % GBUF][:, h], idx0[:, e, h:h + 1], s[f"gather{e % GBUF}"])
                for e in range(GBUF):
                    fetch(e)
                for e in range(E0):
                    pool.wait_ge(s["f0_yg"], e + 1)
                    wait(pool, s["f0_scatter"], 16 * SL0 * e)
                    for h in range(SL0):
                        scatter_add(yg0[e % 2][:, h], idx0[:, e, h:h + 1], s["f0_scatter"])
                    if e + GBUF < E0:
                        fetch(e + GBUF)

            def ffn3(n):
                wide = [P, PAIRS3, NT, TILES3]
                pool.wait_ge(s["f3_place"], 1)
                for v in range(1, 3):
                    e = pool.tensor_tensor(lists3[:, :, :, 3 + v], lists3[:, :, :, 0], part3[v][:].unsqueeze(3).to_broadcast(wide), ALU.mult)
                e.then_inc(s["f3_gates"], 1)
                rows_sent(n)
                pool.wait_ge(s["f3_idx"], 1)
                def fetch(t):
                    wait(pool, s["f3_xt"], t - GBUF + 1)
                    gather(xg3[t % GBUF][:], idx3[:, t:t + 1], s[f"gather{t % GBUF}"])
                for t in range(GBUF):
                    fetch(t)
                for t in range(TILES3):
                    pool.wait_ge(s["f3_yg"], t + 1)
                    wait(pool, s["f3_scatter"], 16 * t)
                    scatter_add(yg3[t % 2][:], idx3[:, t:t + 1], s["f3_scatter"])
                    if t + GBUF < TILES3:
                        fetch(t + GBUF)

            for n, (kind, L) in enumerate(stages):
                if kind == "att":
                    attention(n, L)
                elif L in (0, 3):
                    (ffn0 if L == 0 else ffn3)(n)
                elif L == 1:
                    pool.wait_ge(s["f1_rmax"], 1)
                    pool.partition_all_reduce(rall[:], rmax[:], P, bass.bass_isa.ReduceOp.max).then_inc(s["f1_rall"], 1)

        @block.tensor
        def _(pe):
            pe.sem_inc(s["y_ps"], FREE)
            pe.wait_ge(s["ident_ready"], 3)

            rt_order = {L: i for i, L in enumerate([L for k, L in stages if k == "ffn" and L in (0, 3)])}

            def turn_normed(n, first, j):
                pair = PAIRS * n + first + j
                pe.wait_ge(s["xn_ready"], pair + 1)
                pe.wait_ge(s["xnt_done"], pair + 1)
                bank = ps[2 + j][:]
                if stages[n] == ("ffn", 1):
                    src, bank, eye = qn[j], bank.bitcast(BF16), ident_bf
                else:
                    src, eye = xn[j], ident
                for tt in range(ST):
                    for c in range(KC):
                        last = pe.transpose(bank[:, c, tt * P:(tt + 1) * P], src[:, tt, c * P:(c + 1) * P], eye[:])
                last.then_inc(s["xnt_psum"], 1)

            def router(n, pair, w):
                pe.wait_ge(s["xnt_done"], PAIRS * n + LNB + pair + 1)
                for t in range(ST * pair, ST * pair + ST):
                    for c in range(KC):
                        mm = pe.matmul(ps[0][:].rearrange("p a b -> p (a b)")[:, t * E0:(t + 1) * E0], XNT[:, c, t * P:(t + 1) * P],
                                       w[:, c], start=c == 0, stop=c == KC - 1)
                if pair == PAIRS - 1:
                    mm.then_inc(s["rt_logits"], 1)

            def layernorm(n):
                if stages[n][0] == "att":
                    for j in range(LNB):
                        turn_normed(n, 0, j)
                    return
                if stages[n] not in GATHERED:
                    with pe.Fori(0, PAIRS // LNB) as t:
                        for j in range(LNB):
                            turn_normed(n, LNB * t, j)
                    return
                L = stages[n][1]
                pe.wait_ge(s["rt_const"], 5)
                for pair in range(PAIRS):
                    turn_normed(n, pair - pair % LNB, pair % LNB)
                    if pair == 1:
                        pe.wait_ge(s[f"f{L}_router"], 48 if L == 0 else 16)
                    if pair > 1:
                        router(n, pair - 2, wr0 if L == 0 else wr3)
                for pair in range(PAIRS - 2, PAIRS):
                    router(n, pair, wr0 if L == 0 else wr3)

            def attention(n, L):
                i = order["att", L]
                keys = L in SOFTMAX_KEYS
                w_total = 16 * 4 * (i + 1)
                v_before = 8 * sum(l in (1, 2) for l in n_att[:i])

                def key_product(b, par, v, f, c):
                    if (f, c) == (0, 0):
                        pe.wait_ge(ctx_sem[par], 16 * (4 * i + v + 1))
                        if isinstance(b, int) and b < 3:
                            wait(pe, s["k_evac"], 8 * i + b)
                        else:
                            pe.wait_ge(s["x_res"], FREE + 8 * i + b - 3)
                    mm = pe.matmul(P1[:, f], wk[:, c, f * P:(f + 1) * P], ctxT[par][:, c], start=c == 0, stop=c == KC - 1)
                    if (f, c) == (HALF - 1, KC - 1):
                        mm.then_inc(s["k_psum"], 1)

                def proj_k(b, par, v):
                    for f in range(HALF):
                        for c in range(KC):
                            key_product(b, par, v, f, c)

                def query_product(b, f, c):
                    if (f, c) == (0, 0) and not (isinstance(b, int) and b == 0):
                        pe.wait_ge(s["v_copied"], 8 * i + b)
                    mm = pe.matmul(P0[:, f], wq[:, c, f * P:(f + 1) * P], XNT[:, c, ds(b * S, S)], start=c == 0, stop=c == KC - 1)
                    if (f, c) == (HALF - 1, KC - 1):
                        mm.then_inc(s["q_psum"], 1)

                def proj_q(b):
                    for f in range(HALF):
                        for c in range(KC):
                            query_product(b, f, c)

                def value_product(b, par, t, c):
                    if (t, c) == (0, 0):
                        pe.wait_ge(s["q_evac"], 8 * i + b + 1)
                        if keys and not (isinstance(b, int) and b == 0):
                            pe.wait_ge(s["m_lo"], 8 * m_order[L] + b)
                    mm = pe.matmul(P0[:, t], ctxT[par][:, c, t * P:(t + 1) * P], wv[:, c], start=c == 0, stop=c == KC - 1)
                    if (t, c) == (ST - 1, KC - 1):
                        mm.then_inc(s["v_psum"], 1)

                def proj_v(b, par):
                    for t in range(ST):
                        for c in range(KC):
                            value_product(b, par, t, c)

                def smax(b, par, v, h):
                    m = 8 * m_order[L] + b
                    if h == 0:
                        pe.wait_ge(pack[par], packed(i, v + 1))
                        pe.wait_ge(pack_k[par], keys_packed(i, v + 1))
                        if L == 2:
                            pe.wait_ge(padrow[par], 16 * (v + 1))
                        if not (isinstance(b, int) and b < 2):
                            pe.wait_ge(s["on_ready"], 8 * i + b - 1)
                    wait(pe, s["smax_done"], 16 * m + h - 1)
                    for t in range(ST):
                        mm = pe.matmul(A[2 + h % 2][:, t], Qpack[par][0:MASK_ROW + 1, h, t * P:(t + 1) * P],
                                       Kpack[par][0:MASK_ROW + 1, h], start=True, stop=L != 0)
                        if L == 0:
                            mm = pe.matmul(A[2 + h % 2][:, t], ident_bf[:], mask_bf[:, 0, t], start=False, stop=True)
                    mm.then_inc(s["smax_ps"], 1)

                def max_turn(b):
                    pe.wait_ge(s["smax_done"], 16 * (8 * m_order[L] + b + 1))
                    if exists(b + 1):
                        pe.wait_ge(s["q_evac"], 8 * i + b + 2)
                    else:
                        pe.wait_ge(s["v_copied"], 8 * i + b + 1)
                    for t in range(ST):
                        mm = pe.transpose(P0[0:H, 0, t * P:(t + 1) * P], mx[:, t], ident[:])
                    mm.then_inc(s["mT_ps"], 1)

                def scores(b, par, v, h):
                    q = 16 * (8 * s_order[L] + b) + h
                    if h == 0:
                        if keys:
                            pe.wait_ge(mrow[par], 32 * (4 * m_order[L] + v + 1))
                        else:
                            pe.wait_ge(pack[par], packed(i, v + 1))
                    rows = MAX_ROW + 2 if keys else ROWS
                    ring = 2 if keys else 4
                    wait(pe, s["exp_done"], q - ring + 1)
                    for t in range(ST):
                        mm = pe.matmul(A[h % ring][:, t], Kpack[par][0:rows, h, t * P:(t + 1) * P],
                                       Qpack[par][0:rows, h], start=True, stop=L != 0)
                        if L == 0:
                            mm = pe.matmul(A[h % ring][:, t], ident_bf[:], mask_bf[:, 1, t], start=False, stop=True)
                    mm.then_inc(s["st_ps"], 1)

                def weighted(b, par, h, weights, done):
                    c, r0 = h // GROUP, VW * (h % GROUP)
                    for t in range(ST):
                        mm = pe.matmul(O[c // 2][r0:r0 + VW, c % 2], V[par][:, t, h], weights[:, t],
                                       start=t == 0, stop=t == ST - 1)
                    mm.then_inc(done, 1)

                def values(b, par, h):
                    if keys:
                        if h == 0 and L == 0:
                            pe.wait_ge(s["v_copied"], 8 * i + b + 1)
                        elif h == 0:
                            pe.wait_ge(s["v_ready"], v_before + b + 1)
                        pe.wait_ge(s["exp_done"], 16 * (8 * s_order[L] + b) + h + 1)
                    else:
                        if h == 0:
                            wait(pe, s["on_ready"], 8 * i + b)
                        if h % GROUP == 0:
                            pe.wait_ge(s["vs_ready"], 4 * b + h // GROUP + 1)
                    weighted(b, par, h, pT[h % (4 if keys else 8)], s["av_done"])

                def output_turn(b):
                    pe.wait_ge(s["o_out"], 8 * m_order[L] + b + 1)
                    for t in range(ST):
                        for c in range(CH):
                            mm = pe.transpose(A[2 + t][:].rearrange("p a b -> p (a b)")[:, c * P:(c + 1) * P],
                                              On[:, c, t * P:(t + 1) * P], ident[:])
                    mm.then_inc(s["oT_ps"], 1)

                def output_back(b):
                    pe.wait_ge(s["on_norm"], 8 * m_order[L] + b + 1)
                    for f in range(HALF):
                        for t in range(ST):
                            mm = pe.transpose(A[2][:, f, t * P:(t + 1) * P], Oq[:, t, f * P:(f + 1) * P], ident[:])
                    mm.then_inc(s["o2_ps"], 1)

                tiles, lhs = (HALF, OT) if keys else (CH, On)

                def output_product(b, t, c):
                    if (t, c) == (0, 0):
                        pe.wait_ge(s["on_ready"], 8 * i + b + 1)
                        if exists(b + 3):
                            pe.wait_ge(s["k_evac"], 8 * i + b + 4)
                        else:
                            pe.wait_ge(s["x_res"], FREE + 8 * i + b)
                    mm = pe.matmul(P1[:, t], lhs[:, c, t * P:(t + 1) * P], wo[:, c], start=c == 0, stop=c == tiles - 1)
                    if (t, c) == (ST - 1, tiles - 1):
                        mm.then_inc(s["y_ps"], 1)

                def output(b):
                    for t in range(ST):
                        for c in range(tiles):
                            output_product(b, t, c)

                def for_maxima(b, par, v, t, e):
                    k = 8 * t + e
                    if k == 0:
                        pe.wait_ge(pack[par], packed(i, v + 1))
                    if k < 4:
                        wait(pe, s["exp1_done"], 16 * b)
                    else:
                        pe.wait_ge(s["p1_max"], 16 * b + k - 3)
                    for f in range(2):
                        mm = pe.matmul(A[k % 4][:, f], Kpack[par][0:ROWS, 2 * e + f, t * P:(t + 1) * P],
                                       Qpack[par][0:ROWS, 2 * e + f], start=True, stop=True)
                    mm.then_inc(s["p1_ps"], 1)

                def less_maxima(b, par, t):
                    pe.wait_ge(s["m1_ready"], 2 * b + t + 1)
                    if t == 0:
                        pe.wait_ge(s["p1_max"], 16 * (b + 1))
                    for e in range(H // 2):
                        k = 8 * t + e
                        if k >= 4:
                            pe.wait_ge(s["exp1_done"], 16 * b + k - 3)
                        for f in range(2):
                            pe.matmul(A[k % 4][:, f], Kpack[par][0:ROWS, 2 * e + f, t * P:(t + 1) * P],
                                      Qpack[par][0:ROWS, 2 * e + f], start=True, stop=False)
                            for part in range(2):
                                mm = pe.matmul(A[k % 4][:, f], nident_bf[:], m1p[:, t, part], start=False, stop=part == 1)
                        mm.then_inc(s["p2_ps"], 1)

                def values1(b, par, h):
                    if h == 0:
                        pe.wait_ge(s["norm1"], 2 * (b + 1))
                        pe.wait_ge(s["v_ready"], v_before + b + 1)
                        wait(pe, s["on_ready"], 8 * i + b)
                    weighted(b, par, h, probs[:, :, h], s["av1_done"])

                pe.wait_ge(s["qk_loaded"], qk_total(i))
                proj_k(0, 0, 0)
                pe.wait_ge(s["xnt_done"], PAIRS * n + LNB + 1)
                proj_q(0)
                for pair in range(LNB, PAIRS):
                    turn_normed(n, LNB, pair - LNB)
                pe.wait_ge(s["w_loaded"], w_total)
                proj_v(0, 0)
                proj_k(1, 1, 0)
                pe.wait_ge(s["xnt_done"], PAIRS * (n + 1) + LNB)
                proj_q(1)
                if L == 0:
                    pe.wait_ge(s["mask_ready"], 1)
                if keys:
                    for h in range(H):
                        smax(0, 0, 0, h)
                    max_turn(0)

                def slot_keys(b, par, v):
                    before = exists(b - 1)
                    if exists(b + 2):
                        proj_k(b + 2, par, v + 1)
                    if exists(b + 1):
                        proj_v(b + 1, 1 - par)
                    if before:
                        output_turn(b - 1)
                    for h in range(H):
                        scores(b, par, v, h)
                        if h >= 2:
                            values(b, par, h - 2)
                        if h == 3 and before:
                            output_back(b - 1)
                        if h == 7 and before:
                            output(b - 1)
                        if 6 <= h < 6 + H // 2 and exists(b + 1):
                            for k in range(2):
                                smax(b + 1, 1 - par, v + par, 2 * (h - 6) + k)
                        if h == 7 and exists(b + 2):
                            proj_q(b + 2)
                    if exists(b + 1):
                        max_turn(b + 1)
                    for h in range(H - 2, H):
                        values(b, par, h)

                def slot1(b, par, v):
                    for e in range(6):
                        for_maxima(b, par, v, 0, e)
                    for e in range(6, H // 2):
                        if exists(b - 1):
                            for h in range(4 * (e - 6), 4 * (e - 5)):
                                values1(b - 1, 1 - par, h)
                        for_maxima(b, par, v, 0, e)
                    for e in range(H // 2):
                        for_maxima(b, par, v, 1, e)
                        if e < 4 and exists(b - 1):
                            for h in (2 * e + 8, 2 * e + 9):
                                values1(b - 1, 1 - par, h)
                        if e >= 4 and exists(b + 1):
                            value_product(b + 1, 1 - par, e // 2 % 2, e % 2)
                    less_maxima(b, par, 0)
                    less_maxima(b, par, 1)
                    if exists(b + 2):
                        proj_k(b + 2, par, v + 1)
                    if exists(b - 1):
                        output(b - 1)
                    if exists(b + 2):
                        proj_q(b + 2)

                def slot3(b, par, v):
                    for c in range(CH):
                        for k in range(GROUP):
                            scores(b, par, v, GROUP * c + k)
                            if c == 0 and exists(b + 2):
                                key_product(b + 2, par, v + 1, k // 2, k % 2)
                            if c == 1 and exists(b + 1):
                                value_product(b + 1, 1 - par, k // 2, k % 2)
                            if c == 2 and exists(b - 1):
                                for half in range(2):
                                    output_product(b - 1, k // 2, 2 * (k % 2) + half)
                            if c == 3 and exists(b + 2):
                                query_product(b + 2, k // 2, k % 2)
                        if c:
                            for h in range(GROUP * (c - 1), GROUP * c):
                                values(b, par, h)
                    for h in range(H - GROUP, H):
                        values(b, par, h)

                slots(pe, slot_keys if keys else slot1 if L == 1 else slot3)
                if keys:
                    output_turn(B - 1)
                    output_back(B - 1)
                if L == 1:
                    for h in range(H):
                        values1(B - 1, (B - 1) % 2, h)
                output(B - 1)

            def counts(L, bank, cols):
                pe.matmul(bank[:, 0, 0:cols], upto[:], flags[:].rearrange("p t k e -> p (t k e)")[:, 0:cols], start=True, stop=True)
                pe.matmul(bank[:, 1, 0:cols], ones_bf[:], flags[:].rearrange("p t k e -> p (t k e)")[:, 0:cols], start=True, stop=True)\
                    .then_inc(s["rt_prefix"], 1)

            def ffn0(n):
                with pe.Fori(0, DIGITS // UNROLL0) as i:
                    for d in range(UNROLL0):
                        pe.wait_ge(s["thr_cmp"], UNROLL0 * i + d + 1)
                        pe.matmul(ps[1][:].rearrange("p a b -> p (a b)")[:, 0:DIGIT * NT * E0], ones_bf[:],
                                  above[:].rearrange("p j t e -> p (j t e)"), start=True, stop=True).then_inc(s["thr_cnt"], 1)
                pe.wait_ge(s["thr_cmp"], DIGITS + 1)
                counts(0, ps[2], 2 * NT * E0)

                def lists(e):
                    pe.wait_ge(s["f0_hot"], e + 1)
                    for t in range(NT):
                        mm = pe.matmul(ps[3 + e % 2][:, 0, 0:5 * SL0], hot0[e % 2][:, t],
                                       lists0[:, e, t].rearrange("p v h -> p (v h)"), start=t == 0, stop=t == NT - 1)
                    mm.then_inc(s["f0_list"], 1)

                def turn(e):
                    pe.wait_ge(s[f"gather{e % GBUF}"], 16 * SL0 * (e // GBUF + 1))
                    wait(pe, s["f0_xgT"], e)
                    for h in range(SL0):
                        for c in range(KC):
                            mm = pe.transpose(ps[5][:, c, h * P:(h + 1) * P], xg0[e % GBUF][:, h, c * P:(c + 1) * P], ident[:])
                    mm.then_inc(s["f0_xt"], 1)

                def up(e):
                    pe.wait_ge(s[f"experts_w{e // 2}"], 32)
                    pe.wait_ge(s["f0_xgT"], e + 1)
                    for f in range(FT0):
                        wait(pe, s["f0_mid"], FT0 * e + f - 2)
                        for c in range(KC):
                            mm = pe.matmul(ps[f % 3][:, 0], wu0[:, e // 2, c, f * P:(f + 1) * P], xgT0[e % 2][:, c],
                                           start=c == 0, stop=c == KC - 1)
                        mm.then_inc(s["f0_up"], 1)

                def down(e):
                    pe.wait_ge(s["f0_mid"], FT0 * (e + 1))
                    wait(pe, s["f0_yg"], e - 1)
                    for h in range(SL0):
                        for f in range(FT0):
                            rows = P if f < FT0 - 1 else FL0 + 1
                            mm = pe.matmul(ps[6 + e % 2][:, h], mid0[e % 2][0:rows, f, h * P:(h + 1) * P],
                                           wd0[0:rows, e, f], start=f == 0, stop=f == FT0 - 1)
                    mm.then_inc(s["f0_down"], 1)

                lists(0)
                lists(1)
                turn(0)
                for e in range(E0):
                    if e + 2 < E0:
                        lists(e + 2)
                    up(e)
                    if e + 1 < E0:
                        turn(e + 1)
                    if e:
                        down(e - 1)
                down(E0 - 1)

            def ffn1(n):
                pe.wait_ge(s["xnt_done"], PAIRS * (n + 1) + LNB)
                pe.wait_ge(s["f1_qrhs"], 1)

                def pair(b, j, first):
                    if not first:
                        pe.wait_ge(s["f1_y"], b - 1)
                    for t in range(ST):
                        for c in range(KC):
                            mm = pe.matmul(ps[2 + j][:, t], QT1[:, c, ds(b * S + t * P, P)], qrhs[:, c], start=c == 0, stop=c == KC - 1)
                    mm.then_inc(s["f1_ps"], 1)

                pair(0, 0, True)
                pair(1, 1, True)
                with pe.Fori(1, B // 2) as i:
                    for j in range(2):
                        pair(2 * i + j, j, False)

            def ffn2(n):
                pe.wait_ge(s["xnt_done"], PAIRS * (n + 1) + LNB)
                pe.wait_ge(s["f2_w"], 16 * 3)
                pe.wait_ge(s["rt_const"], 1)

                def wide(k):
                    return pe.value_load(wide2[0:1, k:k + 1], min_val=0, max_val=1)

                def check_sum(k, pieces):
                    pe.wait_ge(s["f2_low"], pieces.stop)
                    pe.matmul(ps[7][0:1, 0, pieces], ones_f[:, 0:1], low2[:, pieces], start=True, stop=True).then_inc(s["f2_low_ps"], 1)

                def up(ch, o, x16):
                    wait(pe, s["f2_hA"], ch * HT + o - 1)
                    for k, w in enumerate((w1_2, w2_2)):
                        bank = ps[2 * (o % 2) + k][:].rearrange("p a b -> p (a b)")
                        cols = slice(o * P, (o + 1) * P)
                        tokens = ds(ch * CHUNK, CHUNK)
                        if x16:
                            pairs = [(high(w[:, c, cols]), high(XNT[:, c, tokens])) for c in range(KC)]
                            pairs += [(high(w[:, c, cols]), partX[:, part, c]) for part in range(2) for c in range(KC)]
                        else:
                            pairs = [(w[:, c, cols], XNT[:, c, tokens]) for c in range(KC)]
                        for i, (w_, x_) in enumerate(pairs):
                            if x16 and o == 0 and k == 0 and i >= KC:
                                pe.wait_ge(s["f2_xpart"], KC * (ch - 1) + (i - KC) % KC + 1)
                            mm = pe.matmul(bank, w_, x_, start=i == 0, stop=i == len(pairs) - 1)
                    mm.then_inc(s["f2_up"], 1)

                def tile_ready(ch, stage, c):
                    if stage == 0:
                        pe.wait_ge(s["f2_hA"], ch * HT + c + 1)
                    else:
                        pe.wait_ge(s["f2_act"], (2 * ch + stage - 1) * HT + c + 1)

                def parts_ready(ch, stage, c):
                    pe.wait_ge(s["f2_part"], ch * SPLITS + stage * HT + c + 1)

                def hidden(ch, stage, x16):
                    w, src, part = ((h1_2, hA, partA), (h2_2, hB, partB))[stage]
                    for o in range(HT):
                        wait(pe, s["f2_act"], (2 * ch + stage) * HT + o - 1)
                        bank = ps[4 + o % 2][:].rearrange("p a b -> p (a b)")
                        for v in range(3 if x16 else 1):
                            for c in range(HT):
                                if o == 0:
                                    (parts_ready if v == 1 else tile_ready)(ch, stage, c)
                                w_ = w[:, c, o * P:(o + 1) * P]
                                if not x16:
                                    mm = pe.matmul(bank, w_, src[:, c], start=c == 0, stop=c == HT - 1)
                                else:
                                    mm = pe.matmul(bank, high(w_), part[:, v - 1, c] if v else high(src[:, c]),
                                                   start=v + c == 0, stop=v == 2 and c == HT - 1)
                        mm.then_inc(s["f2_mm"], 1)

                def last(ch, x16):
                    for t in range(TPC):
                        wait(pe, s["f2_y"], ch * TPC + t - 1)
                        cols = slice(t * P, (t + 1) * P)
                        for v in range(3 if x16 else 1):
                            for c in range(HT):
                                if t == 0:
                                    (parts_ready if v == 1 else tile_ready)(ch, 2, c)
                                if not x16:
                                    mm = pe.matmul(ps[6 + t % 2][:, 0], hA[:, c, cols], w3_2[:, c], start=c == 0, stop=c == HT - 1)
                                else:
                                    mm = pe.matmul(ps[6 + t % 2][:, 0], partA[:, v - 1, c, cols] if v else high(hA[:, c, cols]), high(w3_2[:, c]),
                                                   start=v + c == 0, stop=v == 2 and c == HT - 1)
                        mm.then_inc(s["f2_yps"], 1)

                def either(flag, stage):
                    with pe.If(flag == 0):
                        stage(True)
                    with pe.Else():
                        stage(False)

                def rest(ch):
                    either(wide(1), lambda x16: hidden(ch, 1, x16))
                    either(wide(1), lambda x16: last(ch, x16))

                for o in range(HT):
                    up(0, o, False)
                    if o == HT - 2:
                        check_sum(0, slice(0, CHECK_H1))
                pe.wait_ge(s["f2_wide"], 2)
                either(wide(0), lambda x16: hidden(0, 0, x16))
                check_sum(1, slice(CHECK_H1, CHECK_H1 + CHECK_REST))
                pe.wait_ge(s["f2_wide"], 4)
                rest(0)
                with pe.Fori(1, NCH) as ch:
                    either(wide(1), lambda x16: [up(ch, o, x16) for o in range(HT)])
                    either(wide(0), lambda x16: hidden(ch, 0, x16))
                    rest(ch)

            def ffn3(n):
                gathered = 16 * SL0 * (E0 // GBUF) * (("ffn", 0) in stages)
                pe.wait_ge(s["rt_cnt"], 1)
                counts(3, ps[2], 2 * NT * E3)
                pe.wait_ge(s["f3_gates"], 1)
                for j in range(PAIRS3):
                    pe.wait_ge(s["f3_hot"], j + 1)
                    for t in range(NT):
                        mm = pe.matmul(ps[3][:].rearrange("p a b -> p (a b)")[:, 0:6 * TILES3], hot3[:, j, t],
                                       lists3[:, j, t].rearrange("p v i -> p (v i)"),
                                       start=j + t == 0, stop=j == PAIRS3 - 1 and t == NT - 1)
                mm.then_inc(s["f3_list"], 1)
                pe.wait_ge(s["f3_idx"], 1)

                def expert(t):
                    return pe.value_load(expert3_i[0:1, ds(t, 1)], min_val=0, max_val=E3 - 1)

                def turn(b, k):
                    t = GBUF * b + k
                    pe.wait_ge(s[f"gather{k % GBUF}"], gathered + 16 * (b + k // GBUF + 1))
                    wait(pe, s["f3_xgT"], t - 1)
                    for c in range(KC):
                        mm = pe.transpose(ps[3 + k % 2][:, 0, c * P:(c + 1) * P], xg3[k % GBUF][:, c * P:(c + 1) * P], ident[:])
                    mm.then_inc(s["f3_xt"], 1)

                def up(b, k):
                    t = GBUF * b + k
                    pe.wait_ge(s["f3_w1_act"], t + 1)
                    pe.wait_ge(s["f3_w1_dve"], t + 1)
                    pe.wait_ge(s["f3_xgT"], t + 1)
                    wait(pe, s["f3_mid"], t - 1)
                    for f in range(HT):
                        bank = UP3[k % 2][f // 4][:].rearrange("p a b -> p (a b)")
                        for c in range(KC):
                            mm = pe.matmul(bank[:, f % 4 * P:(f % 4 + 1) * P], w1_tile[k % 2][:, c, f * P:(f + 1) * P], xgT3[k % 2][:, c],
                                           start=c == 0, stop=c == KC - 1)
                    mm.then_inc(s["f3_up"], 1)

                def down(b, k):
                    t = GBUF * b + k
                    e = expert(t)
                    pe.wait_ge(s["f3_loaded"], e + 1)
                    pe.wait_ge(s["f3_mid"], t + 1)
                    wait(pe, s["f3_yg"], t - 1)
                    for c in range(HT):
                        mm = pe.matmul(ps[5 + 2 * (k % 2)][:, 0], mid3[k % 2][:, c], w2_3[:, ds(e, 1), c].squeeze(1), start=c == 0, stop=c == HT - 1)
                    mm.then_inc(s["f3_down"], 1)

                def tiles(b):
                    last = isinstance(b, int) and b == BLOCKS - 1
                    for k in range(GBUF):
                        if not last or k + 1 < GBUF:
                            up(b, k + 1)
                        if not last or k + 2 < GBUF:
                            turn(b, k + 2)
                        down(b, k)

                BLOCKS = TILES3 // GBUF
                turn(0, 0)
                turn(0, 1)
                up(0, 0)
                tiles(0)
                with pe.Fori(1, BLOCKS - 1) as b:
                    tiles(b)
                tiles(BLOCKS - 1)

            for n, (kind, L) in enumerate(stages):
                layernorm(n)
                if kind == "att":
                    attention(n, L)
                else:
                    (ffn0, ffn1, ffn2, ffn3)[L](n)

        @block.scalar
        def _(act):
            act.sem_inc(s["xnt_done"], LNB)
            act.wait_ge(s["gates_loaded"], 32)
            act.activation(tg[:], gb[:], ACT.Tanh).then_inc(s["tg_ready"], 1)

            def layernorm(n):
                act.wait_ge(s["ln_mid"], 4 * n + 3)
                act.activation(ln_tmp[:, 5], ln_tmp[:, 4], ACT.Sqrt).then_inc(s["ln_std"], 1)
                if stages[n][0] == "att":
                    normed_out(n, 0)
                else:
                    with act.Fori(0, PAIRS // LNB) as t:
                        normed_out(n, t)

            def normed_out(n, t):
                for j in range(LNB):
                    pair = LNB * t + j
                    act.wait_ge(s["xnt_psum"], PAIRS * n + pair + 1)
                    if stages[n] == ("ffn", 1):
                        to, bank = QT1, ps[2 + j][:].bitcast(BF16)[:, :, 0:S]
                    else:
                        to, bank = XNT, ps[2 + j][:]
                    act.activation(to[:, :, ds(pair * S, S)], bank, ACT.Copy).then_inc(s["xnt_done"], 1)

            def attention(n, L):
                i = order["att", L]
                keys = L in SOFTMAX_KEYS

                def split_k(b, par, v):
                    g = 8 * i + b
                    act.wait_ge(s["k_psum"], g + 1)
                    if isinstance(b, int) and b == 0:
                        act.wait_ge(s["bias_ready"], 2 * i + 1)
                    if keys:
                        wait(act, pack_k[par], keys_packed(i, v))
                    else:
                        wait(act, pack[par], packed(i, v))
                    wait(act, s["k_r1"], g)
                    for f in range(HALF):
                        act.activation(kf[:, f], P1[:, f], ACT.Identity, bias=bk[:, f:f + 1])
                        e = act.activation(KP[par][:, 0, f], P1[:, f], ACT.Identity, bias=bk[:, f:f + 1])
                    e.then_inc(s["k_evac"], 1)

                def split_q(b, par, v):
                    g = 8 * i + b
                    act.wait_ge(s["q_psum"], g + 1)
                    wait(act, pack[par], packed(i, v))
                    wait(act, s["q_r1"], g)
                    for f in range(HALF):
                        act.activation(qf[:, f], P0[:, f], ACT.Identity, bias=bq4[:, f:f + 1], scale=INV_SQRT)
                        e = act.activation(QP[par][:, 0, f], P0[:, f], ACT.Identity, bias=bq4[:, f:f + 1], scale=INV_SQRT)
                    e.then_inc(s["q_evac"], 1)

                def middle_k(b, par):
                    act.wait_ge(s["k_r1"], 8 * i + b + 1)
                    act.activation(KP[par][:, 1], kr[:], ACT.Copy).then_inc(s["k_mid"], 1)

                def middle_q(b, par):
                    act.wait_ge(s["q_r1"], 8 * i + b + 1)
                    act.activation(QP[par][:, 1], qr[:], ACT.Copy).then_inc(s["q_mid"], 1)

                def max_part(b, par, v):
                    act.wait_ge(s["mT_ps"], 8 * m_order[L] + b + 1)
                    if not (isinstance(b, int) and b == 0):
                        act.wait_ge(mrow[1 - par], 32 * (4 * m_order[L] + v + par))
                    act.activation(MR[:, 0], P0[0:H, 0], ACT.Copy, scale=-1.0).then_inc(s["m_hi"], 1)

                def exps(b, h):
                    q = 16 * (8 * s_order[L] + b) + h
                    if keys:
                        act.wait_ge(s["st_ps"], q + 1)
                        wait(act, s["av_done"], q - 3)
                        act.activation(pT[h % 4][:], A[h % 2][:], ACT.Exp).then_inc(s["exp_done"], 1)
                    else:
                        act.wait_ge(s["nmax_ready"], 16 * b + h + 1)
                        wait(act, s["av_done"], q - 7)
                        for t in range(ST):
                            e = act.activation(pT[h % 8][:, t], A[h % 4][:, t], ACT.Exp, bias=nmax[:, t, h:h + 1],
                                               accum_out=esum[:, t, h:h + 1])
                        e.then_inc(s["exp_done"], 1)

                def exps1(b, t):
                    for e in range(H // 2):
                        k = 8 * t + e
                        act.wait_ge(s["p2_ps"], 16 * b + k + 1)
                        if k == 0:
                            wait(act, s["av1_done"], 16 * b)
                        act.activation(probs[:, t, 2 * e:2 * e + 2], A[k % 4][:], ACT.Exp).then_inc(s["exp1_done"], 1)

                def maxima1(b, t):
                    if not (isinstance(b, int) and b + t == 0):
                        act.wait_ge(s["m1_step"], 6 * b + 3 * t - 1)
                    for e in range(2):
                        k = 16 * b + 8 * t + e
                        act.wait_ge(s["p1_ps"], k + 1)
                        act.activation(M2[:, e], A[e][:], ACT.Copy).then_inc(s["p1_max"], 1)

                def outputs1(b):
                    act.wait_ge(s["av1_done"], 16 * (b + 1))
                    act.wait_ge(s["y_ps"], FREE + 8 * i + b)
                    for c in range(2):
                        e = act.activation(On[:, 2 * c:2 * c + 2], O[c][:], ACT.Copy)
                    e.then_inc(s["on_ready"], 1)

                def outputs_out(b):
                    m = 8 * m_order[L] + b
                    act.wait_ge(s["av_done"], 16 * (8 * s_order[L] + b + 1))
                    wait(act, s["oT_ps"], m)
                    for c in range(2):
                        e = act.activation(On[:, 2 * c:2 * c + 2], O[c][:], ACT.Copy)
                    e.then_inc(s["o_out"], 1)

                def outputs_back(b):
                    act.wait_ge(s["o2_ps"], 8 * m_order[L] + b + 1)
                    act.wait_ge(s["y_ps"], FREE + 8 * i + b)
                    act.activation(OT[:], A[2][:], ACT.Copy).then_inc(s["on_ready"], 1)

                for b in range(2):
                    split_k(b, b, 0)
                    split_q(b, b, 0)
                    middle_k(b, b)
                    middle_q(b, b)
                    if b == 0:
                        normed_out(n, 1)
                if keys:
                    max_part(0, 0, 0)

                def slot_keys(b, par, v):
                    nearer, later = exists(b + 1), exists(b + 2)
                    if later:
                        split_k(b + 2, par, v + 1)
                    for h in range(H):
                        exps(b, h)
                        if h == 3:
                            if later:
                                middle_k(b + 2, par)
                            if exists(b - 1):
                                outputs_back(b - 1)
                        if h == 7 and later:
                            split_q(b + 2, par, v + 1)
                        if h == 9 and later:
                            middle_q(b + 2, par)
                    if nearer:
                        max_part(b + 1, 1 - par, v + par)
                    outputs_out(b)

                def slot1(b, par, v):
                    later = exists(b + 2)
                    maxima1(b, 0)
                    if exists(b - 1) and exists(b + 1):
                        middle_q(b + 1, 1 - par)
                    maxima1(b, 1)
                    if exists(b - 1):
                        outputs1(b - 1)
                    exps1(b, 0)
                    exps1(b, 1)
                    if later:
                        split_k(b + 2, par, v + 1)
                        split_q(b + 2, par, v + 1)
                        middle_k(b + 2, par)

                def slot3(b, par, v):
                    later = exists(b + 2)
                    for h in range(H):
                        exps(b, h)
                        if h == 4 and later:
                            split_k(b + 2, par, v + 1)
                        if h == 8 and later:
                            middle_k(b + 2, par)
                    if later:
                        split_q(b + 2, par, v + 1)
                        middle_q(b + 2, par)

                slots(act, slot_keys if keys else slot1 if L == 1 else slot3)
                if keys:
                    outputs_back(B - 1)
                if L == 1:
                    outputs1(B - 1)

            rt_order = {L: i for i, L in enumerate([L for k, L in stages if k == "ffn" and L in (0, 3)])}

            def route_exp(L):
                act.wait_ge(s["rt_step"], 5 * rt_order[L] + 3)
                act.activation(route[1][:], route[0][:], ACT.Exp).then_inc(s["rt_exp"], 1)

            def ffn0(n):
                route_exp(0)

                act.wait_ge(s["thr_step"], 1)
                def copy(e):
                    act.wait_ge(s["f0_xt"], e + 1)
                    wait(act, s["f0_up"], FT0 * (e - 1))
                    act.activation(xgT0[e % 2][:], ps[5][:], ACT.Copy).then_inc(s["f0_xgT"], 1)

                copy(0)
                for e in range(E0):
                    for f in range(FT0):
                        rows = P if f < FT0 - 1 else FL0
                        act.wait_ge(s["f0_up"], FT0 * e + f + 1)
                        if f == 0:
                            wait(act, s["f0_down"], e - 1)
                        act.activation(mid0[e % 2][0:rows, f], ps[f % 3][0:rows, 0], ACT.Silu,
                                       bias=bu0[0:rows, e // 2, f:f + 1]).then_inc(s["f0_mid"], 1)
                    if e + 1 < E0:
                        copy(e + 1)

            def ffn2(n):
                act.wait_ge(s["f2_w"], 16 * 3)

                pieces = [(h1_2[:, c], s["f2_h1"], 16) for c in range(HT)]
                pieces += [(h2_2[:, c], s["f2_h2"], 16) for c in range(HT)]
                pieces += [(w3_2[:, c:c + CHECK // D].rearrange("p c n -> p (c n)"), s["f2_w3"], 32) for c in range(0, HT, CHECK // D)]
                pieces += [(w[:, c], s["f2_w"], 16 * 3) for w in (w1_2, w2_2) for c in range(KC)]

                def check(i):
                    w, loaded, count = pieces[i]
                    act.wait_ge(loaded, count)
                    if i > 1:
                        act.wait_ge(s["f2_low"], i - 1)
                    act.activation(partX[:, i % 2].rearrange("p c n -> p (c n)"), low(w), ACT.Copy, accum_out=low2[:, i:i + 1])\
                        .then_inc(s["f2_low"], 1)

                def chunk(ch):
                    first = isinstance(ch, int)
                    for o in range(HT):
                        act.wait_ge(s["f2_up"], ch * HT + o + 1)
                        wait(act, s["f2_hA"], ch * HT + o - 1)
                        act.activation(sil[o % 2], ps[2 * (o % 2)][:].rearrange("p a b -> p (a b)"), ACT.Silu, scale=sc2[:, 0, o:o + 1])\
                            .then_inc(s["f2_sil"], 1)
                        if first and 2 <= o < 2 + CHECK_H1 // 2:
                            for i in range(2):
                                check(2 * (o - 2) + i)
                    for stage, dst in enumerate((hB, hA)):
                        for o in range(HT):
                            act.wait_ge(s["f2_mm"], (2 * ch + stage) * HT + o + 1)
                            if o == 0 and stage == 0:
                                wait(act, s["f2_part"], ch * SPLITS)
                            if o == 0 and stage == 1:
                                act.wait_ge(s["f2_mm"], (2 * ch + 1) * HT)
                                act.wait_ge(s["f2_part"], ch * SPLITS + HT)
                            act.activation(dst[:, o], ps[4 + o % 2][:].rearrange("p a b -> p (a b)"), ACT.Gelu,
                                           scale=sc2[:, 2 + stage, o:o + 1]).then_inc(s["f2_act"], 1)
                            if first and stage == 0 and o < CHECK_REST // 2:
                                for i in range(2):
                                    check(CHECK_H1 + 2 * o + i)

                chunk(0)
                with act.Fori(1, NCH) as ch:
                    chunk(ch)

            def ffn3(n):
                route_exp(3)

                act.wait_ge(s["f3_idx"], 1)

                def copy_w1(t, k):
                    e = act.value_load(expert3_i[0:1, ds(t, 1)], min_val=0, max_val=E3 - 1)
                    act.wait_ge(s["f3_loaded"], e + 1)
                    wait(act, s["f3_up"], t - 1)
                    act.activation(w1_tile[k][:, 0], w1_3[:, ds(e, 1), 0].squeeze(1), ACT.Copy).then_inc(s["f3_w1_act"], 1)

                def hidden(t, k):
                    act.wait_ge(s["f3_up"], t + 1)
                    wait(act, s["f3_down"], t - 1)
                    for half in range(2):
                        e = act.activation(mid3[k][:, 4 * half:4 * half + 4], UP3[k][half][:].rearrange("p a (c t) -> p (a c) t", t=P), ACT.Gelu)
                    e.then_inc(s["f3_mid"], 1)

                copy_w1(0, 0)
                copy_w1(1, 1)
                for t in range(2):
                    hidden(t, t)
                    copy_w1(t + 2, t)
                with act.Fori(1, TILES3 // 2 - 1) as i:
                    for k in range(2):
                        hidden(2 * i + k, k)
                        copy_w1(2 * i + k + 2, k)
                for t in range(TILES3 - 2, TILES3):
                    hidden(t, t % 2)

            for n, (kind, L) in enumerate(stages):
                layernorm(n)
                if kind == "att":
                    attention(n, L)
                elif L != 1:
                    {0: ffn0, 2: ffn2, 3: ffn3}[L](n)

        @block.vector
        def _(dve):
            dve.sem_inc(s["x_res"], FREE)
            if ("att", 0) in stages:
                dve.wait_ge(s["mask_loaded"], 32)
                dve.tensor_scalar(mask_bf[:, 0], mask_u8[:, 0], NEG_MAX, None, ALU.mult)
                dve.tensor_scalar(mask_bf[:, 1], mask_u8[:, 1], NEG_EXP, None, ALU.mult).then_inc(s["mask_ready"], 1)

            def quantise(pair, j, e):
                q = 6 * pair
                cols = ds(2 * pair, 2)
                e.then_inc(s["f1_qstep"], 1)
                dve.wait_ge(s["f1_qstep"], q + 1)
                dve.tensor_reduce(lmax[:, cols], xn[j][:], AX.X, ALU.max, apply_absolute_value=True).then_inc(s["f1_qstep"], 1)
                dve.wait_ge(s["f1_qstep"], q + 2)
                dve.tensor_scalar(lscale[:, cols], lmax[:, cols], 1e-12, 1.0 / 127.0, ALU.max, ALU.mult).then_inc(s["f1_qstep"], 1)
                dve.wait_ge(s["f1_qstep"], q + 3)
                dve.reciprocal(linv[:, cols], lscale[:, cols]).then_inc(s["f1_qstep"], 1)
                dve.wait_ge(s["f1_qstep"], q + 4)
                for t in range(ST):
                    e = dve.tensor_scalar(xn[j][:, t], xn[j][:, t], linv[:, ds(2 * pair + t, 1)], -127.0, ALU.mult, ALU.max)
                e.then_inc(s["f1_qstep"], 1)
                dve.wait_ge(s["f1_qstep"], q + 5)
                dve.tensor_scalar(xn[j][:], xn[j][:], 127.0, MAGIC, ALU.min, ALU.add).then_inc(s["f1_qstep"], 1)
                dve.wait_ge(s["f1_qstep"], q + 6)
                dve.tensor_scalar(qn[j][:], xn[j][:], MAGIC, None, ALU.subtract).then_inc(s["xn_ready"], 1)

            def statistics(t):
                dve.bn_stats(ln_st[:, ds(t, 1)], X[:, ds(t, 1)]).then_inc(s["ln_stats"], 1)

            def layernorm(n):
                ready_x(dve, n)
                if n == 0 or stages[n - 1] == ("ffn", 0):
                    with dve.Fori(0, NT // 4) as t:
                        for k in range(4):
                            statistics(4 * t + k)
                dve.wait_ge(s["ln_stats"], NT * (n + 1))
                me, mo = ln_st[:, :, 1], ln_st[:, :, 4]
                dve.tensor_tensor(ln_tmp[:, 0], me, mo, ALU.add)
                dve.tensor_tensor(ln_tmp[:, 1], me, mo, ALU.subtract)
                dve.tensor_tensor(ln_tmp[:, 2], ln_st[:, :, 2], ln_st[:, :, 5], ALU.add).then_inc(s["ln_mid"], 1)
                dve.wait_ge(s["ln_mid"], 4 * n + 1)
                dve.scalar_tensor_tensor(ln_tmp[:, 3], ln_tmp[:, 1], 0.25, ln_tmp[:, 1], ALU.mult, ALU.mult)
                dve.tensor_scalar(ln_tmp[:, 6], ln_tmp[:, 2], 1.0 / D, EPS, ALU.mult, ALU.add)
                dve.tensor_scalar(ln_tmp[:, 7], ln_tmp[:, 0], 0.5, None, ALU.mult).then_inc(s["ln_mid"], 1)
                dve.wait_ge(s["ln_mid"], 4 * n + 2)
                dve.tensor_tensor(ln_tmp[:, 4], ln_tmp[:, 3], ln_tmp[:, 6], ALU.add).then_inc(s["ln_mid"], 1)
                dve.wait_ge(s["ln_std"], n + 1)
                dve.reciprocal(ln_tmp[:, 5], ln_tmp[:, 5]).then_inc(s["ln_mid"], 1)
                dve.wait_ge(s["ln_mid"], 4 * n + 4)
                if stages[n][0] == "att":
                    normed(n, 0)
                else:
                    with dve.Fori(0, PAIRS // LNB) as t:
                        normed(n, t)

            def normed(n, t):
                for j in range(LNB):
                    pair = LNB * t + j
                    if stages[n] in GATHERED or n and stages[n - 1] in GATHERED:
                        sent = sum(st in GATHERED for st in stages[:n]) * PAIRS // LNB
                        dve.wait_ge(xn_out[j], SENT0 + 16 * (sent + (t if stages[n] in GATHERED else 0)))
                    dve.wait_ge(s["xnt_psum"], PAIRS * n + pair + 1 - LNB) if n > 0 else dve.wait_ge(s["xnt_done"], pair + 1)
                    for tt in range(ST):
                        i = 2 * pair + tt
                        e = dve.tensor_scalar(xn[j][:, tt], X[:, ds(i, 1)].squeeze(1), ln_tmp[:, 7, ds(i, 1)], ln_tmp[:, 5, ds(i, 1)],
                                              ALU.subtract, ALU.mult)
                    if stages[n] == ("ffn", 1):
                        quantise(pair, j, e)
                    else:
                        e.then_inc(s["xn_ready"], 1)

            def attention(n, L):
                i = order["att", L]
                keys = L in SOFTMAX_KEYS
                w_total = 16 * 4 * (i + 1)
                dve.wait_ge(s["qk_loaded"], qk_total(i))
                dve.tensor_scalar(bq4[:], bq[:], INV_SQRT, None, ALU.mult).then_inc(s["bias_ready"], 1)
                if L == 2:
                    dve.tensor_scalar(pad_bf[:], pad_u8[:], NEG_MAX, None, ALU.mult)
                    dve.tensor_scalar(keep[:], padT_u8[:], -1.0, 1.0, ALU.mult, ALU.add).then_inc(s["mask_ready"], 1)
                normed(n, 1)

                def constants():
                    for par in range(2):
                        e = dve.memset(V[par][:, :, :, DH + (L == 0):VW], 0.0)
                        if L == 0:
                            e = dve.memset(V[par][:, :, :, DH:DH + 1], 1.0)
                    e.then_inc(s["pack_const"], 1)
                    if L == 1:
                        dve.wait_ge(s["ident_ready"], 2)
                        dve.tensor_scalar(nident_bf[:], ident[:], -1.0, None, ALU.mult)
                    dve.wait_ge(s["w_loaded"], w_total)
                    dve.wait_ge(s["tg_ready"], 1)
                    dve.tensor_scalar(bog[:], bo[:], tg[:, L:L + 1], None, ALU.mult).then_inc(s["bias_ready"], 1)
                    dve.wait_ge(s["pack_const"], i + 1)

                def rest_k(b, par):
                    wait(dve, s["k_split"], 8 * i + b)
                    dve.wait_ge(s["k_evac"], 8 * i + b + 1)
                    dve.tensor_tensor(kr[:], kf[:], KP[par][:, 0], ALU.subtract).then_inc(s["k_r1"], 1)

                def rest_q(b, par):
                    wait(dve, s["q_split"], 8 * i + b)
                    dve.wait_ge(s["q_evac"], 8 * i + b + 1)
                    dve.tensor_tensor(qr[:], qf[:], QP[par][:, 0], ALU.subtract).then_inc(s["q_r1"], 1)

                def low_k(b, par):
                    dve.wait_ge(s["k_mid"], 8 * i + b + 1)
                    dve.tensor_tensor(KP[par][:, 2], kr[:], KP[par][:, 1], ALU.subtract).then_inc(s["k_split"], 1)

                def low_q(b, par):
                    dve.wait_ge(s["q_mid"], 8 * i + b + 1)
                    dve.tensor_tensor(QP[par][:, 2], qr[:], QP[par][:, 1], ALU.subtract).then_inc(s["q_split"], 1)

                def take_values(b, par):
                    g = 8 * i + b
                    dve.wait_ge(s["v_psum"], g + 1)
                    if L == 0:
                        pv = P0[:].rearrange("p t (h d) -> p t h d", h=H)
                        for t in range(ST):
                            e = dve.tensor_copy(V[par][:, t, :, 0:DH], pv[:, t])
                        e.then_inc(s["v_copied"], 1)
                        return
                    dve.tensor_tensor(Vb[par][:], P0[:], bv[:].unsqueeze(1).to_broadcast([P, ST, D]), ALU.add)\
                        .then_inc(s["v_copied"], 1)
                    if L != 3:
                        dve.wait_ge(s["v_copied"], g + 1)
                        if isinstance(b, int) and b == 0 and L == 2:
                            dve.wait_ge(s["mask_ready"], 1 + (("att", 0) in stages))
                        for t in range(ST):
                            vb = Vb[par][:, t].rearrange("p (h d) -> p h d", h=H)
                            if L == 2:
                                dve.tensor_scalar(V[par][:, t, :, 0:DH], vb, keep[:, t, ds(b, 1)], None, ALU.mult)
                                e = dve.tensor_copy(V[par][:, t, :, DH], keep[:, t, ds(b, 1)].to_broadcast([P, H]))
                            else:
                                e = dve.tensor_copy(V[par][:, t, :, 0:DH], vb)
                        e.then_inc(s["v_ready"], 1)

                def row_max(b, h):
                    m = 8 * m_order[L] + b
                    dve.wait_ge(s["smax_ps"], 16 * m + h + 1)
                    dve.tensor_reduce(mx[:, :, h], A[2 + h % 2][:], AX.X, ALU.max).then_inc(s["smax_done"], 1)

                def max_rest(b):
                    m = 8 * m_order[L] + b
                    dve.wait_ge(s["m_hi"], m + 1)
                    dve.scalar_tensor_tensor(MR[:, 1], P0[0:H, 0], -1.0, MR[:, 0], ALU.mult, ALU.subtract).then_inc(s["m_lo"], 1)

                def col_max(b, h):
                    dve.wait_ge(s["st_ps"], 16 * (8 * s_order[L] + b) + h + 1)
                    dve.tensor_reduce(nmax[:, :, h], A[h % 4][:], AX.X, ALU.max, negate=True).then_inc(s["nmax_ready"], 1)

                def scale_values(b, par, c):
                    dve.wait_ge(s["exp_done"], 16 * (8 * s_order[L] + b) + GROUP * (c + 1))
                    hh = slice(GROUP * c, GROUP * (c + 1))
                    dve.reciprocal(rsum[:, :, hh], esum[:, :, hh]).then_inc(s["rsum_ready"], 1)
                    dve.wait_ge(s["rsum_ready"], CH * b + c + 1)
                    for t in range(ST):
                        vb = Vb[par][:, t].rearrange("p (h d) -> p h d", h=H)
                        e = dve.tensor_tensor(V[par][:, t, hh, 0:DH], vb[:, hh], rsum[:, t, hh].unsqueeze(2).to_broadcast([P, GROUP, DH]), ALU.mult)
                    e.then_inc(s["vs_ready"], 1)

                def normalise(b):
                    g = 8 * i + b
                    dve.wait_ge(s["av_done"], 16 * (8 * s_order[L] + b + 1))
                    dve.wait_ge(s["y_ps"], FREE + g)
                    for c in range(2):
                        e = dve.tensor_copy(On[:, 2 * c:2 * c + 2], O[c][:])
                    e.then_inc(s["on_ready"], 1)

                def divide(b):
                    m = 8 * m_order[L] + b
                    dve.wait_ge(s["oT_ps"], m + 1)
                    view = [A[2 + t][:].rearrange("p a b -> p (a b)").rearrange("p (h w) -> p h w", w=VW) for t in range(ST)]
                    for t in range(ST):
                        e = dve.reciprocal(rden[:, t], view[t][:, :, DH])
                    e.then_inc(s["on_rden"], 1)
                    dve.wait_ge(s["on_rden"], m + 1)
                    for t in range(ST):
                        e = dve.tensor_tensor(Oq[:, t].rearrange("p (h d) -> p h d", h=H), view[t][:, :, 0:DH],
                                              rden[:, t].unsqueeze(2).to_broadcast([P, H, DH]), ALU.mult)
                    e.then_inc(s["on_norm"], 1)

                def residual(b):
                    g = 8 * i + b
                    dve.wait_ge(s["y_ps"], FREE + g + 1)
                    xt = X[:, ds(ST * b, ST)]
                    dve.scalar_tensor_tensor(xt, P1[:], tg[:, L:L + 1], xt, ALU.mult, ALU.add).then_inc(s["x_res"], 1)
                    if n + 1 < len(stages):
                        dve.wait_ge(s["x_res"], FREE + g + 1)
                        for t in range(ST):
                            statistics(ST * b + t)

                def maxima1(b, t):
                    for e in range(2, H // 2):
                        k = 16 * b + 8 * t + e
                        dve.wait_ge(s["p1_ps"], k + 1)
                        bank = A[(8 * t + e) % 4]
                        dve.wait_ge(s["p1_max"], max(2, e - 1) + 16 * b + 8 * t)
                        dve.tensor_tensor(M2[:, e % 2], bank[:], M2[:, e % 2], ALU.max).then_inc(s["p1_max"], 1)
                    dve.wait_ge(s["p1_max"], 16 * b + 8 * (t + 1))
                    dve.tensor_tensor(M2[:, 0], M2[:, 0], M2[:, 1], ALU.max).then_inc(s["m1_step"], 1)
                    dve.wait_ge(s["m1_step"], 6 * b + 3 * t + 1)
                    dve.tensor_tensor(M1[:, t], M2[:, 0, 0], M2[:, 0, 1], ALU.max).then_inc(s["m1_step"], 1)
                    dve.wait_ge(s["m1_step"], 6 * b + 3 * t + 2)
                    dve.tensor_copy(m1p[:, t, 0], M1[:, t]).then_inc(s["m1_step"], 1)
                    dve.wait_ge(s["m1_step"], 6 * b + 3 * t + 3)
                    dve.tensor_tensor(m1p[:, t, 1], M1[:, t], m1p[:, t, 0], ALU.subtract).then_inc(s["m1_ready"], 1)

                def sums1(b, t):
                    steps = 4 if t == 0 else 2
                    base = 6 * b + 4 * t
                    if t == 0:
                        for half in range(2):
                            hh = slice(half * HPH, (half + 1) * HPH)
                            dve.wait_ge(s["exp1_done"], 16 * b + 4 * (half + 1))
                            dve.tensor_reduce(hpart[:, half], probs[:, t, hh].rearrange("p h q -> p q h"), AX.X, ALU.add).then_inc(s["sum1_step"], 1)
                        dve.wait_ge(s["sum1_step"], base + 2)
                        dve.tensor_tensor(hsum[:, t], hpart[:, 0], hpart[:, 1], ALU.add).then_inc(s["sum1_step"], 1)
                    else:
                        dve.wait_ge(s["exp1_done"], 16 * (b + 1))
                        dve.tensor_reduce(hsum[:, t], probs[:, t].rearrange("p h q -> p q h"), AX.X, ALU.add).then_inc(s["sum1_step"], 1)
                    dve.wait_ge(s["sum1_step"], base + steps - 1)
                    dve.reciprocal(hsum[:, t], hsum[:, t]).then_inc(s["sum1_step"], 1)
                    dve.wait_ge(s["sum1_step"], base + steps)
                    dve.tensor_tensor(probs[:, t], probs[:, t], hsum[:, t].unsqueeze(1).to_broadcast([P, H, S]), ALU.mult)\
                        .then_inc(s["norm1"], 1)

                for b in range(2):
                    rest_k(b, b)
                    rest_q(b, b)
                    low_k(b, b)
                    low_q(b, b)
                    if b == 0:
                        constants()
                        take_values(0, 0)
                if keys:
                    for h in range(H):
                        row_max(0, h)
                    max_rest(0)
                if L != 0:
                    dve.wait_ge(s["bias_added"], sum(l != 0 for l in n_att[:i + 1]))

                def slot_keys(b, par, v):
                    nearer, later = exists(b + 1), exists(b + 2)
                    if later:
                        rest_k(b + 2, par)
                    if nearer:
                        take_values(b + 1, 1 - par)
                    if exists(b - 1):
                        divide(b - 1)
                    if later:
                        low_k(b + 2, par)
                    if nearer:
                        for h in range(2):
                            row_max(b + 1, h)
                    if exists(b - 1):
                        residual(b - 1)
                    if nearer:
                        for h in range(2, H):
                            row_max(b + 1, h)
                            if later and h == 5:
                                rest_q(b + 2, par)
                            if later and h == 8:
                                low_q(b + 2, par)
                        max_rest(b + 1)

                def slot1(b, par, v):
                    nearer, later = exists(b + 1), exists(b + 2)
                    maxima1(b, 0)
                    maxima1(b, 1)
                    if nearer:
                        take_values(b + 1, 1 - par)
                    sums1(b, 0)
                    if later:
                        rest_k(b + 2, par)
                    sums1(b, 1)
                    if later:
                        rest_q(b + 2, par)
                    if exists(b - 1):
                        residual(b - 1)
                    if later:
                        low_k(b + 2, par)
                        low_q(b + 2, par)

                def slot3(b, par, v):
                    nearer, later = exists(b + 1), exists(b + 2)
                    if exists(b - 1):
                        normalise(b - 1)
                    for c in range(CH):
                        for h in range(GROUP * c, GROUP * (c + 1)):
                            col_max(b, h)
                        if c == 1 and later:
                            rest_k(b + 2, par)
                        if c == 2 and nearer:
                            take_values(b + 1, 1 - par)
                        if c:
                            scale_values(b, par, c - 1)
                        if c == 2 and later:
                            low_k(b + 2, par)
                        if c == 3 and exists(b - 1):
                            residual(b - 1)
                    scale_values(b, par, CH - 1)
                    if later:
                        rest_q(b + 2, par)
                        low_q(b + 2, par)

                slots(dve, slot_keys if keys else slot1 if L == 1 else slot3)
                if keys:
                    divide(B - 1)
                elif L == 3:
                    normalise(B - 1)
                residual(B - 1)

            rt_order = {L: i for i, L in enumerate([L for k, L in stages if k == "ffn" and L in (0, 3)])}
            def bc_row(x):
                return x.unsqueeze(2).to_broadcast([P, NT, E0])

            def bc_exp(x):
                return x.unsqueeze(1).to_broadcast([P, NT, E0])

            def link(k, r, e):
                e.then_inc(s["rt_step"], 1)
                dve.wait_ge(s["rt_step"], k)

            def softmax_rows(L):
                r = rt_order[L]
                dve.wait_ge(s["rt_const"], 5)
                dve.wait_ge(s["rt_logits"], r + 1)
                logits = ps[0][:].rearrange("p a b -> p (a b)")[:, 0:NT * E0].rearrange("p (t e) -> p t e", e=E0)
                if L == 0:
                    dve.wait_ge(s["f0_router"], 48)
                    link(5 * r + 1, r, dve.tensor_tensor(route[2][:], logits, bc_exp(br0[:]), ALU.add))
                else:
                    link(5 * r + 1, r, dve.tensor_copy(route[2][:], logits))
                link(5 * r + 2, r, dve.tensor_reduce(row_m[:, 0], route[2][:], AX.X, ALU.max))
                dve.tensor_tensor(route[0][:], route[2][:], bc_row(row_m[:, 0]), ALU.subtract).then_inc(s["rt_step"], 1)
                dve.wait_ge(s["rt_exp"], r + 1)
                link(5 * r + 4, r, dve.tensor_reduce(row_m[:, 1], route[1][:], AX.X, ALU.add))
                link(5 * r + 5, r, dve.reciprocal(row_m[:, 2], row_m[:, 1]))

            def running_counts(nk, chain, c0, r):
                dve.wait_ge(s["rt_prefix"], r + 1)
                bank = ps[2]
                tot = bank[:, 1, 0:NT * nk].rearrange("p (t k) -> p t k", k=nk)
                chain(c0 + 1, dve.tensor_copy(totals[:, :, 0:nk], tot))
                for k in range(nk):
                    e = dve.tensor_tensor_scan(sums[:, :, k], ones_f[:], totals[:, :, k], 0.0, ALU.mult, ALU.add)
                chain(c0 + 2, e)
                chain(c0 + 3, dve.tensor_tensor(totals[:, :, 0:nk], sums[:, :, 0:nk], totals[:, :, 0:nk], ALU.subtract))
                chain(c0 + 4, dve.tensor_tensor(totals[:, :, 0:nk], totals[:, :, 0:nk],
                                                bank[:, 0, 0:NT * nk].rearrange("p (t k) -> p t k", k=nk), ALU.add))

            def route0(n):
                r = rt_order[0]
                softmax_rows(0)
                def chain(k, e):
                    e.then_inc(s["thr_step"], 1)
                    dve.wait_ge(s["thr_step"], k)

                dve.memset(mid0[0][32:64, FT0 - 1], 1.0)
                dve.memset(mid0[1][32:64, FT0 - 1], 1.0)
                dve.memset(thr[:], 0)
                for j in range(DIGIT):
                    dve.memset(step_f[:, j], (j + 1) * 2.0 ** (DIGIT_BITS * (DIGITS - 1)))
                    dve.memset(step_i[:, j], (j + 1) << (DIGIT_BITS * (DIGITS - 1)))
                chain(1, dve.tensor_tensor(probs_e[:], route[1][:], bc_row(row_m[:, 2]), ALU.mult))
                with dve.Fori(0, DIGITS // UNROLL0) as i:
                    for d in range(UNROLL0):
                        k = 1 + 6 * (UNROLL0 * i + d)
                        wide = [P, DIGIT, NT, E0]
                        chain(k + 1, dve.tensor_tensor(cand[:], thr[:].unsqueeze(1).to_broadcast([P, DIGIT, E0]), step_i[:], ALU.bitwise_or))
                        dve.tensor_tensor(above[:], probs_e[:].unsqueeze(1).to_broadcast(wide),
                                          cand[:].bitcast(F32).unsqueeze(2).to_broadcast(wide), ALU.is_ge).then_inc(s["thr_cmp"], 1)
                        dve.wait_ge(s["thr_cnt"], UNROLL0 * i + d + 1)
                        counted = ps[1][:].rearrange("p a b -> p (a b)")[:, 0:DIGIT * NT * E0]
                        chain(k + 2, dve.tensor_reduce(cnt[:], counted.rearrange("p (j t e) -> p j e t", j=DIGIT, e=E0), AX.X, ALU.add))
                        chain(k + 3, dve.scalar_tensor_tensor(reached[:], cnt[:], TOP0 - 0.5, step_f[:], ALU.is_ge, ALU.mult))
                        dve.tensor_scalar(step_f[:], step_f[:], 0.5 ** DIGIT_BITS, None, ALU.mult)
                        chain(k + 4, dve.tensor_reduce(taken[:], reached[:].rearrange("p j e -> p e j"), AX.X, ALU.max))
                        dve.tensor_tensor(thr[:], thr[:], taken[:], ALU.bitwise_or).then_inc(s["thr_step"], 1)
                        chain(k + 6, dve.tensor_copy(step_i[:], step_f[:]))
                k = 1 + 6 * DIGITS
                dve.tensor_tensor(flags[:, :, 0], probs_e[:], bc_exp(thr[:].bitcast(F32)), ALU.is_gt)
                dve.tensor_tensor(flags[:, :, 1], probs_e[:], bc_exp(thr[:].bitcast(F32)), ALU.is_equal).then_inc(s["thr_cmp"], 1)
                running_counts(2 * E0, chain, k, r)
                k += 4
                chain(k + 1, dve.tensor_scalar(need[:], sums[:, NT - 1, 0:E0], -1.0, float(TOP0), ALU.mult, ALU.add))
                chain(k + 2, dve.tensor_tensor(route[0][:], totals[:, :, E0:2 * E0], bc_exp(need[:]), ALU.is_le))
                chain(k + 3, dve.tensor_tensor(route[2][:], route[0][:], flags[:, :, 1], ALU.mult))
                chain(k + 4, dve.tensor_tensor(route[0][:], route[2][:], flags[:, :, 0], ALU.add))
                chain(k + 5, dve.scalar_tensor_tensor(coef[:], route[0][:], tg[:, 4:5], probs_e[:], ALU.mult, ALU.mult))
                chain(k + 6, dve.tensor_tensor(route[1][:], totals[:, :, E0:2 * E0], bc_exp(need[:]), ALU.min))
                chain(k + 7, dve.tensor_tensor(route[2][:], route[1][:], totals[:, :, 0:E0], ALU.add))
                chain(k + 8, dve.tensor_tensor(route[1][:], route[2][:], route[0][:], ALU.mult))
                chain(k + 9, dve.tensor_scalar(pos_i[:], route[1][:], 1.0, None, ALU.subtract))

            def parts(x, part, rest, step):
                step(dve.tensor_copy(part[0][:], x))
                step(dve.tensor_tensor(rest[0][:], x, part[0][:], ALU.subtract))
                step(dve.tensor_copy(part[1][:], rest[0][:]))
                step(dve.tensor_tensor(part[2][:], rest[0][:], part[1][:], ALU.subtract))

            def ffn0(n):
                dve.wait_ge(s["tg_ready"], 1)
                route0(n)
                steps = [0]

                def step(e):
                    steps[0] += 1
                    e.then_inc(s["f0_step"], 1)
                    dve.wait_ge(s["f0_step"], steps[0])

                dve.tensor_scalar(place_i[:], pos_i[:], P - 1, None, ALU.bitwise_and)
                step(dve.tensor_scalar(half_i[:], pos_i[:], P.bit_length() - 1, None, ALU.arith_shift_right))
                dve.tensor_copy(place0[:], place_i[:])
                step(dve.tensor_copy(route[3][:], half_i[:]))
                for h in range(SL0):
                    e = dve.tensor_scalar(in_half[:, :, :, h], route[3][:], float(h), None, ALU.is_equal)
                step(e)
                parts(coef[:], gpart, grest, step)
                per = in_half[:].rearrange("p t e h -> p e t h")
                wide = [P, E0, NT, SL0]
                dve.tensor_tensor(lists0[:, :, :, 0], per, col[:, 0:NT].unsqueeze(1).unsqueeze(3).to_broadcast(wide), ALU.mult)
                dve.tensor_scalar(lists0[:, :, :, 1], per, row[:], None, ALU.mult)
                for v in range(3):
                    e = dve.tensor_tensor(lists0[:, :, :, 2 + v], per, gpart[v][:].rearrange("p t e -> p e t").unsqueeze(3).to_broadcast(wide), ALU.mult)
                step(e)

                def hot(e):
                    dve.tensor_tensor(hot0[e % 2][:], place0[:, :, e].unsqueeze(2).to_broadcast([P, NT, P]),
                                      col[:].unsqueeze(1).to_broadcast([P, NT, P]), ALU.is_equal).then_inc(s["f0_hot"], 1)

                def index(e):
                    dve.wait_ge(s["f0_list"], e + 1)
                    got = ps[3 + e % 2][:, 0, 0:5 * SL0].rearrange("p (v h) -> p v h", v=5)
                    dve.tensor_copy(idl0[:, e], got[:, 1])
                    dve.tensor_copy(gsum0[:, e], got[:, 3]).then_inc(s["f0_idstep"], 1)
                    dve.wait_ge(s["f0_idstep"], 3 * e + 1)
                    dve.scalar_tensor_tensor(idx0[:, e], got[:, 0], float(P), idl0[:, e], ALU.mult, ALU.add)
                    dve.tensor_tensor(gate0[:, e], got[:, 2], gsum0[:, e], ALU.add).then_inc(s["f0_idstep"], 1)
                    dve.wait_ge(s["f0_idstep"], 3 * e + 2)
                    dve.tensor_tensor(gate0[:, e], gate0[:, e], got[:, 4], ALU.add).then_inc(s["f0_idstep"], 1)
                    dve.wait_ge(s["f0_idstep"], 3 * e + 3)
                    dve.sem_inc(s["f0_idx"], 1)

                def weigh(e):
                    dve.wait_ge(s["f0_down"], e + 1)
                    wait(dve, s["f0_scatter"], 16 * SL0 * (e - 1))
                    for h in range(SL0):
                        y = dve.tensor_scalar(yg0[e % 2][:, h], ps[6 + e % 2][:, h], gate0[:, e, h:h + 1], None, ALU.mult)
                    y.then_inc(s["f0_yg"], 1)

                hot(0)
                for e in range(E0):
                    index(e)
                    if e == 0:
                        hot(1)
                    if e + 2 < E0:
                        hot(e + 2)
                    if e >= 3:
                        weigh(e - 3)
                for e in range(E0 - 3, E0):
                    weigh(e)
                dve.wait_ge(s["x_back"], 16)
                dve.sem_inc(s["x_ffn"], 1)

            def ffn1_rhs():
                dve.wait_ge(s["f1_rhs"], 16)
                dve.tensor_reduce(rmax[:], rhs1[:].rearrange("p c n -> p n c"), AX.X, ALU.max, apply_absolute_value=True).then_inc(s["f1_rmax"], 1)
                dve.wait_ge(s["f1_rall"], 1)

                def chain(k, e):
                    e.then_inc(s["f1_rstep"], 1)
                    dve.wait_ge(s["f1_rstep"], k)

                chain(1, dve.tensor_scalar(rscale[:], rall[:], 1e-12, 1.0 / 127.0, ALU.max, ALU.mult))
                chain(2, dve.reciprocal(rinv[:], rscale[:]))
                chain(3, dve.tensor_tensor(rtmp[:], rhs1[:], rinv[:].unsqueeze(1).to_broadcast([P, KC, D]), ALU.mult))
                chain(4, dve.tensor_scalar(rtmp[:], rtmp[:], -127.0, 127.0, ALU.max, ALU.min))
                chain(5, dve.tensor_scalar(rtmp[:], rtmp[:], MAGIC, None, ALU.add))
                dve.tensor_scalar(qrhs[:], rtmp[:], MAGIC, None, ALU.subtract).then_inc(s["f1_qrhs"], 1)

            def ffn1(n):
                dve.wait_ge(s["tg_ready"], 1)

                def pair(b, j):
                    dve.wait_ge(s["f1_ps"], b + 1)
                    for t in range(ST):
                        e = dve.scalar_tensor_tensor(y1[j][:, t], ps[2 + j][:, t], lscale[:, ds(ST * b + t, 1)], rscale[:], ALU.mult, ALU.mult)
                    e.then_inc(s["f1_y"], 1)
                    dve.wait_ge(s["f1_y"], b + 1)
                    xt = X[:, ds(ST * b, ST)]
                    dve.scalar_tensor_tensor(xt, y1[j][:], tg[:, 5:6], xt, ALU.mult, ALU.add).then_inc(s["f1_acc"], 1)
                    if n + 1 < len(stages):
                        dve.wait_ge(s["f1_acc"], b + 1)
                        for t in range(ST):
                            statistics(ST * b + t)

                with dve.Fori(0, B // 2) as i:
                    for j in range(2):
                        pair(2 * i + j, j)
                dve.wait_ge(s["f1_acc"], B)
                dve.sem_inc(s["x_ffn"], 1)

            def ffn2(n):
                dve.wait_ge(s["tg_ready"], 1)
                dve.wait_ge(s["f2_w"], 16 * 3)

                def split(k, src, left, mid, lowest, step, done):
                    dve.tensor_tensor(left, src, high(src), ALU.subtract).then_inc(step, 1)
                    dve.wait_ge(step, 2 * k + 1)
                    dve.tensor_copy(mid, left).then_inc(step, 1)
                    dve.wait_ge(step, 2 * k + 2)
                    dve.tensor_tensor(lowest, left, mid, ALU.subtract).then_inc(done, 1)

                def look(k, pieces):
                    dve.wait_ge(s["f2_low_ps"], k + 1)
                    dve.tensor_reduce(lowest2[:, k:k + 1], ps[7][0:1, 0, pieces], AX.X, ALU.max).then_inc(s["f2_wide"], 1)
                    dve.wait_ge(s["f2_wide"], 2 * k + 1)
                    dve.tensor_scalar(wide2[:, k:k + 1], lowest2[:, k:k + 1], 1.0, None, ALU.min).then_inc(s["f2_wide"], 1)

                def chunk(ch):
                    first = isinstance(ch, int) and ch == 0
                    for o in range(HT):
                        k = ch * SPLITS + o
                        dve.wait_ge(s["f2_sil"], ch * HT + o + 1)
                        if o == 0:
                            wait(dve, s["f2_yps"], ch * TPC)
                        dve.scalar_tensor_tensor(hA[:, o], ps[2 * (o % 2) + 1][:].rearrange("p a b -> p (a b)"), sc2[:, 1, o:o + 1], sil[o % 2],
                                                 ALU.mult, ALU.mult).then_inc(s["f2_hA"], 1)
                        if first and o == HT - 2:
                            look(0, slice(0, CHECK_H1))
                        dve.wait_ge(s["f2_hA"], ch * HT + o + 1)
                        wait(dve, s["f2_part"], k)
                        split(k, hA[:, o], left2, partA[:, 0, o], partA[:, 1, o], s["f2_step"], s["f2_part"])
                    for stage, (h, part) in enumerate(((hB, partB), (hA, partA))):
                        for o in range(HT):
                            k = ch * SPLITS + (stage + 1) * HT + o
                            if first and stage == 0 and o == HT - 1:
                                look(1, slice(CHECK_H1, CHECK_H1 + CHECK_REST))
                            dve.wait_ge(s["f2_act"], (2 * ch + stage) * HT + o + 1)
                            dve.wait_ge(s["f2_part"], k)
                            split(k, h[:, o], left2, part[:, 0, o], part[:, 1, o], s["f2_step"], s["f2_part"])
                        if stage == 0 and not (isinstance(ch, int) and ch == NCH - 1):
                            dve.wait_ge(s["f2_up"], (ch + 1) * HT)
                            for c in range(KC):
                                k = KC * ch + c
                                wait(dve, s["f2_xpart"], k)
                                split(k, XNT[:, c, ds((ch + 1) * CHUNK, CHUNK)], leftX, partX[:, 0, c], partX[:, 1, c], s["f2_xstep"], s["f2_xpart"])
                    if first:
                        dve.wait_ge(s["f2_w3"], 32)
                    for t in range(TPC):
                        k = ch * TPC + t
                        dve.wait_ge(s["f2_yps"], k + 1)
                        dve.tensor_tensor(y2[t % 2], ps[6 + t % 2][:, 0], s3_2[:], ALU.mult).then_inc(s["f2_y"], 1)
                        dve.wait_ge(s["f2_y"], k + 1)
                        xt = X[:, ds(k, 1)].squeeze(1)
                        dve.scalar_tensor_tensor(xt, y2[t % 2], tg[:, 6:7], xt, ALU.mult, ALU.add).then_inc(s["f2_acc"], 1)
                        if n + 1 < len(stages):
                            dve.wait_ge(s["f2_acc"], k + 1)
                            statistics(k)

                chunk(0)
                with dve.Fori(1, NCH - 1) as ch:
                    chunk(ch)
                chunk(NCH - 1)
                dve.wait_ge(s["f2_acc"], NT)
                dve.sem_inc(s["x_ffn"], 1)

            def route3(n):
                r = rt_order[3]
                softmax_rows(3)
                k = [5 * (r + 1)]

                def chain(e):
                    k[0] += 1
                    e.then_inc(s["rt_step"], 1)
                    dve.wait_ge(s["rt_step"], k[0])

                chain(dve.tensor_tensor(probs_e[:], route[1][:], bc_row(row_m[:, 2]), ALU.mult))
                left = probs_e
                for j in range(2):
                    chain(dve.tensor_reduce(row_m[:, 3 + j], left[:], AX.X, ALU.max))
                    chain(dve.tensor_tensor(route[2][:], left[:], bc_row(row_m[:, 3 + j]), ALU.is_equal))
                    chain(dve.tensor_tensor(route[3][:], route[2][:], bc_exp(rev[:]), ALU.mult))
                    chain(dve.tensor_reduce(row_m[:, 0], route[3][:], AX.X, ALU.max))
                    chain(dve.tensor_tensor(flags[:, :, j], route[3][:], bc_row(row_m[:, 0]), ALU.is_equal))
                    if j == 0:
                        chain(dve.scalar_tensor_tensor(route[4][:], flags[:, :, 0], -2.0, probs_e[:], ALU.mult, ALU.add))
                        left = route[4]
                dve.sem_inc(s["rt_cnt"], 1)
                chain(dve.tensor_tensor(row_m[:, 5], row_m[:, 3], row_m[:, 4], ALU.add))
                chain(dve.reciprocal(row_m[:, 5], row_m[:, 5]))
                chain(dve.tensor_scalar(row_m[:, 5], row_m[:, 5], tg[:, 7:8], None, ALU.mult))
                for j in range(2):
                    e = dve.tensor_tensor(row_m[:, j], row_m[:, 3 + j], row_m[:, 5], ALU.mult)
                chain(e)
                running_counts(2 * E3, lambda _, e: chain(e), 0, r)
                for j in range(PAIRS3):
                    of = slice(j * E3, (j + 1) * E3)
                    dve.scalar_tensor_tensor(kept[j][:], totals[:, :, of], CAP3 + 0.5, flags[:, :, j], ALU.is_le, ALU.mult)
                    e = dve.tensor_scalar(count3[:, j], sums[:, NT - 1, of], float(CAP3), None, ALU.min)
                chain(e)
                chain(dve.scalar_tensor_tensor(load3_i[:], count3[:, 0], float(P - 1), count3[:, 1], ALU.add, ALU.add))
                chain(dve.tensor_scalar(load3_i[:], load3_i[:], P.bit_length() - 1, None, ALU.arith_shift_right))
                chain(dve.tensor_copy(tiles3[:], load3_i[:]))
                chain(dve.tensor_tensor_scan(upto3[:], ones_f[:, 0:E3], tiles3[:], 0.0, ALU.mult, ALU.add))
                chain(dve.tensor_tensor(load3[:], upto3[:], tiles3[:], ALU.subtract))
                chain(dve.tensor_scalar(start3[:, 0], load3[:], float(P), None, ALU.mult))
                chain(dve.tensor_tensor(start3[:, 1], start3[:, 0], count3[:, 0], ALU.add))
                for j in range(PAIRS3):
                    chain(dve.tensor_tensor(route[j][:], totals[:, :, j * E3:(j + 1) * E3], bc_exp(start3[:, j]), ALU.add))
                    chain(dve.tensor_tensor(route[2 + j][:], route[j][:], kept[j][:], ALU.mult))
                    chain(dve.tensor_reduce(slot3[:, j], route[2 + j][:], AX.X, ALU.add))
                chain(dve.tensor_scalar(slot3_i[:], slot3[:], 1.0, None, ALU.subtract))
                dve.tensor_scalar(place3_i[:], slot3_i[:], P - 1, None, ALU.bitwise_and)
                chain(dve.tensor_scalar(tile3_i[:], slot3_i[:], P.bit_length() - 1, None, ALU.arith_shift_right))
                dve.tensor_copy(place3[:], place3_i[:])
                chain(dve.tensor_copy(tile3[:], tile3_i[:]))
                parts(row_m[:, 0:PAIRS3], part3, rest3, chain)
                per = lists3[:, :, :, 0]
                wide = [P, PAIRS3, NT, TILES3]
                chain(dve.tensor_tensor(per, tile3[:].unsqueeze(3).to_broadcast(wide),
                                        col[:, 0:TILES3].unsqueeze(1).unsqueeze(1).to_broadcast(wide), ALU.is_equal))
                dve.sem_inc(s["f3_place"], 1)
                dve.tensor_tensor(lists3[:, :, :, 1], per, col[:, 0:NT].unsqueeze(1).unsqueeze(3).to_broadcast(wide), ALU.mult)
                dve.tensor_scalar(lists3[:, :, :, 2], per, row[:], None, ALU.mult)
                dve.tensor_tensor(lists3[:, :, :, 3], per, part3[0][:].unsqueeze(3).to_broadcast(wide), ALU.mult)
                for j in range(PAIRS3):
                    dve.tensor_tensor(hot3[:, j], place3[:, j].unsqueeze(2).to_broadcast([P, NT, P]),
                                      col[:].unsqueeze(1).to_broadcast([P, NT, P]), ALU.is_equal).then_inc(s["f3_hot"], 1)
                wide = [P, TILES3, E3]
                chain(dve.tensor_tensor(before3[:], col[:, 0:TILES3].unsqueeze(2).to_broadcast(wide),
                                        upto3[:].unsqueeze(1).to_broadcast(wide), ALU.is_ge))
                chain(dve.tensor_reduce(expert3[:], before3[:], AX.X, ALU.add))
                chain(dve.tensor_scalar(expert3_i[:], expert3[:], E3 - 1.0, None, ALU.min))
                dve.wait_ge(s["f3_list"], 1)
                got = ps[3][:].rearrange("p a b -> p (a b)")[:, 0:6 * TILES3].rearrange("p (v i) -> p v i", v=6)
                dve.tensor_scalar(idl3[0][:], got[:, 0], spare[:, 1:2], spare[:, 0:1], ALU.mult, ALU.add)
                chain(dve.tensor_copy(gate3[1][:], got[:, 4]))
                dve.tensor_tensor(gate3[0][:], got[:, 3], gate3[1][:], ALU.add)
                chain(dve.scalar_tensor_tensor(idl3[1][:], got[:, 1], float(P), idl3[0][:], ALU.mult, ALU.add))
                dve.tensor_tensor(idx3[:], idl3[1][:], got[:, 2], ALU.add)
                chain(dve.tensor_tensor(gate3[1][:], gate3[0][:], got[:, 5], ALU.add))
                dve.sem_inc(s["f3_idx"], 1)

            def ffn3(n):
                dve.wait_ge(s["tg_ready"], 1)
                route3(n)

                dve.wait_ge(s["f3_idx"], 1)

                def copy(t, k):
                    dve.wait_ge(s["f3_xt"], t + 1)
                    wait(dve, s["f3_up"], t - 1)
                    dve.tensor_copy(xgT3[k % 2][:], ps[3 + k % 2][:, 0].rearrange("p (c t) -> p c t", c=KC)).then_inc(s["f3_xgT"], 1)

                def copy_w1(t, k):
                    e = dve.value_load(expert3_i[0:1, ds(t, 1)], min_val=0, max_val=E3 - 1)
                    dve.wait_ge(s["f3_loaded"], e + 1)
                    wait(dve, s["f3_up"], t - 1)
                    dve.tensor_copy(w1_tile[k][:, 1], w1_3[:, ds(e, 1), 1].squeeze(1)).then_inc(s["f3_w1_dve"], 1)

                def weigh(t, k):
                    dve.wait_ge(s["f3_down"], t + 1)
                    wait(dve, s["f3_scatter"], 16 * (t - 1))
                    dve.tensor_scalar(yg3[k % 2][:], ps[5 + 2 * (k % 2)][:, 0], gate3[1][:, ds(t, 1)], None, ALU.mult).then_inc(s["f3_yg"], 1)

                def pair(t0):
                    for k in range(2):
                        t = t0 + k
                        if not isinstance(t, int) or t + 2 < TILES3:
                            copy_w1(t + 2, k)
                            copy(t + 2, k)
                        weigh(t, k)

                for t in range(2):
                    copy_w1(t, t)
                    copy(t, t)
                pair(0)
                with dve.Fori(1, TILES3 // 2 - 1) as i:
                    pair(2 * i)
                pair(TILES3 - 2)

            for n, (kind, L) in enumerate(stages):
                if (kind, L) == ("ffn", 1):
                    ffn1_rhs()
                layernorm(n)
                if kind == "att":
                    attention(n, L)
                else:
                    (ffn0, ffn1, ffn2, ffn3)[L](n)


def layout(v):
    n = {k: np.asarray(x) for k, x in v.items()}
    o = {"x": n["x"].reshape(T, D), "g_xattn": n["g_xattn"], "g_ffn": n["g_ffn"]}

    def rows(w):
        c, m = w.shape
        return w.reshape(c // P, P, m).transpose(1, 0, 2)

    o["ctxT"] = rows(n["ctx_1024"].reshape(T, D).T)
    mask = n["mask_1x1xSxS2_bk1"].reshape(S, S)
    o["mask_qk"], o["mask_kq"] = rows(mask), rows(mask.T)
    pad = n["mask_BxS2_bf0"]
    o["pad"], o["padT"] = pad, rows(pad.T)
    def heads(w):
        lead = w.shape[:-1]
        k = len(lead)
        w = w.reshape(lead + (HPH, HALF, DH))
        return w.transpose(tuple(range(k)) + (k + 1, k + 2, k)).reshape(lead + (D,))

    def padded(w):
        z = np.zeros((H, VW, D), w.dtype)
        z[:, :DH] = w.reshape(H, DH, D)
        return rows(z.reshape(H * VW, D))

    zeros = np.zeros(D, n["x"].dtype)
    kv = n["L3_xattn_Wkv"]
    ws = [
        (n["L0_xattn_Wq"].T, n["L0_xattn_Wk"].T, n["L0_xattn_Wv"].T, n["L0_xattn_Wo"].T, zeros, zeros, zeros, zeros),
        (n["L1_xattn_Wq_w"].T, n["L1_xattn_Wk_w"].T, n["L1_xattn_Wv_w"].T, n["L1_xattn_Wo_w"].T,
         n["L1_xattn_Wq_b"], n["L1_xattn_Wk_b"], n["L1_xattn_Wv_b"], n["L1_xattn_Wo_b"]),
        (n["L2_xattn_wq"].T, n["L2_xattn_wk"].T, n["L2_xattn_wv"].T, n["L2_xattn_wo"].T,
         n["L2_xattn_bq"], n["L2_xattn_bk"], n["L2_xattn_bv"], n["L2_xattn_bo"]),
        (n["L3_xattn_Wq"], kv[:, :D], kv[:, D:], n["L3_xattn_Wo"], n["L3_xattn_bq"],
         n["L3_xattn_bkv"][:D], n["L3_xattn_bkv"][D:], n["L3_xattn_bo"]),
    ]
    for L, (q, k, w, wo_, bq_, bk_, bv_, bo_) in enumerate(ws):
        o[f"wq{L}"], o[f"wk{L}"], o[f"wv{L}"] = rows(heads(q)), rows(heads(k)), rows(w)
        o[f"wo{L}"] = rows(wo_) if L in SOFTMAX_KEYS else padded(wo_)
        o[f"bq{L}"], o[f"bk{L}"] = heads(bq_).reshape(HALF, P).T, heads(bk_).reshape(HALF, P).T
        o[f"bv{L}"], o[f"bo{L}"] = bv_, bo_
    o["wr0"], o["br0"] = rows(n["L0_ffn_Wr"]), n["L0_ffn_br"]
    z = np.zeros((NG0, D, FT0 * P), n["x"].dtype)
    z[:, :, :F0] = n["L0_ffn_W_up"]
    o["wu0"] = z.reshape(NG0, KC, P, FT0 * P).transpose(2, 0, 1, 3)
    z = np.zeros((NG0, FT0 * P), n["x"].dtype)
    z[:, :F0] = n["L0_ffn_b_up"]
    o["bu0"] = z.reshape(NG0, FT0, P).transpose(2, 0, 1)
    z = np.zeros((E0, FT0 * P, D), n["x"].dtype)
    z[:, :F0], z[:, F0] = n["L0_ffn_W_down"], n["L0_ffn_b_down"]
    o["wd0"] = z.reshape(E0, FT0, P, D).transpose(2, 0, 1, 3)
    o["rhs1"] = rows(n["L1_ffn_rhs"])
    for name, key in (("w1_2", "w1"), ("w2_2", "w2"), ("h1_2", "h1"), ("h2_2", "h2"), ("w3_2", "w3")):
        o[name] = rows(n[f"L2_ffn_{key}_w"].T)
    o["sc2"] = np.stack([n[f"L2_ffn_{key}_s"].reshape(HT, P).T for key in ("w1", "w2", "h1", "h2")], 1)
    o["s3_2"] = n["L2_ffn_w3_s"]
    o["wr3"] = rows(n["L3_ffn_router_w"].T)
    o["w1_3"] = n["L3_ffn_w1"].reshape(E3, KC, P, HID).transpose(0, 2, 1, 3)
    o["w2_3"] = n["L3_ffn_w2"].reshape(E3, HT, P, D).transpose(0, 2, 1, 3)
    return {k: np.ascontiguousarray(x) for k, x in o.items()}


STAGES = [("att", 0), ("ffn", 0), ("att", 1), ("ffn", 1), ("att", 2), ("ffn", 2), ("att", 3), ("ffn", 3)]


def kernel(**inputs):
    import concourse.bacc as bacc
    from concourse.bass_utils import run_bass_kernel_spmd

    nc = bacc.Bacc("TRN2", target_bir_lowering=False, num_devices=1)
    arrays = {f"in_{k}": x for k, x in layout(inputs).items()}
    args = {k[3:]: nc.dram_tensor(k, x.shape, mybir.dt.from_np(x.dtype), kind="ExternalInput").ap() for k, x in arrays.items()}
    out = nc.dram_tensor("out", (T, D), F32, kind="ExternalOutput").ap()
    program(nc, args, out, STAGES)
    r = run_bass_kernel_spmd(nc, [arrays], core_ids=[0])
    return r.results[0]["out"].reshape(B, S, D)
```
